# Optimizing a Trainium2 kernel written in Bass

```python
import numpy as np
import jax
import jax.numpy as jnp

def _softmax(x, axis=-1):
    return jax.nn.softmax(x, axis=axis)

def _gelu(x):
    return jax.nn.gelu(x, approximate=True)

def _silu(x):
    return jax.nn.silu(x)

def _sigmoid(x):
    return jax.nn.sigmoid(x)

def _layernorm(x, axis=-1, eps=1e-05):
    m = jnp.mean(x, axis=axis, keepdims=True)
    v = jnp.var(x, axis=axis, keepdims=True)
    return (x - m) / jnp.sqrt(v + eps)

def _scatter_add(tgt, idx, src, axis=0):
    return tgt.at[idx].add(src)

def _segment_sum(src, seg, n):
    return jax.ops.segment_sum(src, seg, n)
kernel_name = 'mk_flamingo_gated_d1_seqx_r8_8f1c74'

def setup_inputs(seed: int=0):
    np.random.seed(seed)
    _w = jnp.asarray

    def _rec_inputs():
        import jax
        import jax.numpy as jnp
        _rk = jax.random.key(seed)
        x = 0.002226 + 0.9996 * jax.random.normal(jax.random.fold_in(_rk, 1), (64, 64, 128), jnp.float32)
        _lenS = 64 - jax.random.randint(jax.random.fold_in(_rk, 7), (64,), 0, max(1, 64 // 4) + 1, jnp.int32)
        _lenS2 = 64 - jax.random.randint(jax.random.fold_in(_rk, 8), (64,), 0, max(1, 64 // 4) + 1, jnp.int32)
        _ctx_1024P = jax.random.normal(jax.random.fold_in(_rk, 11), (64, 16, 128), jnp.float32)
        _ctx_1024c = jax.random.dirichlet(jax.random.fold_in(_rk, 511), 0.3 * jnp.ones((16,), jnp.float32), (64, 64))
        _ctx_1024t = jnp.einsum('bsk,bkd->bsd', _ctx_1024c, _ctx_1024P)
        _ctx_1024t = _ctx_1024t * jax.lax.rsqrt(jnp.mean(jnp.square(_ctx_1024t)) + 1e-12) * 0.953939
        ctx_1024 = -0.000125008 + 0.999885 * (_ctx_1024t + 0.3 * jax.random.normal(jax.random.fold_in(_rk, 611), (64, 64, 128), jnp.float32))
        _validS = jnp.arange(64)[None, :] < _lenS[:, None]
        _validS2 = jnp.arange(64)[None, :] < _lenS2[:, None]
        _causal = jnp.tril(jnp.ones((64, 64), dtype=bool))
        mask_BxS2_bk0 = jnp.logical_not(jnp.broadcast_to(_validS2[:, :], (64, 64)))
        _g = jax.random.normal(jax.random.fold_in(_rk, 9001), (2, 1), jnp.float32)
        _g = jnp.sign(_g) * jnp.maximum(jnp.abs(_g), 1.0) + (_g == 0) * 1.0
        g_xattn = _g[0]
        g_ffn = _g[1]
        return (x, ctx_1024, mask_BxS2_bk0, g_xattn, g_ffn)
    x, ctx_1024, mask_BxS2_bk0, g_xattn, g_ffn = _rec_inputs()

    def _L0_xattn_setup():
        import jax, jax.numpy as jnp
        import numpy as np
        DIM = 128
        DIM_HEAD = 64
        NUM_HEADS = 16
        HIDDEN = DIM_HEAD * NUM_HEADS
        EPS = 1e-05

        def layer_norm(t, gamma, beta):
            mu = jnp.mean(t, axis=-1, keepdims=True)
            var = jnp.var(t, axis=-1, keepdims=True)
            return (t - mu) * jax.lax.rsqrt(var + EPS) * gamma + beta
        key = jax.random.key(seed)
        ks = jax.random.split(key, 12)
        B, F, Q = (8, 512, 64)
        x = jax.random.normal(ks[0], (B, F, DIM), dtype=jnp.float32)
        latents = jax.random.normal(ks[1], (B, Q, DIM), dtype=jnp.float32)
        mask = jax.random.randint(ks[2], (B, F), 0, 2) == 1
        s = 1.0 / np.sqrt(DIM)
        Wq = jax.random.normal(ks[3], (DIM, HIDDEN), dtype=jnp.float32) * s
        Wkv = jax.random.normal(ks[4], (DIM, 2 * HIDDEN), dtype=jnp.float32) * s
        Wout = jax.random.normal(ks[5], (HIDDEN, DIM), dtype=jnp.float32) * (1.0 / np.sqrt(HIDDEN))
        bout = jnp.zeros((DIM,), dtype=jnp.float32)
        g_media = jnp.ones((DIM,), dtype=jnp.float32)
        b_media = jnp.zeros((DIM,), dtype=jnp.float32)
        g_latent = jnp.ones((DIM,), dtype=jnp.float32)
        b_latent = jnp.zeros((DIM,), dtype=jnp.float32)
        return {'x': x, 'latents': latents, 'mask': mask, 'Wq': Wq, 'Wkv': Wkv, 'Wout': Wout, 'bout': bout, 'g_media': g_media, 'b_media': b_media, 'g_latent': g_latent, 'b_latent': b_latent}
    _L0_xattn_all = _L0_xattn_setup()
    _L0_xattn_in = {k: v for k, v in _L0_xattn_all.items() if k in ('Wq', 'Wkv', 'Wout', 'bout', 'g_media', 'b_media', 'g_latent', 'b_latent')}
    del _L0_xattn_all

    def _L0_ffn_setup():
        import jax, jax.numpy as jnp
        import numpy as np
        DIM = 128
        DEPTH = 2
        HEADS = 8
        DIM_HEAD = 64
        WINDOW = 64
        INNER = HEADS * DIM_HEAD
        HID = int(DIM * 4 * 2 / 3)
        B, N = (2, 1024)
        QK_SCALE = 8.0

        def shift_token(t):
            t1, t2 = jnp.split(t, 2, axis=-1)
            t2 = jnp.pad(t2, ((0, 0), (1, 0), (0, 0)))[:, :-1]
            return jnp.concatenate([t1, t2], axis=-1)

        def l2norm(t):
            return t / jnp.clip(jnp.linalg.norm(t, axis=-1, keepdims=True), 1e-12)

        def rotate_half(x):
            x1, x2 = jnp.split(x, 2, axis=-1)
            return jnp.concatenate([-x2, x1], axis=-1)

        def rotary_xpos(q, k):
            n = q.shape[-2]
            half_idx = jnp.arange(0, DIM_HEAD, 2, dtype=jnp.float32)
            inv_freq = 1.0 / 10000.0 ** (half_idx / DIM_HEAD)
            t = jnp.arange(n, dtype=jnp.float32)
            freqs = t[:, None] * inv_freq[None, :]
            freqs = jnp.concatenate([freqs, freqs], axis=-1)
            base = (half_idx + 0.4 * DIM_HEAD) / (1.4 * DIM_HEAD)
            power = (t - n // 2) / float(WINDOW // 2)
            scale = base[None, :] ** power[:, None]
            scale = jnp.concatenate([scale, scale], axis=-1)
            cos, sin = (jnp.cos(freqs), jnp.sin(freqs))
            q = q * cos * scale + rotate_half(q) * sin * scale
            k = k * cos / scale + rotate_half(k) * sin / scale
            return (q, k)

        def local_attention(q, k, v):
            b, h, n, d = q.shape
            w = n // WINDOW
            bq = q.reshape(b, h, w, WINDOW, d) * QK_SCALE
            bk = k.reshape(b, h, w, WINDOW, d)
            bv = v.reshape(b, h, w, WINDOW, d)

            def look_around(t):
                p = jnp.pad(t, ((0, 0), (0, 0), (1, 0), (0, 0), (0, 0)))
                return jnp.concatenate([p[:, :, :w], p[:, :, 1:]], axis=3)
            bk, bv = (look_around(bk), look_around(bv))
            bt = jnp.arange(n).reshape(w, WINDOW)
            btp = jnp.pad(bt, ((1, 0), (0, 0)), constant_values=-1)
            btk = jnp.concatenate([btp[:w], btp[1:]], axis=1)
            sim = jnp.einsum('bhwid,bhwjd->bhwij', bq, bk)
            i = bt[:, :, None]
            j = btk[:, None, :]
            mask = (i < j) | (i > j + WINDOW) | (j == -1)
            sim = jnp.where(mask, -jnp.finfo(sim.dtype).max, sim)
            attn = jax.nn.softmax(sim, axis=-1)
            out = jnp.einsum('bhwij,bhwjd->bhwid', attn, bv)
            return out.reshape(b, h, n, d)

        def _layer(x, wqkv, qs, ksc, wo, lg, lb, w1, b1, w2, b2):
            b, n, _ = x.shape
            h = shift_token(x)
            qkv = h @ wqkv
            q, k, v = jnp.split(qkv, 3, axis=-1)
            to_heads = lambda t: t.reshape(b, n, HEADS, DIM_HEAD).transpose(0, 2, 1, 3)
            q, k, v = (to_heads(q), to_heads(k), to_heads(v))
            q = l2norm(q) * qs
            k = l2norm(k) * ksc
            q, k = rotary_xpos(q, k)
            o = local_attention(q, k, v)
            o = o.transpose(0, 2, 1, 3).reshape(b, n, INNER)
            x = x + o @ wo
            h = shift_token(x)
            mu = h.mean(-1, keepdims=True)
            var = h.var(-1, keepdims=True)
            h = (h - mu) / jnp.sqrt(var + 1e-05) * lg + lb
            h = h @ w1 + b1
            a, g = jnp.split(h, 2, axis=-1)
            h = a * jax.nn.gelu(g, approximate=False)
            x = x + h @ w2 + b2
            return x
        key = jax.random.key(seed)
        ks = jax.random.split(key, 6)
        return {'x': jax.random.normal(ks[0], (B, N, DIM), jnp.float32), 'wqkv': jax.random.normal(ks[1], (DEPTH, DIM, 3 * INNER), jnp.float32) * 0.02, 'q_scale': jnp.ones((DEPTH, DIM_HEAD), jnp.float32), 'k_scale': jnp.ones((DEPTH, DIM_HEAD), jnp.float32), 'wo': jax.random.normal(ks[2], (DEPTH, INNER, DIM), jnp.float32) * 0.02, 'ln_g': jnp.ones((DEPTH, DIM), jnp.float32), 'ln_b': jnp.zeros((DEPTH, DIM), jnp.float32), 'w1': jax.random.normal(ks[3], (DEPTH, DIM, 2 * HID), jnp.float32) * 0.02, 'b1': jnp.zeros((DEPTH, 2 * HID), jnp.float32), 'w2': jax.random.normal(ks[4], (DEPTH, HID, DIM), jnp.float32) * 0.02, 'b2': jnp.zeros((DEPTH, DIM), jnp.float32)}
    _L0_ffn_all = _L0_ffn_setup()
    _L0_ffn_in = {k: v for k, v in _L0_ffn_all.items() if k in ('wqkv', 'q_scale', 'k_scale', 'wo', 'ln_g', 'ln_b', 'w1', 'b1', 'w2', 'b2')}
    del _L0_ffn_all
    return {'x': x, 'ctx_1024': ctx_1024, 'mask_BxS2_bk0': mask_BxS2_bk0, 'g_xattn': g_xattn, 'g_ffn': g_ffn, 'L0_xattn_Wq': _L0_xattn_in['Wq'], 'L0_xattn_Wkv': _L0_xattn_in['Wkv'], 'L0_xattn_Wout': _L0_xattn_in['Wout'], 'L0_xattn_bout': _L0_xattn_in['bout'], 'L0_xattn_g_media': _L0_xattn_in['g_media'], 'L0_xattn_b_media': _L0_xattn_in['b_media'], 'L0_xattn_g_latent': _L0_xattn_in['g_latent'], 'L0_xattn_b_latent': _L0_xattn_in['b_latent'], 'L0_ffn_wqkv': _L0_ffn_in['wqkv'], 'L0_ffn_q_scale': _L0_ffn_in['q_scale'], 'L0_ffn_k_scale': _L0_ffn_in['k_scale'], 'L0_ffn_wo': _L0_ffn_in['wo'], 'L0_ffn_ln_g': _L0_ffn_in['ln_g'], 'L0_ffn_ln_b': _L0_ffn_in['ln_b'], 'L0_ffn_w1': _L0_ffn_in['w1'], 'L0_ffn_b1': _L0_ffn_in['b1'], 'L0_ffn_w2': _L0_ffn_in['w2'], 'L0_ffn_b2': _L0_ffn_in['b2']}

def reference(x, ctx_1024, mask_BxS2_bk0, g_xattn, g_ffn, L0_xattn_Wq, L0_xattn_Wkv, L0_xattn_Wout, L0_xattn_bout, L0_xattn_g_media, L0_xattn_b_media, L0_xattn_g_latent, L0_xattn_b_latent, L0_ffn_wqkv, L0_ffn_q_scale, L0_ffn_k_scale, L0_ffn_wo, L0_ffn_ln_g, L0_ffn_ln_b, L0_ffn_w1, L0_ffn_b1, L0_ffn_w2, L0_ffn_b2):
    import jax
    import jax.numpy as jnp

    def _L0_xattn_ref(x, latents, mask, Wq, Wkv, Wout, bout, g_media, b_media, g_latent, b_latent):
        import jax, jax.numpy as jnp
        import numpy as np
        DIM = 128
        DIM_HEAD = 64
        NUM_HEADS = 16
        HIDDEN = DIM_HEAD * NUM_HEADS
        EPS = 1e-05

        def layer_norm(t, gamma, beta):
            mu = jnp.mean(t, axis=-1, keepdims=True)
            var = jnp.var(t, axis=-1, keepdims=True)
            return (t - mu) * jax.lax.rsqrt(var + EPS) * gamma + beta
        B, F, _ = x.shape
        Q = latents.shape[1]
        scale = DIM_HEAD ** (-0.5)
        xn = layer_norm(x, g_media, b_media)
        ln = layer_norm(latents, g_latent, b_latent)
        q = (ln @ Wq).reshape(B, Q, NUM_HEADS, DIM_HEAD).transpose(0, 2, 1, 3) * scale
        kv_input = jnp.concatenate([xn, ln], axis=1)
        kv = kv_input @ Wkv
        k, v = jnp.split(kv, 2, axis=-1)
        k = k.reshape(B, F + Q, NUM_HEADS, DIM_HEAD).transpose(0, 2, 1, 3)
        v = v.reshape(B, F + Q, NUM_HEADS, DIM_HEAD).transpose(0, 2, 1, 3)
        sim = jnp.einsum('bhqd,bhfd->bhqf', q, k)
        latent_mask = jnp.zeros((B, Q), dtype=bool)
        full_mask = jnp.concatenate([mask, latent_mask], axis=1)
        max_neg = -jnp.finfo(sim.dtype).max
        sim = jnp.where(full_mask[:, None, None, :], max_neg, sim)
        alphas = jax.nn.softmax(sim, axis=-1)
        out = jnp.einsum('bhqf,bhfv->bhqv', alphas, v)
        out = out.transpose(0, 2, 1, 3).reshape(B, Q, HIDDEN)
        return out @ Wout + bout

    def _L0_ffn_ref(x, wqkv, q_scale, k_scale, wo, ln_g, ln_b, w1, b1, w2, b2):
        import jax, jax.numpy as jnp
        import numpy as np
        DIM = 128
        DEPTH = 2
        HEADS = 8
        DIM_HEAD = 64
        WINDOW = 64
        INNER = HEADS * DIM_HEAD
        HID = int(DIM * 4 * 2 / 3)
        B, N = (2, 1024)
        QK_SCALE = 8.0

        def shift_token(t):
            t1, t2 = jnp.split(t, 2, axis=-1)
            t2 = jnp.pad(t2, ((0, 0), (1, 0), (0, 0)))[:, :-1]
            return jnp.concatenate([t1, t2], axis=-1)

        def l2norm(t):
            return t / jnp.clip(jnp.linalg.norm(t, axis=-1, keepdims=True), 1e-12)

        def rotate_half(x):
            x1, x2 = jnp.split(x, 2, axis=-1)
            return jnp.concatenate([-x2, x1], axis=-1)

        def rotary_xpos(q, k):
            n = q.shape[-2]
            half_idx = jnp.arange(0, DIM_HEAD, 2, dtype=jnp.float32)
            inv_freq = 1.0 / 10000.0 ** (half_idx / DIM_HEAD)
            t = jnp.arange(n, dtype=jnp.float32)
            freqs = t[:, None] * inv_freq[None, :]
            freqs = jnp.concatenate([freqs, freqs], axis=-1)
            base = (half_idx + 0.4 * DIM_HEAD) / (1.4 * DIM_HEAD)
            power = (t - n // 2) / float(WINDOW // 2)
            scale = base[None, :] ** power[:, None]
            scale = jnp.concatenate([scale, scale], axis=-1)
            cos, sin = (jnp.cos(freqs), jnp.sin(freqs))
            q = q * cos * scale + rotate_half(q) * sin * scale
            k = k * cos / scale + rotate_half(k) * sin / scale
            return (q, k)

        def local_attention(q, k, v):
            b, h, n, d = q.shape
            w = n // WINDOW
            bq = q.reshape(b, h, w, WINDOW, d) * QK_SCALE
            bk = k.reshape(b, h, w, WINDOW, d)
            bv = v.reshape(b, h, w, WINDOW, d)

            def look_around(t):
                p = jnp.pad(t, ((0, 0), (0, 0), (1, 0), (0, 0), (0, 0)))
                return jnp.concatenate([p[:, :, :w], p[:, :, 1:]], axis=3)
            bk, bv = (look_around(bk), look_around(bv))
            bt = jnp.arange(n).reshape(w, WINDOW)
            btp = jnp.pad(bt, ((1, 0), (0, 0)), constant_values=-1)
            btk = jnp.concatenate([btp[:w], btp[1:]], axis=1)
            sim = jnp.einsum('bhwid,bhwjd->bhwij', bq, bk)
            i = bt[:, :, None]
            j = btk[:, None, :]
            mask = (i < j) | (i > j + WINDOW) | (j == -1)
            sim = jnp.where(mask, -jnp.finfo(sim.dtype).max, sim)
            attn = jax.nn.softmax(sim, axis=-1)
            out = jnp.einsum('bhwij,bhwjd->bhwid', attn, bv)
            return out.reshape(b, h, n, d)

        def _layer(x, wqkv, qs, ksc, wo, lg, lb, w1, b1, w2, b2):
            b, n, _ = x.shape
            h = shift_token(x)
            qkv = h @ wqkv
            q, k, v = jnp.split(qkv, 3, axis=-1)
            to_heads = lambda t: t.reshape(b, n, HEADS, DIM_HEAD).transpose(0, 2, 1, 3)
            q, k, v = (to_heads(q), to_heads(k), to_heads(v))
            q = l2norm(q) * qs
            k = l2norm(k) * ksc
            q, k = rotary_xpos(q, k)
            o = local_attention(q, k, v)
            o = o.transpose(0, 2, 1, 3).reshape(b, n, INNER)
            x = x + o @ wo
            h = shift_token(x)
            mu = h.mean(-1, keepdims=True)
            var = h.var(-1, keepdims=True)
            h = (h - mu) / jnp.sqrt(var + 1e-05) * lg + lb
            h = h @ w1 + b1
            a, g = jnp.split(h, 2, axis=-1)
            h = a * jax.nn.gelu(g, approximate=False)
            x = x + h @ w2 + b2
            return x
        for l in range(DEPTH):
            x = _layer(x, wqkv[l], q_scale[l], k_scale[l], wo[l], ln_g[l], ln_b[l], w1[l], b1[l], w2[l], b2[l])
        return x
    x = x + jnp.tanh(g_xattn[0]) * _L0_xattn_ref(ctx_1024, _layernorm(x, axis=-1), mask_BxS2_bk0, L0_xattn_Wq, L0_xattn_Wkv, L0_xattn_Wout, L0_xattn_bout, L0_xattn_g_media, L0_xattn_b_media, L0_xattn_g_latent, L0_xattn_b_latent)
    x = x + jnp.tanh(g_ffn[0]) * _L0_ffn_ref(_layernorm(x, axis=-1), L0_ffn_wqkv, L0_ffn_q_scale, L0_ffn_k_scale, L0_ffn_wo, L0_ffn_ln_g, L0_ffn_ln_b, L0_ffn_w1, L0_ffn_b1, L0_ffn_w2, L0_ffn_b2)
    return x

_drawn_inputs = setup_inputs


def setup_inputs(seed=0):
    import zlib

    import numpy as np

    out = dict(_drawn_inputs(seed))
    spreads = {'L0_xattn_bout': (0.0, 0.1),
     'L0_xattn_g_media': (1.0, 0.2),
     'L0_xattn_b_media': (0.0, 0.1),
     'L0_xattn_g_latent': (1.0, 0.2),
     'L0_xattn_b_latent': (0.0, 0.1),
     'L0_ffn_q_scale': (1.0, 0.2),
     'L0_ffn_k_scale': (1.0, 0.593),
     'L0_ffn_ln_g': (1.0, 0.6),
     'L0_ffn_ln_b': (0.0, 0.77),
     'L0_ffn_b1': (0.0, 0.1),
     'L0_ffn_b2': (0.0, 0.1)}
    factors = {}
    for name, (base, spread) in spreads.items():
        noise = np.random.default_rng([zlib.crc32(name.encode()), seed]).standard_normal(out[name].shape)
        drawn = base * np.exp(spread * noise) if base else spread * noise
        out[name] = jnp.asarray(drawn.astype(out[name].dtype))
    for name, factor in factors.items():
        out[name] = (out[name] * factor).astype(out[name].dtype)
    return out
```

```python
import concourse.bass as bass
from concourse import mybir
from contextlib import ExitStack

fp32 = mybir.dt.float32
bf16 = mybir.dt.bfloat16
fp32r = mybir.dt.float32r
u8 = mybir.dt.uint8
ALU = mybir.AluOpType
ACT = mybir.ActivationFunctionType
AX = mybir.AxisListType

BATCH, SEQ, DIM = 64, 64, 128
P = 128
PAIRS = BATCH // 2
XH, DH = 16, 64
HPB = XH // 2
KEYS = 2 * SEQ
FH = 8
INNER = FH * DH
LAYERS = 2
HID = DIM * 4 * 2 // 3
HB = [(0, 128), (128, 128), (256, HID - 256)]
GROUP = 4
GROUPS = PAIRS // GROUP
EPS = 1e-5
NEG = -1e30
X_SCALE = DH ** -0.5
F_SCALE = 8.0


def valid(i, n):
    return not isinstance(i, int) or 0 <= i < n


def wait(eng, sem, value):
    if not isinstance(value, int) or value > 0:
        eng.wait_ge(sem, value)


def att_loop(eng, tile, base, n):
    def need(sem, value):
        if not isinstance(value, int) or value > 0:
            eng.wait_ge(sem, base + value)
    for t in range(6):
        tile(need, t, t % 2)
    with eng.Fori(3, n // 2 - 1) as k:
        tile(need, k * 2, 0)
        tile(need, k * 2 + 1, 1)
    for t in range(n - 2, n + 4):
        tile(need, t, t % 2)


def mlp_loop(eng, group, base, base3, n):
    def need(sem, value, triple=False):
        if not isinstance(value, int) or value > 0:
            eng.wait_ge(sem, (base3 if triple else base) + value)
    group(need, 0)
    group(need, 1)
    with eng.Fori(2, n) as g:
        group(need, g)
    group(need, n)


def moments(dve, stats, mean, var, tmp, n, sem, base):
    half = DIM // 2
    me, mo, ve_, vo = stats[:, 0:n, 1], stats[:, 0:n, 4], stats[:, 0:n, 2], stats[:, 0:n, 5]
    dve.tensor_tensor(tmp[:, 0:n], me, mo, ALU.subtract).then_inc(sem, 1)
    dve.wait_ge(sem, base + 1)
    dve.tensor_tensor(mean[:, 0:n], me, mo, ALU.add)
    dve.tensor_tensor(tmp[:, 0:n], tmp[:, 0:n], tmp[:, 0:n], ALU.mult)
    dve.tensor_tensor(var[:, 0:n], ve_, vo, ALU.add).then_inc(sem, 1)
    dve.wait_ge(sem, base + 2)
    dve.tensor_scalar(mean[:, 0:n], mean[:, 0:n], 0.5, None, ALU.mult)
    dve.tensor_scalar(tmp[:, 0:n], tmp[:, 0:n], 0.25, None, ALU.mult).then_inc(sem, 1)
    dve.wait_ge(sem, base + 3)
    dve.scalar_tensor_tensor(tmp[:, 0:n], var[:, 0:n], 1.0 / (2 * half), tmp[:, 0:n],
                             ALU.mult, ALU.add).then_inc(sem, 1)
    dve.wait_ge(sem, base + 4)
    dve.tensor_scalar(var[:, 0:n], tmp[:, 0:n], EPS, None, ALU.add).then_inc(sem, 1)
    dve.wait_ge(sem, base + 5)


def build(nc, x, ctx_t, mask, g_x, g_f, wq, wkv, wout, bout, g_media, b_media, g_latent, b_latent,
          wqkv, q_scale, k_scale, wo, ln_g, ln_b, w1, b1, w2, b2, ident_d, shift_d, causal_d,
          rot_d, out, pairs=PAIRS):
    groups = pairs // GROUP
    stack = ExitStack()
    with stack:
        stack.enter_context(nc.allow_non_contiguous_dma(reason="parameters that lie one to a partition"))

        def sb(name, shape, dt=fp32):
            return stack.enter_context(nc.sbuf_tensor(name, shape, dt))

        def sem(name):
            return stack.enter_context(nc.semaphore(name))

        NB = 2 * pairs
        XC = sb("XC", [P, BATCH, DIM])
        X1 = sb("X1", [P, pairs, DIM])
        Y = XC[:, 0:pairs, :]
        XS = XC[:, PAIRS:BATCH, :].rearrange("p (k a) d -> p k (a d)", k=4)
        ident = sb("ident", [P, P])
        identb = sb("identb", [P, P], bf16)
        shift = sb("shift", [P, P])
        causal = sb("causal", [P, SEQ], bf16)
        ones_row = sb("ones_row", [1, P], bf16)
        mask_row = sb("mask_row", [1, NB, KEYS], bf16)
        G = sb("G", [P, DIM])
        Bt = sb("Bt", [P, DIM])
        bout_t = sb("bout_t", [P, DIM])
        gates = sb("gates", [P, 2])
        tg = sb("tg", [P, 2])
        mhb = sb("mhb", [P, NB])
        scratch = sb("scratch", [P, 8])
        lnp = sb("lnp", [P, 2 * LAYERS])
        ST = sb("ST", [P, NB, 6])
        ST1 = sb("ST1", [P, pairs, 6])
        mean = sb("mean", [P, NB])
        rstd = sb("rstd", [P, NB])
        tmpA = sb("tmpA", [P, NB])
        tmpB = sb("tmpB", [P, NB])
        Am = sb("Am", [P, XH, DIM])
        Bm = sb("Bm", [P, XH, DIM])
        XN = sb("XN", [P, 2, 2, DIM])
        KN = sb("KN", [P, 2, 2, DIM])
        KX = sb("KX", [P, 2, 2, DIM])
        KT = sb("KT", [P, 2, 2, KEYS])
        QP = sb("QP", [P, 2, 2, XH, SEQ])
        YT = sb("YT", [P, 2, XH, 2, SEQ])
        QPf = QP[:, :, :, :, :].rearrange("p a b h q -> p (a b h q)")
        YTf = YT[:, :, :, :, :].rearrange("p a h b q -> p (a h b q)")
        Wq = QPf[:, 0:XH * DH]
        Wkv = QPf[:, XH * DH:3 * XH * DH]
        Wout = QPf[:, 3 * XH * DH:4 * XH * DH].rearrange("p (c o) -> p c o", o=DIM)
        WT = YTf[:, 0:3 * XH * DH].rearrange("p (w c o) -> p w c o", w=3, o=DIM)
        mask_u8 = YTf[0:1, 3 * XH * DH:3 * XH * DH + NB * SEQ // 4].bitcast(u8).rearrange("p (b s) -> p b s", s=SEQ)
        Pr = sb("Pr", [P, 4, 4, KEYS])
        PTs = sb("PTs", [P, 2, 512])
        mx = sb("mx", [P, 4, 4])
        sm = sb("sm", [P, 4, 4])
        rc = sb("rc", [P, 4, 4])
        Wqkv = sb("Wv", [P, INNER])
        Wh = sb("Wh", [P, 2 * INNER], fp32r)
        Wl = sb("Wl", [P, 2 * INNER], fp32r)
        Wo = sb("Wo", [P, FH // 2, DIM])
        W1 = sb("W1", [P, 2 * HID])
        W2 = sb("W2", [P, 3, DIM])
        b1a = sb("b1a", [P, 3])
        b1g = sb("b1g", [P, 3])
        b2t = sb("b2t", [P, DIM])
        lng = sb("lng", [P, 1])
        lnb = sb("lnb", [P, 1])
        rot = sb("rot", [P, 4, DH])
        qks = sb("qks", [P, 2, DH])
        RT1 = sb("RT1", [P, 2, DH])
        RT2 = sb("RT2", [P, 2, DH])
        yc = sb("yc", [P, 2, DIM])
        hT = sb("hT", [P, 2, P])
        hTh = sb("hTh", [P, 2, P], fp32r)
        hTl = sb("hTl", [P, 2, P], fp32r)
        sq = XS[:, 0, :].rearrange("p (h d) -> p h d", d=DH)
        ss = sb("ss", [P, 2, 16])
        rn = sb("rn", [P, 2, 16])
        qn = XS[:, 1, :].rearrange("p (w h d) -> p w h d", w=2, d=DH)
        ra = XS[:, 2, :].rearrange("p (w h d) -> p w h d", w=2, d=DH)
        rb = XS[:, 3, :].rearrange("p (w h d) -> p w h d", w=2, d=DH)
        Wraw = XS[:, 1, :]
        FT = sb("FT", [P, 8, P])
        V = sb("V", [P, 2, 2, 4, DH])
        Pf = sb("Pf", [P, 2, 4, 2, SEQ])
        fm = sb("fm", [P, 2, 4, 2])
        fs = sb("fs", [P, 2, 4, 2])
        fr = sb("fr", [P, 2, 4, 2])
        PTf = sb("PTf", [P, 4, P])
        Of = sb("Of", [P, 4, 2, DH])
        OTf = sb("OTf", [P, 4, P])
        ST2 = sb("ST2", [P, GROUP, 6])
        MV = sb("MV", [P, GROUP, 2])
        ve = sb("ve", [P, GROUP])
        rs = sb("rs", [P, GROUP])
        hn = sb("hn", [P, GROUP, DIM])
        nT = sb("nT", [P, 512])
        ge = QPf[:, 0:3 * 512].rearrange("p (k n) -> p k n", k=3)
        u = QPf[:, 3 * 512:6 * 512].rearrange("p (k n) -> p k n", k=3)

        bank = [stack.enter_context(nc.psum_tensor(f"bank{i}", [P, 512], fp32)) for i in range(8)]

        s_w = sem("weights_loaded")
        s_ctab = sem("constants_loaded")
        s_in = [sem(f"tokens_loaded{i}") for i in range(4)]
        s_xp = sem("pair_tiles_loaded")
        s_set = sem("vector_setup_done")
        s_pset = sem("pool_setup_done")
        s_aset = sem("scalar_setup_done")
        s_tset = sem("tensor_setup_done")

        block = stack.enter_context(nc.Block())
        N_CONST = 14

        s_out = sem("output_stored")
        s_fin = sem("final_tile_ready")
        s_lw = sem("attention_weights_loaded")
        s_mw = sem("mlp_weights_loaded")
        s_A = sem("attention_phase_done")
        s_M = sem("mlp_phase_done")
        s_rt = sem("rotary_tables_built")
        s_bn = sem("row_statistics")
        s_ws = sem("attention_weights_split")
        s_bz = sem("mask_row_zeroed")
        s_pm = sem("pool_constants")
        LW, MW = 5, 11

        @block.sync
        def _(sp):
            sp.dma_start(Wq[:, :], wq).then_inc(s_w, 16)
            sp.dma_start(Wkv[:, :], wkv).then_inc(s_w, 16)
            sp.dma_start(Wout[:, :, :], wout.rearrange("(c p) o -> p c o", p=P)).then_inc(s_w, 16)
            for i in range(4):
                q = NB // 4
                r = slice(i * q, (i + 1) * q)
                sp.dma_start(XC[0:SEQ, r, :], ctx_t[r].rearrange("b s d -> s b d")).then_inc(s_in[i], 16)
                sp.dma_start(XC[SEQ:P, r, :], x[r].rearrange("b s d -> s b d")).then_inc(s_in[i], 16)
            sp.dma_start(X1[:, :, :], x.rearrange("(t b) s d -> (b s) t d", b=2)).then_inc(s_xp, 16)
            with sp.Fori(0, LAYERS) as lay:
                sp.wait_ge(s_A, lay * 1 + 1)
                wl = wqkv[bass.ds(lay, 1)].rearrange("l p n -> (l p) n")
                sp.dma_start(Wraw, wl[:, 0:2 * INNER]).then_inc(s_lw, 16)
                sp.dma_start(Wqkv[:, :], wl[:, 2 * INNER:]).then_inc(s_lw, 16)
                sp.dma_start(Wo[:, :, :], wo[bass.ds(lay, 1)].rearrange("l (c p) o -> p (l c) o", p=P)).then_inc(s_lw, 16)
                sp.dma_start(qks[:, 0, :], q_scale[bass.ds(lay, 1), :].to_broadcast([P, DH])).then_inc(s_lw, 16)
                sp.dma_start(qks[:, 1, :], k_scale[bass.ds(lay, 1), :].to_broadcast([P, DH])).then_inc(s_lw, 16)
                sp.wait_ge(s_M, lay * 1 + 1)
                sp.dma_start(W1[:, :], w1[bass.ds(lay, 1)].rearrange("l p n -> (l p) n")).then_inc(s_mw, 16)
                w2l = w2[bass.ds(lay, 1)].rearrange("l k o -> (l k) o")
                b1l = b1[bass.ds(lay, 1), :].rearrange("l k -> k l")
                for j, (h0, hn_) in enumerate(HB):
                    sp.dma_start(W2[0:hn_, j, :], w2l[h0:h0 + hn_, :]).then_inc(s_mw, 16)
                    sp.dma_start(b1a[0:hn_, j:j + 1], b1l[h0:h0 + hn_, :]).then_inc(s_mw, 16)
                    sp.dma_start(b1g[0:hn_, j:j + 1], b1l[HID + h0:HID + h0 + hn_, :]).then_inc(s_mw, 16)
                sp.dma_start(b2t[:, :], b2[bass.ds(lay, 1), :].to_broadcast([P, DIM])).then_inc(s_mw, 16)
            NST = 4
            for i in range(NST):
                q = pairs // NST
                sp.wait_ge(s_fin, i + 1)
                sp.dma_start(out.rearrange("(t b) s d -> (b s) t d", b=2)[:, i * q:(i + 1) * q, :],
                             Y[:, i * q:(i + 1) * q, :]).then_inc(s_out, 16)
            sp.wait_ge(s_out, 16 * NST)

        s_S, s_max, s_sub, s_exp = sem("scores"), sem("maxima"), sem("shifted"), sem("exps")
        s_sum, s_rec, s_pn = sem("sums"), sem("reciprocals"), sem("probs_normalised")
        s_PT, s_PTe = sem("probs_transposed"), sem("probsT_in_sbuf")
        s_Y, s_Ye = sem("mixed_keys"), sem("mixed_keys_in_sbuf")
        s_Q, s_Qe = sem("queries"), sem("queries_in_sbuf")
        s_XN, s_KG, s_KN = sem("tokens_normalised"), sem("keys_scaled"), sem("keys_ready")
        s_KT, s_KTe, s_KX = sem("keys_transposed"), sem("keysT_in_sbuf"), sem("keys_copied")
        s_OUT, s_xa, s_x1 = sem("cross_out"), sem("cross_out_added"), sem("x1_ready")
        S_BANK, Q_BANK, PT_BANK, Y_BANK, OUT_BANK, KT_BANK = (0, 1), (2, 3), 4, 5, 6, 7
        STEPS = 4 * pairs

        names = ["yc", "h", "he", "qk", "sqd", "ssd", "rnd", "qnd", "rad", "rbd", "v", "ve",
                 "f", "fe", "s", "m", "sb", "e", "su", "r", "pt", "pte", "o", "oe", "ot",
                 "ote", "wo", "res", "cl", "hh", "hl"]
        label = {"yc": "copied", "h": "hT_psum", "he": "hT_sbuf", "qk": "qk_psum", "sqd": "squares",
                 "ssd": "norms2", "rnd": "inv_norms", "qnd": "qk_normed", "rad": "cos_part",
                 "rbd": "sin_part", "v": "v_psum", "ve": "v_sbuf", "f": "qkT_psum", "fe": "qkT_sbuf",
                 "s": "f_scores", "m": "f_max", "sb": "f_shifted", "e": "f_exp", "su": "f_sum",
                 "r": "f_rec", "pt": "f_probsT_psum", "pte": "f_probsT_sbuf", "o": "f_out_psum",
                 "oe": "f_out_sbuf", "ot": "f_outT_psum", "ote": "f_outT_sbuf", "wo": "f_proj",
                 "res": "f_residual", "cl": "norms2_clipped",
                 "hh": "hT_high_part", "hl": "hT_low_part"}
        A = {k: sem(label[k]) for k in names}
        mnames = {"h": "m_shifted", "bs": "m_stats", "ba": "m_aggr", "ve": "m_var_eps", "rs": "m_rstd",
                  "hn": "m_normed", "t": "m_normedT", "te": "m_normedT_sbuf", "a": "m_up", "g": "m_gelu",
                  "u": "m_gated", "d": "m_down", "res": "m_residual", "r2": "m_biased"}
        M = {k: sem(v) for k, v in mnames.items()}

        @block.tensor
        def _(pe):
            pe.wait_ge(s_ctab, 16 * N_CONST)
            pe.wait_ge(s_w, 48)
            for g in range(6):
                for i in range(4):
                    blk = 4 * (g % 2) + i
                    src = Wq if g < 2 else Wkv
                    c = (blk + (HPB if g >= 4 else 0)) * P
                    last = nc.tensor.transpose(bank[g][:, i * P:(i + 1) * P], src[:, c:c + P], ident[:, :])
                last.then_inc(s_tset, 1)
            for g in range(8):
                par, quad, isb = g // 2 % 2, g % 2, g // 4
                pe.wait_ge(s_aset, 3 if isb == 0 else 6)
                pe.wait_ge(s_set, 3)
                r = slice(64 * par, 64 * par + 64)
                for i in range(4):
                    hb = 4 * quad + i
                    if isb:
                        l, rr = WT[r, 2, hb, :], Wout[r, hb, :]
                    else:
                        l, rr = WT[r, 0, hb, :], WT[r, 1, hb, :]
                    last = nc.tensor.matmul(bank[g][:, i * P:(i + 1) * P], l, rr, start=True, stop=True)
                last.then_inc(s_tset, 1)

            def keys_transposed(t, par):
                pe.wait_ge(s_KN, t + 1)
                wait(pe, s_KTe, t)
                for b in range(2):
                    last = nc.tensor.transpose(bank[KT_BANK][:, b * KEYS:(b + 1) * KEYS],
                                               KN[:, par, b, :], ident[:, :])
                last.then_inc(s_KT, 1)

            def queries(t, par, c):
                pe.wait_ge(s_KTe, t + 1)
                wait(pe, s_Qe, 4 * t + c - 1)
                for i in range(4):
                    last = nc.tensor.matmul(bank[Q_BANK[c % 2]][:, i * P:(i + 1) * P], Am[:, 4 * c + i, :],
                                            KT[:, par, :, SEQ:KEYS], start=True, stop=True)
                last.then_inc(s_Q, 1)

            def probs_transposed(n, uu):
                pe.wait_ge(s_pn, n + 1)
                wait(pe, s_PTe, n)
                for i in range(4):
                    last = nc.tensor.transpose(bank[PT_BANK][:, i * P:(i + 1) * P], Pr[:, uu, i, :], ident[:, :])
                last.then_inc(s_PT, 1)

            def scores(t, par, uu):
                n, b, half = 4 * t + uu, uu // 2, uu % 2
                pe.wait_ge(s_Qe, 4 * t + 2 * half + 2)
                pe.wait_ge(s_KTe, t + 1)
                wait(pe, s_sub, n - 1)
                for i in range(4):
                    h = 8 * half + 2 * i
                    nc.tensor.matmul(bank[S_BANK[uu % 2]][:, i * P:(i + 1) * P], QP[:, par, b, h:h + 2, :],
                                     KT[:, par, b, :], start=(i == 0), stop=False, skip_group_check=True)
                m = mask_row[0:1, bass.ds(2 * t + b, 1), :].to_broadcast([1, 4, KEYS])
                nc.tensor.matmul(bank[S_BANK[uu % 2]][:, :].rearrange("p (a k) -> p a k", a=4), ones_row[:, :], m,
                                 start=False, stop=True, skip_group_check=True).then_inc(s_S, 1)

            def mixed(t, par, uu):
                n, b = 4 * t + uu, uu // 2
                pe.wait_ge(s_PTe, n + 1)
                pe.wait_ge(s_KX, t + 1)
                wait(pe, s_Ye, n)
                nc.tensor.matmul(bank[Y_BANK][:, :], KX[:, par, b, :], PTs[:, uu % 2, :],
                                 start=True, stop=True).then_inc(s_Y, 1)

            def cross_out(t, par, half):
                if half == 0:
                    pe.wait_ge(s_Ye, 4 * t + 4)
                    wait(pe, s_xa, t)
                for h in range(8 * half, 8 * half + 8):
                    last = nc.tensor.matmul(bank[OUT_BANK][:, 0:DIM], YT[:, par, h, :, :], Bm[:, h, :],
                                            start=(h == 0), stop=(h == XH - 1))
                if half == 1:
                    last.then_inc(s_OUT, 1)

            pe.wait_ge(s_set, 8)
            pe.wait_ge(s_aset, 10)
            keys_transposed(0, 0)
            for c in range(4):
                queries(0, 0, c)
            keys_transposed(1, 1)

            def body(t0):
                for dt in range(2):
                    t = t0 + dt
                    par = dt
                    for uu in range(4):
                        tl, ul = (t, uu - 2) if uu >= 2 else (t - 1, uu + 2)
                        lpar = par if uu >= 2 else 1 - par
                        if valid(tl, pairs):
                            probs_transposed(4 * tl + ul, ul)
                        if valid(t, pairs):
                            scores(t, par, uu)
                        if valid(t + 1, pairs):
                            queries(t + 1, 1 - par, uu)
                        if valid(tl, pairs):
                            mixed(tl, lpar, ul)
                        if uu >= 2 and valid(t - 1, pairs):
                            cross_out(t - 1, 1 - par, uu - 2)
                        if uu == 3 and valid(t + 2, pairs):
                            keys_transposed(t + 2, par)

            body(0)
            with pe.Fori(1, pairs // 2 - 1) as k:
                body(k * 2)
            body(pairs - 2)
            body(pairs)

            def att_tile(need, t, p):
                q = 1 - p
                if valid(t, pairs):
                    need(A["yc"], t + 1)
                    need(A["ve"], t - 1)
                    nc.tensor.matmul(bank[2][0:64, 0:P], yc[:, p, 0:64], ident[:, :], start=True, stop=True)
                    nc.tensor.matmul(bank[2][64:P, 0:P], yc[:, p, 64:P], shift[:, :],
                                     start=True, stop=True).then_inc(A["h"], 1)
                if valid(t - 2, pairs):
                    j = t - 2
                    need(A["oe"], j - 1)
                    need(A["rad"], j + 1)
                    need(A["rbd"], j + 1)
                    for c in range(8):
                        dst = bank[3 + c // 4][:, (c % 4) * P:(c % 4 + 1) * P]
                        w, hb = c // 4, c % 4
                        nc.tensor.matmul(dst, ra[:, w, 2 * hb:2 * hb + 2, :], ident[:, :],
                                         start=True, stop=False, is_transpose=True)
                        last = nc.tensor.matmul(dst, rb[:, w, 2 * hb:2 * hb + 2, :], ident[:, :],
                                                start=False, stop=True, is_transpose=True)
                    last.then_inc(A["f"], 1)
                if valid(t - 3, pairs):
                    j = t - 3
                    need(A["r"], j + 1)
                    need(A["pte"], j)
                    need(A["res"], j - 1)
                    for c in range(4):
                        last = nc.tensor.transpose(bank[7][:, c * P:(c + 1) * P], Pf[:, q, c, :, :], ident[:, :])
                    last.then_inc(A["pt"], 1)
                if valid(t, pairs):
                    need(A["hl"], t + 1)
                    need(A["qnd"], t)
                    need(A["sqd"], t)
                    for w in range(2):
                        for k, (l, r) in enumerate(((hTh, Wh), (hTh, Wl), (hTl, Wh))):
                            last = nc.tensor.matmul(bank[w][:, :], l[:, p, :], r[:, w * 512:(w + 1) * 512],
                                                    start=(k == 0), stop=(k == 2))
                    last.then_inc(A["qk"], 1)
                if valid(t - 2, pairs):
                    j = t - 2
                    need(A["fe"], j + 1)
                    need(A["sb"], j)
                    for e in range(2):
                        nc.tensor.matmul(bank[5 + e][:, 0:256].rearrange("p (c k) -> p c k", c=4), identb[:, :],
                                         causal[:, None, :].to_broadcast([P, 4, SEQ]),
                                         start=True, stop=False, skip_group_check=True)
                    for c in range(4):
                        for e in range(2):
                            for b in range(2):
                                r = slice(64 * e, 64 * e + 64)
                                last = nc.tensor.matmul(
                                    bank[5 + e][64 * b:64 * b + 64, c * SEQ:(c + 1) * SEQ],
                                    FT[r, c, 64 * b:64 * b + 64], FT[r, 4 + c, 64 * b:64 * b + 64],
                                    start=False, stop=(c == 3), skip_group_check=True)
                    last.then_inc(A["s"], 1)
                if valid(t - 4, pairs):
                    j = t - 4
                    need(A["oe"], j + 1)
                    need(A["pte"], min(j + 2, pairs) if isinstance(j, int) else j + 2)
                    need(A["res"], j)
                    for c in range(4):
                        last = nc.tensor.transpose(bank[7][:, c * P:(c + 1) * P], Of[:, c, :, :], ident[:, :])
                    last.then_inc(A["ot"], 1)
                if valid(t - 3, pairs):
                    j = t - 3
                    need(A["pte"], j + 1)
                    need(A["fe"], min(j + 2, pairs) if isinstance(j, int) else j + 2)
                    need(A["ve"], j + 1)
                    nc.tensor.matmul(bank[3][:, 256:256 + 8], identb[:, :], identb[:, 0:8], start=True, stop=True)
                    for c in range(4):
                        for e in range(2):
                            for b in range(2):
                                r = slice(64 * e, 64 * e + 64)
                                last = nc.tensor.matmul(
                                    bank[3 + e][64 * b:64 * b + 64, c * DH:(c + 1) * DH],
                                    PTf[r, c, 64 * b:64 * b + 64], V[r, q, b, c, :], start=True, stop=True)
                    last.then_inc(A["o"], 1)
                if valid(t - 1, pairs):
                    j = t - 1
                    need(A["he"], min(j + 2, pairs) if isinstance(j, int) else j + 2)
                    wv = Wqkv[:, :].rearrange("p (c e d) -> p c e d", e=2, d=DH)
                    nc.tensor.matmul(bank[2][:, 0:8], identb[:, :], identb[:, 0:8], start=True, stop=True)
                    for b in range(2):
                        for e in range(2):
                            last = nc.tensor.matmul(
                                bank[2][64 * e:64 * e + 64, b * 256:(b + 1) * 256].rearrange("p (c d) -> p c d", d=DH),
                                hT[:, q, 64 * b:64 * b + 64], wv[:, :, e, :], start=True, stop=True)
                    last.then_inc(A["v"], 1)
                if valid(t - 4, pairs):
                    j = t - 4
                    need(A["ote"], j + 1)
                    for c in range(4):
                        last = nc.tensor.matmul(bank[7][:, 0:DIM], OTf[:, c, :], Wo[:, c, :],
                                                start=(c == 0), stop=(c == 3))
                    last.then_inc(A["wo"], 1)

            def mlp_group(need, g):
                if valid(g, groups):
                    need(M["hn"], g)
                    ytile = Y[:, bass.ds(g * GROUP, GROUP), :]
                    hb = bank[0][:, :].rearrange("p (t d) -> p t d", t=GROUP)
                    nc.tensor.matmul(hb[:, :, 0:64], ident[:, :], ytile[:, :, 0:64], start=True, stop=False,
                                     skip_group_check=True)
                    nc.tensor.matmul(hb[:, :, 64:P], shift[:, :], ytile[:, :, 64:P],
                                     start=False, stop=True, skip_group_check=True).then_inc(M["h"], 1)
                if valid(g - 1, groups):
                    j = g - 1
                    need(M["hn"], j + 1)
                    need(M["te"], j)
                    for k in range(GROUP):
                        last = nc.tensor.transpose(bank[1][:, k * P:(k + 1) * P], hn[:, k, :], ident[:, :])
                    last.then_inc(M["t"], 1)
                    need(M["te"], j + 1)
                    for k, (h0, hw) in enumerate(HB):
                        need(M["u"], 3 * j + k - 2, True)
                        if k == 0:
                            need(M["res"], j)
                        nc.tensor.matmul(bank[2 + k][0:hw, :], W1[:, h0:h0 + hw], nT[:, :], start=True, stop=True)
                        nc.tensor.matmul(bank[5 + k][0:hw, :], W1[:, HID + h0:HID + h0 + hw], nT[:, :],
                                         start=True, stop=True).then_inc(M["a"], 1)
                    need(M["u"], 3 * j + 3, True)
                    for k in range(GROUP):
                        for c, (h0, hw) in enumerate(HB):
                            last = nc.tensor.matmul(bank[2][:, k * DIM:(k + 1) * DIM], u[0:hw, c, k * P:(k + 1) * P],
                                                    W2[0:hw, c, :], start=(c == 0), stop=(c == 2))
                    last.then_inc(M["d"], 1)

            with pe.Fori(0, LAYERS) as lay:
                li = lay * pairs
                gi = lay * groups
                gi3 = lay * (3 * groups)
                pe.wait_ge(s_lw, lay * (16 * LW) + 16 * LW)
                pe.wait_ge(s_ws, lay * 2 + 2)
                pe.wait_ge(s_M, lay * 1 + 1)
                att_loop(pe, att_tile, li, pairs)
                pe.wait_ge(s_mw, lay * (16 * MW) + 16 * MW)
                pe.wait_ge(s_A, lay * 1 + 2)
                mlp_loop(pe, mlp_group, gi, gi3, groups)

        @block.scalar
        def _(act):
            for dst, src in ((ident[:, :], ident_d), (shift[:, :], shift_d),
                             (rot[:, :, :], rot_d),
                             (G[0:SEQ, :], g_media[None, :].to_broadcast([SEQ, DIM])),
                             (G[SEQ:P, :], g_latent[None, :].to_broadcast([SEQ, DIM])),
                             (Bt[0:SEQ, :], b_media[None, :].to_broadcast([SEQ, DIM])),
                             (Bt[SEQ:P, :], b_latent[None, :].to_broadcast([SEQ, DIM])),
                             (bout_t[:, :], bout[None, :].to_broadcast([P, DIM])),
                             (gates[:, 0:1], g_x[None, :].to_broadcast([P, 1])),
                             (gates[:, 1:2], g_f[None, :].to_broadcast([P, 1])),
                             (hT[:, 0, 0:SEQ], causal_d),
                             (mask_u8[:, :, :], mask[None, :, :]),
                             (yc[:, 0, 0:LAYERS], ln_g.rearrange("l p -> p l")),
                             (yc[:, 0, 2:2 + LAYERS], ln_b.rearrange("l p -> p l"))):
                act.dma_start(dst, src).then_inc(s_ctab, 16)
            act.wait_ge(s_ctab, 16 * N_CONST)
            act.activation(tg[:, :], gates[:, :], ACT.Tanh).then_inc(s_aset, 1)
            for g in (0, 2, 4):
                act.wait_ge(s_tset, g + 1)
                act.activation(WT[:, g // 2, 0:4, :], bank[g][:, :], ACT.Copy).then_inc(s_aset, 1)
            act.wait_ge(s_ctab, 16 * N_CONST)
            act.activation(causal[:, :], hT[:, 0, 0:SEQ], ACT.Copy).then_inc(s_aset, 1)
            act.activation(identb[:, :], ident[:, :], ACT.Copy).then_inc(s_aset, 1)
            for k, g in enumerate((0, 2, 4, 6)):
                act.wait_ge(s_tset, 7 + g)
                dstm = Am if g < 4 else Bm
                par = g // 2 % 2
                act.activation(dstm[:, par:8:2, :], bank[g][:, :], ACT.Copy).then_inc(s_aset, 1)

            def keysT_out(t, par):
                act.wait_ge(s_KT, t + 1)
                wait(act, s_S, 4 * (t - 1))
                wait(act, s_Q, 4 * (t - 1))
                act.activation(KT[:, par, :, :], bank[KT_BANK][:, 0:2 * KEYS], ACT.Copy).then_inc(s_KTe, 1)

            def queries_out(t, par, c):
                act.wait_ge(s_Q, 4 * t + c + 1)
                wait(act, s_S, 4 * (t - 1))
                src = bank[Q_BANK[c % 2]][:, :].rearrange("p (h b q) -> p b h q", h=4, b=2)
                act.activation(QP[:, par, :, 4 * c:4 * c + 4, :], src, ACT.Copy).then_inc(s_Qe, 1)

            def probsT_out(n, uu):
                act.wait_ge(s_PT, n + 1)
                wait(act, s_Y, n - 1)
                act.activation(PTs[:, uu % 2, :], bank[PT_BANK][:, :], ACT.Copy).then_inc(s_PTe, 1)

            def exps(n, uu):
                act.wait_ge(s_sub, n + 1)
                act.activation(Pr[:, uu, :, :], Pr[:, uu, :, :], ACT.Exp, scale=X_SCALE).then_inc(s_exp, 1)

            def mixed_out(t, par, uu):
                b, half = uu // 2, uu % 2
                act.wait_ge(s_Y, 4 * t + uu + 1)
                wait(act, s_OUT, t - 1)
                src = bank[Y_BANK][:, :].rearrange("p (h q) -> p h q", q=SEQ)
                act.activation(YT[:, par, 8 * half:8 * half + 8, b, :], src, ACT.Copy).then_inc(s_Ye, 1)

            keysT_out(0, 0)
            for c in range(4):
                queries_out(0, 0, c)
            keysT_out(1, 1)

            def body(t0):
                for dt in range(2):
                    t = t0 + dt
                    par = dt
                    for uu in range(4):
                        tl, ul = (t, uu - 2) if uu >= 2 else (t - 1, uu + 2)
                        lpar = par if uu >= 2 else 1 - par
                        if valid(tl, pairs):
                            probsT_out(4 * tl + ul, ul)
                        if valid(t + 1, pairs):
                            queries_out(t + 1, 1 - par, uu)
                        if valid(t, pairs):
                            exps(4 * t + uu, uu)
                        if valid(tl, pairs):
                            mixed_out(tl, lpar, ul)
                        if uu == 3 and valid(t + 2, pairs):
                            keysT_out(t + 2, par)

            body(0)
            with act.Fori(1, pairs // 2 - 1) as k:
                body(k * 2)
            body(pairs - 2)
            body(pairs)

            def att_tile(need, t, p):
                q = 1 - p
                if valid(t, pairs):
                    need(A["h"], t + 1)
                    need(A["v"], t - 1)
                    act.activation(hT[:, p, :], bank[2][:, 0:P], ACT.Copy).then_inc(A["he"], 1)
                if valid(t - 2, pairs):
                    j = t - 2
                    need(A["f"], j + 1)
                    need(A["s"], j)
                    act.activation(FT[:, 0:4, :], bank[3][:, :], ACT.Copy)
                    act.activation(FT[:, 4:8, :], bank[4][:, :], ACT.Copy).then_inc(A["fe"], 1)
                if valid(t - 3, pairs):
                    j = t - 3
                    need(A["pt"], j + 1)
                    need(A["o"], j)
                    act.activation(PTf[:, :, :], bank[7][:, :], ACT.Copy).then_inc(A["pte"], 1)
                if valid(t, pairs):
                    need(A["qk"], t + 1)
                    need(A["ssd"], t)
                    act.activation(sq[:, 0:8, :], bank[0][:, :], ACT.Square)
                    act.activation(sq[:, 8:16, :], bank[1][:, :], ACT.Square).then_inc(A["sqd"], 1)
                if valid(t - 4, pairs):
                    j = t - 4
                    need(A["ot"], j + 1)
                    need(A["wo"], j)
                    act.activation(OTf[:, :, :], bank[7][:, :], ACT.Copy).then_inc(A["ote"], 1)
                if valid(t - 2, pairs):
                    j = t - 2
                    need(A["sb"], j + 1)
                    act.activation(Pf[:, p, :, :, :], Pf[:, p, :, :, :], ACT.Exp, scale=F_SCALE).then_inc(A["e"], 1)
                if valid(t - 1, pairs):
                    j = t - 1
                    need(A["v"], j + 1)
                    need(A["o"], j - 1)
                    act.activation(V[:, q, :, :, :], bank[2][:, :], ACT.Copy).then_inc(A["ve"], 1)

            def mlp_group(need, g):
                if valid(g - 1, groups):
                    j = g - 1
                    need(M["t"], j + 1)
                    need(M["a"], 3 * j, True)
                    act.activation(nT[:, :], bank[1][:, :], ACT.Identity, bias=lnb[:, 0:1],
                                   scale=lng[:, 0:1]).then_inc(M["te"], 1)
                    for k, (h0, hw) in enumerate(HB):
                        need(M["a"], 3 * j + k + 1, True)
                        need(M["u"], 3 * j + k - 2, True)
                        act.activation(ge[0:hw, k, :], bank[5 + k][0:hw, :], ACT.Gelu,
                                       bias=b1g[0:hw, k:k + 1]).then_inc(M["g"], 1)

            with act.Fori(0, LAYERS) as lay:
                att_loop(act, att_tile, lay * pairs, pairs)
                act.wait_ge(s_mw, lay * (16 * MW) + 16 * MW)
                act.wait_ge(s_rt, lay * 2 + 2)
                mlp_loop(act, mlp_group, lay * groups, lay * (3 * groups), groups)

        @block.vector
        def _(dve):
            dve.memset(ones_row[:, :], 1.0)
            dve.memset(mask_row[:, :, :], 0.0).then_inc(s_bz, 1)
            for g in (1, 3, 5):
                dve.wait_ge(s_tset, g + 1)
                dve.tensor_copy(WT[:, g // 2, 4:8, :], bank[g][:, :]).then_inc(s_set, 1)
            for k, g in enumerate((1, 3, 5, 7)):
                dve.wait_ge(s_tset, 7 + g)
                dstm = Am if g < 4 else Bm
                par = g // 2 % 2
                dve.tensor_copy(dstm[:, 8 + par:16:2, :], bank[g][:, :]).then_inc(s_set, 1)
            dve.wait_ge(s_ctab, 16 * N_CONST)
            dve.wait_ge(s_bz, 1)
            dve.tensor_scalar(mask_row[:, :, 0:SEQ], mask_u8[:, :, :], NEG, None, ALU.mult).then_inc(s_set, 1)
            q = NB // 4
            for c in range(4):
                dve.wait_ge(s_in[c], 32)
                with dve.Fori(c * q, (c + 1) * q) as b:
                    dve.bn_stats(ST[:, bass.ds(b, 1), :], XC[:, bass.ds(b, 1), :]).then_inc(s_bn, 1)
            dve.wait_ge(s_bn, NB)
            moments(dve, ST, mean, rstd, tmpA, NB, s_set, 8)
            dve.wait_ge(s_pset, 1)
            dve.tensor_tensor(tmpB[:, :], rstd[:, :], rstd[:, :], ALU.mult).then_inc(s_set, 1)
            dve.wait_ge(s_set, 14)
            dve.tensor_tensor(tmpB[:, :], tmpA[:, :], tmpB[:, :], ALU.mult).then_inc(s_set, 1)
            dve.wait_ge(s_set, 15)
            dve.tensor_scalar(tmpB[:, :], tmpB[:, :], EPS, None, ALU.add).then_inc(s_set, 1)
            dve.wait_ge(s_pset, 2)
            dve.tensor_tensor(rstd[SEQ:P, :], rstd[SEQ:P, :], tmpB[SEQ:P, :], ALU.mult).then_inc(s_set, 1)
            dve.wait_ge(s_set, 17)

            def normalise(t, par):
                wait(dve, s_KG, t - 1)
                for b in range(2):
                    bb = bass.ds(2 * t + b, 1)
                    last = dve.tensor_scalar(XN[:, par, b, :], XC[:, bb, :].rearrange("p o d -> p (o d)"),
                                             mean[:, bb], rstd[:, bb], ALU.subtract, ALU.mult)
                last.then_inc(s_XN, 1)

            def softmax_first(n, uu):
                dve.wait_ge(s_S, n + 1)
                sv = bank[S_BANK[uu % 2]][:, :].rearrange("p (h k) -> p h k", h=4)
                dve.tensor_reduce(mx[:, uu, :], sv, AX.X, ALU.max).then_inc(s_max, 1)
                dve.wait_ge(s_max, n + 1)
                wait(dve, s_PT, n - 3)
                dve.tensor_tensor(Pr[:, uu, :, :], sv, mx[:, uu, :, None].to_broadcast([P, 4, KEYS]),
                                  ALU.subtract).then_inc(s_sub, 1)

            def softmax_second(n, uu):
                dve.wait_ge(s_exp, n + 1)
                dve.tensor_reduce(sm[:, uu, :], Pr[:, uu, :, :], AX.X, ALU.add).then_inc(s_sum, 1)
                dve.wait_ge(s_sum, n + 1)
                dve.reciprocal(rc[:, uu, :], sm[:, uu, :]).then_inc(s_rec, 1)

            def add_cross(t):
                dve.wait_ge(s_OUT, t + 1)
                x1 = X1[:, bass.ds(t, 1), :].rearrange("p o d -> p (o d)")
                dve.scalar_tensor_tensor(x1, bank[OUT_BANK][:, 0:DIM], tg[:, 0:1], x1,
                                         ALU.mult, ALU.add).then_inc(s_xa, 1)
                dve.wait_ge(s_xa, t + 1)
                dve.tensor_tensor(x1, x1, bout_t[:, :], ALU.add).then_inc(s_x1, 1)
                dve.wait_ge(s_x1, t + 1)
                dve.bn_stats(ST1[:, bass.ds(t, 1), :], X1[:, bass.ds(t, 1), :]).then_inc(s_bn, 1)

            normalise(0, 0)
            normalise(1, 1)
            dve.wait_ge(s_aset, 1)
            dve.tensor_scalar(bout_t[:, :], bout_t[:, :], tg[:, 0:1], None, ALU.mult).then_inc(s_set, 1)
            dve.wait_ge(s_set, 18)
            dve.wait_ge(s_xp, 16)

            def body(t0):
                for dt in range(2):
                    t = t0 + dt
                    par = dt
                    for uu in range(4):
                        if valid(t, pairs):
                            softmax_first(4 * t + uu, uu)
                        if uu == 0 and valid(t - 2, pairs):
                            add_cross(t - 2)
                        if uu == 1 and valid(t + 2, pairs):
                            normalise(t + 2, par)
                        if valid(t, pairs):
                            softmax_second(4 * t + uu, uu)

            body(0)
            with dve.Fori(1, pairs // 2 - 1) as k:
                body(k * 2)
            body(pairs - 2)
            body(pairs)
            dve.memset(scratch[:, 1:2], 0.0).then_inc(s_A, 1)
            dve.wait_ge(s_bn, NB + pairs)
            moments(dve, ST1, mean, rstd, tmpA, pairs, s_set, 18)
            dve.wait_ge(s_pset, 3)
            dve.tensor_tensor(Y[:, :, :], X1[:, :, :], mean[:, 0:pairs, None].to_broadcast([P, pairs, DIM]),
                              ALU.subtract).then_inc(s_set, 1)
            dve.wait_ge(s_set, 24)
            dve.tensor_tensor(Y[:, :, :], Y[:, :, :], rstd[:, 0:pairs, None].to_broadcast([P, pairs, DIM]),
                              ALU.mult).then_inc(s_M, 1)

            def att_tile(need, t, p):
                q = 1 - p
                if valid(t, pairs):
                    need(A["he"], t + 1)
                    need(A["qk"], t - 1)
                    dve.tensor_copy(hTh[:, p, :], hT[:, p, :]).then_inc(A["hh"], 1)
                    need(A["hh"], t + 1)
                    dve.tensor_tensor(hTl[:, p, :], hT[:, p, :], hTh[:, p, :].bitcast(fp32),
                                      ALU.subtract).then_inc(A["hl"], 1)
                if valid(t - 1, pairs):
                    j = t - 1
                    need(A["rnd"], j + 1)
                    need(A["rad"], j)
                    need(A["rbd"], j)
                    for w in range(2):
                        last = dve.tensor_tensor(qn[:, w, :, :], bank[w][:, :].rearrange("p (h d) -> p h d", d=DH),
                                                 rn[:, q, 8 * w:8 * w + 8, None].to_broadcast([P, FH, DH]), ALU.mult)
                    last.then_inc(A["qnd"], 1)
                    need(A["qnd"], j + 1)
                    need(A["f"], j)
                    for o, s_ in ((0, 32), (32, 0)):
                        last = dve.tensor_tensor(rb[:, :, :, o:o + 32], qn[:, :, :, s_:s_ + 32],
                                                 RT2[:, :, None, o:o + 32].to_broadcast([P, 2, FH, 32]), ALU.mult)
                    last.then_inc(A["rbd"], 1)
                if valid(t, pairs):
                    need(A["sqd"], t + 1)
                    dve.tensor_reduce(ss[:, p, :], sq[:, :, :], AX.X, ALU.add).then_inc(A["ssd"], 1)
                    need(A["ssd"], t + 1)
                    dve.tensor_scalar(ss[:, p, :], ss[:, p, :], 1e-24, None, ALU.max).then_inc(A["cl"], 1)
                if valid(t - 2, pairs):
                    j = t - 2
                    need(A["s"], j + 1)
                    need(A["pt"], j - 1)
                    for e in range(2):
                        sv = bank[5 + e][:, 0:256].rearrange("p (c k) -> p c k", c=4)
                        last = dve.tensor_reduce(fm[:, p, :, e], sv, AX.X, ALU.max)
                    last.then_inc(A["m"], 1)
                    need(A["m"], j + 1)
                    for e in range(2):
                        sv = bank[5 + e][:, 0:256].rearrange("p (c k) -> p c k", c=4)
                        last = dve.tensor_tensor(Pf[:, p, :, e, :], sv,
                                                 fm[:, p, :, e:e + 1].to_broadcast([P, 4, SEQ]), ALU.subtract)
                    last.then_inc(A["sb"], 1)
                if valid(t - 3, pairs):
                    j = t - 3
                    need(A["o"], j + 1)
                    need(A["ot"], j)
                    for e in range(2):
                        last = dve.tensor_tensor(Of[:, :, e, :], bank[3 + e][:, 0:256].rearrange("p (c d) -> p c d", d=DH),
                                                 fr[:, q, :, e:e + 1].to_broadcast([P, 4, DH]), ALU.mult)
                    last.then_inc(A["oe"], 1)
                if valid(t - 2, pairs):
                    j = t - 2
                    need(A["e"], j + 1)
                    dve.tensor_reduce(fs[:, p, :, :], Pf[:, p, :, :, :], AX.X, ALU.add).then_inc(A["su"], 1)
                    need(A["su"], j + 1)
                    dve.reciprocal(fr[:, p, :, :], fs[:, p, :, :]).then_inc(A["r"], 1)
                if valid(t - 4, pairs):
                    j = t - 4
                    need(A["wo"], j + 1)
                    y = Y[:, bass.ds(t - 4, 1), :].rearrange("p o d -> p (o d)")
                    dve.tensor_tensor(y, bank[7][:, 0:DIM], y, ALU.add).then_inc(A["res"], 1)

            def mlp_group(need, g):
                if valid(g, groups):
                    need(M["h"], g + 1)
                    hb = bank[0][:, :].rearrange("p (t d) -> p t d", t=GROUP)
                    for k in range(GROUP):
                        last = dve.bn_stats(ST2[:, k, :], hb[:, k, :])
                    last.then_inc(M["bs"], 1)
                    need(M["bs"], g + 1)
                    dve.memset(scratch[:, 0:1], 0.0)
                    for k in range(GROUP):
                        last = dve.bn_aggr(MV[:, k, :], ST2[:, k, :])
                    last.then_inc(M["ba"], 1)
                    need(M["ba"], g + 1)
                    dve.tensor_scalar(ve[:, :], MV[:, :, 1], EPS, None, ALU.add).then_inc(M["ve"], 1)
                if valid(g - 1, groups):
                    j = g - 1
                    for k, (h0, hw) in enumerate(HB):
                        need(M["g"], 3 * j + k + 1, True)
                        need(M["d"], j)
                        dve.scalar_tensor_tensor(u[0:hw, k, :], bank[2 + k][0:hw, :], b1a[0:hw, k:k + 1],
                                                 ge[0:hw, k, :], ALU.add, ALU.mult).then_inc(M["u"], 1)
                if valid(g, groups):
                    need(M["rs"], g + 1)
                    need(M["t"], g)
                    hb = bank[0][:, :].rearrange("p (t d) -> p t d", t=GROUP)
                    for k in range(GROUP):
                        last = dve.tensor_scalar(hn[:, k, :], hb[:, k, :], MV[:, k, 0:1], rs[:, k:k + 1],
                                                 ALU.subtract, ALU.mult)
                    last.then_inc(M["hn"], 1)
                if valid(g - 1, groups):
                    j = g - 1
                    need(M["d"], j + 1)
                    y = Y[:, bass.ds((g - 1) * GROUP, GROUP), :]
                    dve.tensor_tensor(y, bank[2][:, :].rearrange("p (t d) -> p t d", t=GROUP), y,
                                      ALU.add).then_inc(M["res"], 1)
                    need(M["res"], j + 1)
                    dve.tensor_tensor(y, y, b2t[:, None, :].to_broadcast([P, GROUP, DIM]), ALU.add).then_inc(M["r2"], 1)

            with dve.Fori(0, LAYERS) as lay:
                li = lay * pairs
                gi = lay * groups
                gi3 = lay * (3 * groups)
                dve.wait_ge(s_lw, lay * (16 * LW) + 16 * LW)
                dve.wait_ge(s_M, lay * 1 + 1)
                dve.tensor_tensor(RT1[:, :, :], rot[:, 0:2, :], qks[:, :, :], ALU.mult)
                for o, s_ in ((0, 32), (32, 0)):
                    last = dve.tensor_tensor(RT2[:, :, o:o + 32], rot[:, 2:4, o:o + 32], qks[:, :, s_:s_ + 32], ALU.mult)
                last.then_inc(s_rt, 1)
                dve.tensor_copy(Wh[:, :], Wraw).then_inc(s_ws, 1)
                dve.wait_ge(s_rt, lay * 2 + 1)
                dve.wait_ge(s_pm, 2)
                dve.wait_ge(s_ws, lay * 2 + 1)
                dve.tensor_tensor(Wl[:, :], Wraw, Wh[:, :].bitcast(fp32), ALU.subtract).then_inc(s_ws, 1)
                dve.tensor_copy(lng[:, :], lnp[:, bass.ds(lay, 1)])
                dve.tensor_copy(lnb[:, :], lnp[:, bass.ds(lay + LAYERS, 1)]).then_inc(s_rt, 1)
                att_loop(dve, att_tile, li, pairs)
                dve.wait_ge(A["res"], li + pairs)
                dve.memset(scratch[:, 1:2], 0.0).then_inc(s_A, 1)
                dve.wait_ge(s_mw, lay * (16 * MW) + 16 * MW)
                mlp_loop(dve, mlp_group, gi, gi3, groups)
                dve.wait_ge(M["r2"], gi + groups)
                dve.memset(scratch[:, 2:3], 0.0).then_inc(s_M, 1)
            dve.wait_ge(s_M, LAYERS + 1)
            q = pairs // 4
            for c in range(4):
                r = slice(c * q, (c + 1) * q)
                dve.scalar_tensor_tensor(Y[:, r, :], Y[:, r, :], tg[:, 1:2], X1[:, r, :],
                                         ALU.mult, ALU.add).then_inc(s_fin, 1)

        @block.gpsimd
        def _(pool):
            pool.memset(mhb[:, :], -0.5).then_inc(s_pm, 1)
            pool.wait_ge(s_ctab, 16 * N_CONST)
            pool.tensor_copy(lnp[:, :], yc[:, 0, 0:2 * LAYERS]).then_inc(s_pm, 1)
            pool.wait_ge(s_pm, 2)
            pool.wait_ge(s_set, 13)
            pool.tensor_tensor(rstd[:, :], rstd[:, :], mhb[:, :], ALU.pow).then_inc(s_pset, 1)
            pool.wait_ge(s_set, 16)
            pool.tensor_tensor(tmpB[:, :], tmpB[:, :], mhb[:, :], ALU.pow).then_inc(s_pset, 1)

            def scale_keys(t, par):
                pool.wait_ge(s_XN, t + 1)
                wait(pool, s_KT, t - 1)
                wait(pool, s_KX, t - 1)
                pool.tensor_tensor(KN[:, par, :, :], XN[:, par, :, :], G[:, None, :].to_broadcast([P, 2, DIM]),
                                   ALU.mult).then_inc(s_KG, 1)
                pool.wait_ge(s_KG, t + 1)
                pool.tensor_tensor(KN[:, par, :, :], KN[:, par, :, :], Bt[:, None, :].to_broadcast([P, 2, DIM]),
                                   ALU.add).then_inc(s_KN, 1)

            def copy_keys(t, par):
                pool.tensor_copy(KX[:, par, :, :], KN[:, par, :, :]).then_inc(s_KX, 1)

            scale_keys(0, 0)
            scale_keys(1, 1)
            pool.wait_ge(s_KN, 1)
            copy_keys(0, 0)

            def body(t0):
                for dt in range(2):
                    t = t0 + dt
                    par = dt
                    for uu in range(4):
                        n = 4 * t + uu
                        if valid(t, pairs):
                            if uu == 2 and valid(t + 1, pairs):
                                pool.wait_ge(s_KN, t + 2)
                            pool.wait_ge(s_rec, n + 1)
                            pool.tensor_tensor(Pr[:, uu, :, :], Pr[:, uu, :, :],
                                               rc[:, uu, :, None].to_broadcast([P, 4, KEYS]), ALU.mult).then_inc(s_pn, 1)
                        if uu == 1 and valid(t + 2, pairs):
                            scale_keys(t + 2, par)
                        if uu == 2 and valid(t + 1, pairs):
                            copy_keys(t + 1, 1 - par)

            body(0)
            with pool.Fori(1, pairs // 2 - 1) as k:
                body(k * 2)
            body(pairs - 2)
            pool.wait_ge(s_set, 23)
            pool.tensor_tensor(rstd[:, 0:pairs], rstd[:, 0:pairs], mhb[:, 0:pairs], ALU.pow).then_inc(s_pset, 1)

            def att_tile(need, t, p):
                if valid(t - 1, pairs):
                    j = t - 1
                    need(A["qnd"], j + 1)
                    need(A["f"], j)
                    pool.tensor_tensor(ra[:, :, :, :], qn[:, :, :, :],
                                       RT1[:, :, None, :].to_broadcast([P, 2, FH, DH]), ALU.mult).then_inc(A["rad"], 1)
                if valid(t, pairs):
                    need(A["cl"], t + 1)
                    pool.tensor_tensor(rn[:, p, :], ss[:, p, :], mhb[:, 0:16], ALU.pow).then_inc(A["rnd"], 1)
                    if valid(t + 1, pairs):
                        copy_tile(t + 1, 1 - p)

            def copy_tile(t, p):
                pool.tensor_copy(yc[:, p, :], Y[:, bass.ds(t, 1), :].rearrange("p o d -> p (o d)")).then_inc(A["yc"], 1)

            def mlp_group(need, g):
                if valid(g, groups):
                    need(M["ve"], g + 1)
                    pool.tensor_tensor(rs[:, :], ve[:, :], mhb[:, 0:GROUP], ALU.pow).then_inc(M["rs"], 1)

            with pool.Fori(0, LAYERS) as lay:
                pool.wait_ge(s_rt, lay * 2 + 2)
                pool.wait_ge(s_ws, lay * 2 + 2)
                pool.tensor_tensor(scratch[:, 4:5], mhb[:, 0:1], mhb[:, 0:1], ALU.add)
                copy_tile(0, 0)
                att_loop(pool, att_tile, lay * pairs, pairs)
                mlp_loop(pool, mlp_group, lay * groups, lay * (3 * groups), groups)


def tables():
    import numpy as np
    ident = np.eye(P, dtype=np.float32)
    shift = np.zeros((P, P), np.float32)
    for o in range(P):
        if o % SEQ:
            shift[o - 1, o] = 1.0
    q = np.arange(P)[:, None] % SEQ
    causal = np.where(q < np.arange(SEQ)[None, :], np.float32(NEG), np.float32(0.0)).astype(np.float32)
    half = np.arange(0, DH, 2, dtype=np.float32)
    freqs = np.arange(SEQ, dtype=np.float32)[:, None] * (1.0 / 10000.0 ** (half / DH)).astype(np.float32)[None, :]
    freqs = np.concatenate([freqs, freqs], -1)
    base = (half + 0.4 * DH) / (1.4 * DH)
    power = (np.arange(SEQ, dtype=np.float32) - SEQ // 2) / 32.0
    scale = base[None, :] ** power[:, None]
    scale = np.concatenate([scale, scale], -1)
    cos, sin = np.cos(freqs), np.sin(freqs)
    sign = np.where(np.arange(DH) < DH // 2, -1.0, 1.0)[None, :]
    rot = np.stack([cos * scale, cos / scale, sign * sin * scale, sign * sin / scale], 1).astype(np.float32)
    return ident, shift, causal, np.ascontiguousarray(np.concatenate([rot, rot], 0))


_INS = ["x", "ctx_1024", "mask_BxS2_bk0", "g_xattn", "g_ffn", "L0_xattn_Wq", "L0_xattn_Wkv",
        "L0_xattn_Wout", "L0_xattn_bout", "L0_xattn_g_media", "L0_xattn_b_media",
        "L0_xattn_g_latent", "L0_xattn_b_latent", "L0_ffn_wqkv", "L0_ffn_q_scale",
        "L0_ffn_k_scale", "L0_ffn_wo", "L0_ffn_ln_g", "L0_ffn_ln_b", "L0_ffn_w1", "L0_ffn_b1",
        "L0_ffn_w2", "L0_ffn_b2"]


def kernel(**inputs):
    import numpy as np
    import concourse.bacc as bacc
    from concourse.bass_utils import run_bass_kernel_spmd

    nc = bacc.Bacc("TRN2", target_bir_lowering=False, num_devices=1)
    arrays, args = {}, []
    for name, a in [(n, inputs[n]) for n in _INS] + list(zip(("ident", "shift", "causal", "rot"), tables())):
        a = np.ascontiguousarray(a)
        arrays[f"in_{name}"] = a
        args.append(nc.dram_tensor(f"in_{name}", a.shape, mybir.dt.from_np(a.dtype), kind="ExternalInput").ap())
    shape = (BATCH, SEQ, DIM)
    args.append(nc.dram_tensor("out", shape, fp32, kind="ExternalOutput").ap())
    build(nc, *args)
    r = run_bass_kernel_spmd(nc, [arrays], core_ids=[0])
    return r.results[0]["out"]
```

```python
import concourse.bass as bass
from concourse import mybir
from contextlib import ExitStack

fp32 = mybir.dt.float32
bf16 = mybir.dt.bfloat16
fp32r = mybir.dt.float32r
u8 = mybir.dt.uint8
ALU = mybir.AluOpType
ACT = mybir.ActivationFunctionType
AX = mybir.AxisListType

BATCH, SEQ, DIM = 64, 64, 128
P = 128
PAIRS = BATCH // 2
XH, DH = 16, 64
HPB = XH // 2
KEYS = 2 * SEQ
FH = 8
INNER = FH * DH
LAYERS = 2
HID = DIM * 4 * 2 // 3
HB = [(0, 128), (128, 128), (256, HID - 256)]
GROUP = 4
GROUPS = PAIRS // GROUP
EPS = 1e-5
NEG = -1e30
X_SCALE = DH ** -0.5
F_SCALE = 8.0


def valid(i, n):
    return not isinstance(i, int) or 0 <= i < n


def wait(eng, sem, value):
    if not isinstance(value, int) or value > 0:
        eng.wait_ge(sem, value)


def att_loop(eng, tile, base, n):
    def need(sem, value):
        if not isinstance(value, int) or value > 0:
            eng.wait_ge(sem, base + value)
    for t in range(6):
        tile(need, t, t % 2)
    with eng.Fori(3, n // 2 - 1) as k:
        tile(need, k * 2, 0)
        tile(need, k * 2 + 1, 1)
    for t in range(n - 2, n + 4):
        tile(need, t, t % 2)


def mlp_loop(eng, prologue, group, base, base3, n):
    def need(sem, value, triple=False):
        if not isinstance(value, int) or value > 0:
            eng.wait_ge(sem, (base3 if triple else base) + value)
    prologue(need)
    group(need, 0, 0)
    group(need, 1, 1)
    with eng.Fori(1, n // 2 - 1) as k:
        group(need, k * 2, 0)
        group(need, k * 2 + 1, 1)
    for g in range(n - 2, n + 1):
        group(need, g, g % 2)


def moments(dve, stats, mean, var, tmp, n, sem, base):
    half = DIM // 2
    me, mo, ve_, vo = stats[:, 0:n, 1], stats[:, 0:n, 4], stats[:, 0:n, 2], stats[:, 0:n, 5]
    dve.tensor_tensor(tmp[:, 0:n], me, mo, ALU.subtract).then_inc(sem, 1)
    dve.wait_ge(sem, base + 1)
    dve.tensor_tensor(mean[:, 0:n], me, mo, ALU.add)
    dve.tensor_tensor(tmp[:, 0:n], tmp[:, 0:n], tmp[:, 0:n], ALU.mult)
    dve.tensor_tensor(var[:, 0:n], ve_, vo, ALU.add).then_inc(sem, 1)
    dve.wait_ge(sem, base + 2)
    dve.tensor_scalar(mean[:, 0:n], mean[:, 0:n], 0.5, None, ALU.mult)
    dve.tensor_scalar(tmp[:, 0:n], tmp[:, 0:n], 0.25, None, ALU.mult).then_inc(sem, 1)
    dve.wait_ge(sem, base + 3)
    dve.scalar_tensor_tensor(tmp[:, 0:n], var[:, 0:n], 1.0 / (2 * half), tmp[:, 0:n],
                             ALU.mult, ALU.add).then_inc(sem, 1)
    dve.wait_ge(sem, base + 4)
    dve.tensor_scalar(var[:, 0:n], tmp[:, 0:n], EPS, None, ALU.add).then_inc(sem, 1)
    dve.wait_ge(sem, base + 5)


def build(nc, x, ctx_t, mask, g_x, g_f, wq, wkv, wout, bout, g_media, b_media, g_latent, b_latent,
          wqkv, q_scale, k_scale, wo, ln_g, ln_b, w1, b1, w2, b2, ident_d, shift_d, causal_d,
          rot_d, out, pairs=PAIRS):
    groups = pairs // GROUP
    stack = ExitStack()
    with stack:
        stack.enter_context(nc.allow_non_contiguous_dma(reason="parameters that lie one to a partition"))

        def sb(name, shape, dt=fp32):
            return stack.enter_context(nc.sbuf_tensor(name, shape, dt))

        def sem(name):
            return stack.enter_context(nc.semaphore(name))

        NB = 2 * pairs
        XC = sb("XC", [P, BATCH, DIM])
        X1 = sb("X1", [P, pairs, DIM])
        Y = XC[:, 0:pairs, :]
        XS = XC[:, PAIRS:BATCH, :].rearrange("p (k a) d -> p k (a d)", k=4)
        ident = sb("ident", [P, P])
        identb = sb("identb", [P, P], bf16)
        shift = sb("shift", [P, P])
        causal = sb("causal", [P, SEQ], bf16)
        ones_row = sb("ones_row", [1, P], bf16)
        mask_row = sb("mask_row", [1, NB, SEQ], bf16)
        G = sb("G", [P, DIM])
        Bt = sb("Bt", [P, DIM])
        bout_t = sb("bout_t", [P, DIM])
        gates = sb("gates", [P, 2])
        tg = sb("tg", [P, 2])
        mhb = sb("mhb", [P, NB])
        scratch = sb("scratch", [P, 8])
        lnp = sb("lnp", [P, 2 * LAYERS])
        ST = sb("ST", [P, 2, 2, 6])
        MX = sb("MX", [P, 2, 2, 2])
        V1 = sb("V1", [P, 2, 2])
        R1 = sb("R1", [P, 2, 2])
        V2 = sb("V2", [P, 2, 2])
        R2 = sb("R2", [P, 2, 2])
        ST1 = sb("ST1", [P, 6])
        MX1 = sb("MX1", [P, 2])
        VX1 = sb("VX1", [P, 1])
        RX1 = sb("RX1", [P, 1])
        Am = sb("Am", [P, XH, DIM])
        Bm = sb("Bm", [P, XH, DIM])
        XN = sb("XN", [P, 2, 2, DIM])
        KN = sb("KN", [P, 2, 2, DIM])
        KXh = sb("KXh", [P, 2, 2, DIM], fp32r)
        KXl = sb("KXl", [P, 2, 2, DIM], fp32r)
        KT = sb("KT", [P, 2, 2, KEYS])
        QP = sb("QP", [P, 2, 2, XH, SEQ])
        YT = sb("YT", [P, 2, XH, 2, SEQ])
        QPf = QP[:, :, :, :, :].rearrange("p a b h q -> p (a b h q)")
        YTf = YT[:, :, :, :, :].rearrange("p a h b q -> p (a h b q)")
        Wq = QPf[:, 0:XH * DH]
        Wkv = QPf[:, XH * DH:3 * XH * DH]
        Wout = QPf[:, 3 * XH * DH:4 * XH * DH].rearrange("p (c o) -> p c o", o=DIM)
        WT = YTf[:, 0:3 * XH * DH].rearrange("p (w c o) -> p w c o", w=3, o=DIM)
        mask_u8 = YTf[0:1, 3 * XH * DH:3 * XH * DH + NB * SEQ // 4].bitcast(u8).rearrange("p (b s) -> p b s", s=SEQ)
        Pr = sb("Pr", [P, 4, 4, KEYS])
        PTh = sb("PTh", [P, 2, 512], fp32r)
        PTl = sb("PTl", [P, 2, 512], fp32r)
        mx = sb("mx", [P, 4, 4])
        sm = sb("sm", [P, 4, 4])
        rc = sb("rc", [P, 4, 4])
        Wqkv = sb("Wv", [P, INNER])
        Wh = sb("Wh", [P, 2 * INNER], fp32r)
        Wl = sb("Wl", [P, 2 * INNER], fp32r)
        Wo = sb("Wo", [P, FH // 2, DIM])
        W1h = sb("W1h", [P, 2 * HID], fp32r)
        W1l = sb("W1l", [P, 2 * HID], fp32r)
        W2 = sb("W2", [P, 3, DIM])
        b1a = sb("b1a", [P, 3])
        b1g = sb("b1g", [P, 3])
        b2t = sb("b2t", [P, DIM])
        lng = sb("lng", [P, 1])
        lnb = sb("lnb", [P, 1])
        rot = sb("rot", [P, 4, DH])
        qks = sb("qks", [P, 2, DH])
        RT1 = sb("RT1", [P, 2, DH])
        RT2 = sb("RT2", [P, 2, DH])
        yc = sb("yc", [P, 2, DIM])
        hT = sb("hT", [P, 2, P])
        hTh = sb("hTh", [P, 2, P], fp32r)
        hTl = sb("hTl", [P, 2, P], fp32r)
        sq = XS[:, 0, :].rearrange("p (h d) -> p h d", d=DH)
        ss = sb("ss", [P, 2, 16])
        rn = sb("rn", [P, 2, 16])
        qn = XS[:, 1, :].rearrange("p (w h d) -> p w h d", w=2, d=DH)
        qs = QPf[:, 2048:4096].rearrange("p (a w h d) -> p a w h d", a=2, w=2, d=DH)
        ra = XS[:, 2, :].rearrange("p (w h d) -> p w h d", w=2, d=DH)
        rb = XS[:, 3, :].rearrange("p (w h d) -> p w h d", w=2, d=DH)
        Wraw = XS[:, 1, :]
        FT = YTf[:, 0:1024].rearrange("p (c n) -> p c n", n=P)
        V = sb("V", [P, 2, 2, 4, DH])
        Pf = sb("Pf", [P, 2, 4, 2, SEQ])
        fm = sb("fm", [P, 2, 4, 2])
        fs = sb("fs", [P, 2, 4, 2])
        fr = sb("fr", [P, 2, 4, 2])
        PTf = YTf[:, 1024:1536].rearrange("p (c n) -> p c n", n=P)
        OTf = YTf[:, 2048:2560].rearrange("p (c n) -> p c n", n=P)
        ST2 = sb("ST2", [P, GROUP, 6])
        MV = sb("MV", [P, GROUP, 2])
        ve = sb("ve", [P, GROUP])
        rs = sb("rs", [P, GROUP])
        hn = YTf[:, 2560:3072].rearrange("p (t d) -> p t d", d=DIM)
        nT = YTf[:, 3072:3584]
        nTh = sb("nTh", [P, 512], fp32r)
        nTl = sb("nTl", [P, 512], fp32r)
        W1raw = Pr[:, :, :, :].rearrange("p a h k -> p (a h k)")[:, 0:2 * HID]
        ge = QPf[:, 0:3 * 512].rearrange("p (k n) -> p k n", k=3)
        u = sb("u", [P, 2, 3, 512])

        bank = [stack.enter_context(nc.psum_tensor(f"bank{i}", [P, 512], fp32)) for i in range(8)]

        s_wq, s_wk, s_wo_ = sem("wq_loaded"), sem("wkv_loaded"), sem("wout_loaded")
        s_id = sem("identity_loaded")
        s_ctab = sem("constants_loaded")
        s_msk = sem("mask_loaded")
        s_in = [sem(f"tokens_loaded{i}") for i in range(2)]
        s_xp = sem("pair_tiles_loaded")
        s_tr, s_pa, s_pb = sem("weights_transposed"), sem("qk_products"), sem("vo_products")
        s_wta, s_wtv = sem("weightsT_by_scalar"), sem("weightsT_by_vector")
        s_aa, s_av = sem("qk_products_by_scalar"), sem("qk_products_by_vector")
        s_ba, s_bv = sem("vo_products_by_scalar"), sem("vo_products_by_vector")
        s_tanh, s_cb = sem("gates_ready"), sem("bf16_constants")
        s_mr = sem("mask_row_ready")
        s_set = sem("vector_chain")
        s_pset = sem("rstd_ready")

        block = stack.enter_context(nc.Block())
        N_CONST = 12
        FIRST = min(12, NB)

        s_out = sem("output_stored")
        s_fin = sem("final_tile_ready")
        s_lw = sem("attention_weights_loaded")
        s_mw = sem("mlp_weights_loaded")
        s_A = sem("attention_phase_done")
        s_M = sem("mlp_phase_done")
        s_rt = sem("rotary_tables_built")
        s_bn = sem("row_statistics")
        s_ws = sem("attention_weights_split")
        s_w1 = sem("mlp_weights_split")
        s_pm = sem("pool_constants")
        s_XN = sem("tokens_normalised")
        LW, MW = 5, 11
        RAW_FREE = 3 * PAIRS // 4

        @block.sync
        def _(sp):
            sp.dma_start(ident[:, :], ident_d).then_inc(s_id, 16)
            sp.dma_start(Wq[:, :], wq).then_inc(s_wq, 16)
            for i, r in enumerate((slice(0, FIRST), slice(FIRST, NB))):
                sp.dma_start(XC[0:SEQ, r, :], ctx_t[r].rearrange("b s d -> s b d")).then_inc(s_in[i], 16)
                sp.dma_start(XC[SEQ:P, r, :], x[r].rearrange("b s d -> s b d")).then_inc(s_in[i], 16)
                if i == 0:
                    sp.dma_start(Wkv[:, :], wkv).then_inc(s_wk, 16)
                    sp.dma_start(Wout[:, :, :], wout.rearrange("(c p) o -> p c o", p=P)).then_inc(s_wo_, 16)
            sp.dma_start(X1[:, :, :], x.rearrange("(t b) s d -> (b s) t d", b=2)).then_inc(s_xp, 16)
            def load_attention(lay):
                wl = wqkv[bass.ds(lay, 1)].rearrange("l p n -> (l p) n")
                sp.dma_start(Wraw, wl[:, 0:2 * INNER]).then_inc(s_lw, 16)
                sp.dma_start(Wqkv[:, :], wl[:, 2 * INNER:]).then_inc(s_lw, 16)
                sp.dma_start(Wo[:, :, :], wo[bass.ds(lay, 1)].rearrange("l (c p) o -> p (l c) o", p=P)).then_inc(s_lw, 16)
                sp.dma_start(qks[:, 0, :], q_scale[bass.ds(lay, 1), :].to_broadcast([P, DH])).then_inc(s_lw, 16)
                sp.dma_start(qks[:, 1, :], k_scale[bass.ds(lay, 1), :].to_broadcast([P, DH])).then_inc(s_lw, 16)

            def load_mlp(lay):
                sp.dma_start(W1raw, w1[bass.ds(lay, 1)].rearrange("l p n -> (l p) n")).then_inc(s_mw, 16)
                w2l = w2[bass.ds(lay, 1)].rearrange("l k o -> (l k) o")
                b1l = b1[bass.ds(lay, 1), :].rearrange("l k -> k l")
                for j, (h0, hn_) in enumerate(HB):
                    sp.dma_start(W2[0:hn_, j, :], w2l[h0:h0 + hn_, :]).then_inc(s_mw, 16)
                    sp.dma_start(b1a[0:hn_, j:j + 1], b1l[h0:h0 + hn_, :]).then_inc(s_mw, 16)
                    sp.dma_start(b1g[0:hn_, j:j + 1], b1l[HID + h0:HID + h0 + hn_, :]).then_inc(s_mw, 16)
                sp.dma_start(b2t[:, :], b2[bass.ds(lay, 1), :].to_broadcast([P, DIM])).then_inc(s_mw, 16)

            sp.wait_ge(s_XN, min(RAW_FREE, pairs))
            load_attention(0)
            sp.wait_ge(s_A, 1)
            load_mlp(0)
            with sp.Fori(1, LAYERS) as lay:
                sp.wait_ge(s_A, lay * 1 + 1)
                load_attention(lay)
                sp.wait_ge(s_M, lay * 1 + 1)
                load_mlp(lay)
            NST = 4
            for i in range(NST):
                q = pairs // NST
                sp.wait_ge(s_fin, i + 1)
                sp.dma_start(out.rearrange("(t b) s d -> (b s) t d", b=2)[:, i * q:(i + 1) * q, :],
                             Y[:, i * q:(i + 1) * q, :]).then_inc(s_out, 16)
            sp.wait_ge(s_out, 16 * NST)

        s_S, s_max, s_sub, s_exp = sem("scores"), sem("maxima"), sem("shifted"), sem("exps")
        s_sum, s_rec, s_pn = sem("sums"), sem("reciprocals"), sem("probs_normalised")
        s_PT, s_PTe = sem("probs_transposed"), sem("probsT_in_sbuf")
        s_Y, s_Ye = sem("mixed_keys"), sem("mixed_keys_in_sbuf")
        s_xb, s_xg, s_xv, s_xr, s_yn = (sem("x_biased"), sem("x1_aggr"), sem("x1_var_eps"),
                                        sem("x1_rstd"), sem("x1_normalised"))
        s_Q, s_Qe = sem("queries"), sem("queries_in_sbuf")
        s_KG, s_KN = sem("keys_scaled"), sem("keys_ready")
        s_PTl = sem("probsT_split")
        s_st, s_ag, s_v1, s_r1 = sem("x_stats"), sem("x_aggr"), sem("x_var_eps"), sem("x_rstd")
        s_v2, s_r2, s_r3 = sem("x_var2"), sem("x_rstd2"), sem("x_rstd_product")
        s_KXh = sem("keys_high")
        s_KT, s_KTe, s_KX = sem("keys_transposed"), sem("keysT_in_sbuf"), sem("keys_copied")
        s_OUT, s_xa, s_x1 = sem("cross_out"), sem("cross_out_added"), sem("x1_ready")
        S_BANK, Q_BANK, PT_BANK, Y_BANK, OUT_BANK, KT_BANK = (0, 1), (2, 3), 4, 5, 6, 7
        STEPS = 4 * pairs

        label = {"yc": "copied", "h": "hT_psum", "he": "hT_sbuf", "hl": "hT_low_part", "qk": "qk_psum",
                 "qs": "qk_sbuf", "sqd": "squares", "ssd": "norms2", "cl": "norms2_clipped",
                 "rnd": "inv_norms", "qnd": "qk_normed", "rad": "cos_part", "rbd": "sin_part",
                 "ad": "qk_rotated", "v": "v_psum", "ve": "v_sbuf", "f": "qkT_psum", "fe": "qkT_sbuf",
                 "s": "f_scores", "m": "f_max", "sb": "f_shifted", "e": "f_exp", "su": "f_sum",
                 "r": "f_rec", "pn": "f_probs", "pt": "f_probsT_psum", "pte": "f_probsT_sbuf",
                 "o": "f_outT_psum", "ote": "f_outT_sbuf", "wo": "f_proj", "res": "f_residual"}
        A = {k: sem(v) for k, v in label.items()}
        mnames = {"h": "m_shifted", "bs": "m_stats", "ba": "m_aggr", "ve": "m_var_eps", "rs": "m_rstd",
                  "hn": "m_normed", "t": "m_normedT", "te": "m_normedT_sbuf", "a": "m_up", "g": "m_gelu",
                  "u": "m_gated", "d": "m_down", "res": "m_residual", "r2": "m_biased",
                  "nh": "m_high_part", "nl": "m_low_part"}
        M = {k: sem(v) for k, v in mnames.items()}

        @block.tensor
        def _(pe):
            pe.wait_ge(s_id, 16)
            pe.wait_ge(s_wq, 16)
            for g in range(6):
                if g == 2:
                    pe.wait_ge(s_wk, 16)
                for i in range(4):
                    blk = 4 * (g % 2) + i
                    src = Wq if g < 2 else Wkv
                    c = (blk + (HPB if g >= 4 else 0)) * P
                    last = nc.tensor.transpose(bank[g][:, i * P:(i + 1) * P], src[:, c:c + P], ident[:, :])
                last.then_inc(s_tr, 1)
            for g in range(8):
                par, quad, isb = g // 2 % 2, g % 2, g // 4
                if g == 0:
                    pe.wait_ge(s_wta, 2)
                    pe.wait_ge(s_wtv, 2)
                if g == 4:
                    pe.wait_ge(s_wta, 3)
                    pe.wait_ge(s_wtv, 3)
                    pe.wait_ge(s_wo_, 16)
                r = slice(64 * par, 64 * par + 64)
                for i in range(4):
                    hb = 4 * quad + i
                    if isb:
                        l, rr = WT[r, 2, hb, :], Wout[r, hb, :]
                    else:
                        l, rr = WT[r, 0, hb, :], WT[r, 1, hb, :]
                    last = nc.tensor.matmul(bank[g][:, i * P:(i + 1) * P], l, rr, start=True, stop=True)
                last.then_inc(s_pb if isb else s_pa, 1)

            def keys_transposed(t, par):
                pe.wait_ge(s_KN, t + 1)
                wait(pe, s_KTe, t)
                for b in range(2):
                    last = nc.tensor.transpose(bank[KT_BANK][:, b * KEYS:(b + 1) * KEYS],
                                               KN[:, par, b, :], ident[:, :])
                last.then_inc(s_KT, 1)

            def queries(t, par, c):
                pe.wait_ge(s_KTe, t + 1)
                wait(pe, s_Qe, 4 * t + c - 1)
                for i in range(4):
                    last = nc.tensor.matmul(bank[Q_BANK[c % 2]][:, i * P:(i + 1) * P], Am[:, 4 * c + i, :],
                                            KT[:, par, :, SEQ:KEYS], start=True, stop=True)
                last.then_inc(s_Q, 1)

            def probs_transposed(n, uu):
                pe.wait_ge(s_pn, n + 1)
                wait(pe, s_PTl, n)
                for i in range(4):
                    last = nc.tensor.transpose(bank[PT_BANK][:, i * P:(i + 1) * P], Pr[:, uu, i, :], ident[:, :])
                last.then_inc(s_PT, 1)

            def scores(t, par, uu):
                n, b, half = 4 * t + uu, uu // 2, uu % 2
                pe.wait_ge(s_Qe, 4 * t + 2 * half + 2)
                pe.wait_ge(s_KTe, t + 1)
                wait(pe, s_sub, n - 1)
                for i in range(4):
                    h = 8 * half + 2 * i
                    nc.tensor.matmul(bank[S_BANK[uu % 2]][:, i * P:(i + 1) * P], QP[:, par, b, h:h + 2, :],
                                     KT[:, par, b, :], start=(i == 0), stop=False, skip_group_check=True)
                m = mask_row[0:1, bass.ds(2 * t + b, 1), :].to_broadcast([1, 4, SEQ])
                sv = bank[S_BANK[uu % 2]][:, :].rearrange("p (a k) -> p a k", a=4)[:, :, 0:SEQ]
                nc.tensor.matmul(sv, ones_row[:, :], m,
                                 start=False, stop=True, skip_group_check=True).then_inc(s_S, 1)

            def mixed(t, par, uu):
                n, b = 4 * t + uu, uu // 2
                pe.wait_ge(s_PTl, n + 1)
                pe.wait_ge(s_KX, t + 1)
                wait(pe, s_Ye, n)
                for k, (l, r) in enumerate(((KXh, PTh), (KXh, PTl), (KXl, PTh))):
                    last = nc.tensor.matmul(bank[Y_BANK][:, :], l[:, par, b, :], r[:, uu % 2, :],
                                            start=(k == 0), stop=(k == 2))
                last.then_inc(s_Y, 1)

            def cross_out(t, par, quarter):
                if quarter == 0:
                    pe.wait_ge(s_Ye, 4 * t + 4)
                    wait(pe, s_xa, t)
                for h in range(4 * quarter, 4 * quarter + 4):
                    last = nc.tensor.matmul(bank[OUT_BANK][:, 0:DIM], YT[:, par, h, :, :], Bm[:, h, :],
                                            start=(h == 0), stop=(h == XH - 1))
                if quarter == 3:
                    last.then_inc(s_OUT, 1)

            pe.wait_ge(s_aa, 2)
            pe.wait_ge(s_av, 2)
            pe.wait_ge(s_ba, 2)
            pe.wait_ge(s_bv, 2)
            pe.wait_ge(s_mr, 1)
            pe.wait_ge(s_cb, 2)
            keys_transposed(0, 0)
            for c in range(4):
                queries(0, 0, c)
            keys_transposed(1, 1)

            def body(t0):
                for dt in range(2):
                    t = t0 + dt
                    par = dt
                    for uu in range(4):
                        tl, ul = (t, 0) if uu == 3 else (t - 1, uu + 1)
                        if valid(t, pairs):
                            scores(t, par, uu)
                        if valid(t - 2, pairs):
                            cross_out(t - 2, par, uu)
                        if valid(tl, pairs):
                            probs_transposed(4 * tl + ul, ul)
                        if uu == 3 and valid(t + 2, pairs):
                            keys_transposed(t + 2, par)
                        if valid(t + 1, pairs):
                            queries(t + 1, 1 - par, uu)
                        if valid(t - 1, pairs):
                            mixed(t - 1, 1 - par, uu)

            body(0)
            with pe.Fori(1, pairs // 2 - 2) as k:
                body(k * 2)
            body(pairs - 4)
            body(pairs - 2)
            body(pairs)

            def att_tile(need, t, p):
                q = 1 - p
                if valid(t, pairs):
                    need(A["yc"], t + 1)
                    need(A["ve"], t - 1)
                    nc.tensor.matmul(bank[2][0:64, 0:P], yc[:, p, 0:64], ident[:, :], start=True, stop=True)
                    nc.tensor.matmul(bank[2][64:P, 0:P], yc[:, p, 64:P], shift[:, :],
                                     start=True, stop=True).then_inc(A["h"], 1)
                if valid(t - 2, pairs):
                    j = t - 2
                    need(A["ote"], j - 1)
                    need(A["ad"], j + 1)
                    for c in range(8):
                        last = nc.tensor.transpose(bank[3 + c // 4][:, (c % 4) * P:(c % 4 + 1) * P],
                                                   rb[:, c // 4, 2 * (c % 4):2 * (c % 4) + 2, :], ident[:, :])
                    last.then_inc(A["f"], 1)
                if valid(t, pairs):
                    need(A["hl"], t + 1)
                    need(A["qs"], t)
                    for w in range(2):
                        for k, (l, r) in enumerate(((hTh, Wh), (hTh, Wl), (hTl, Wh))):
                            last = nc.tensor.matmul(bank[w][:, :], l[:, p, :], r[:, w * 512:(w + 1) * 512],
                                                    start=(k == 0), stop=(k == 2))
                    last.then_inc(A["qk"], 1)
                if valid(t - 3, pairs):
                    j = t - 3
                    need(A["pn"], j + 1)
                    need(A["res"], j)
                    for c in range(4):
                        last = nc.tensor.transpose(bank[7][:, c * P:(c + 1) * P], Pf[:, q, c, :, :], ident[:, :])
                    last.then_inc(A["pt"], 1)
                if valid(t - 2, pairs):
                    j = t - 2
                    need(A["fe"], j + 1)
                    need(A["sb"], j)
                    for e in range(2):
                        nc.tensor.matmul(bank[5 + e][:, 0:256].rearrange("p (c k) -> p c k", c=4), identb[:, :],
                                         causal[:, None, :].to_broadcast([P, 4, SEQ]),
                                         start=True, stop=False, skip_group_check=True)
                    for c in range(4):
                        for e in range(2):
                            for b in range(2):
                                r = slice(64 * e, 64 * e + 64)
                                last = nc.tensor.matmul(
                                    bank[5 + e][64 * b:64 * b + 64, c * SEQ:(c + 1) * SEQ],
                                    FT[r, c, 64 * b:64 * b + 64], FT[r, 4 + c, 64 * b:64 * b + 64],
                                    start=False, stop=(c == 3), skip_group_check=True)
                    last.then_inc(A["s"], 1)
                if valid(t - 3, pairs):
                    j = t - 3
                    need(A["pte"], j + 1)
                    need(A["fe"], min(j + 2, pairs) if isinstance(j, int) else j + 2)
                    need(A["ve"], j + 1)
                    nc.tensor.matmul(bank[3][:, 0:8], identb[:, :], identb[:, 0:8], start=True, stop=True)
                    for c in range(4):
                        for b in range(2):
                            for e in range(2):
                                r = slice(64 * e, 64 * e + 64)
                                last = nc.tensor.matmul(
                                    bank[3 + e][r, c * P + 64 * b:c * P + 64 * b + 64],
                                    V[r, q, b, c, :], PTf[r, c, 64 * b:64 * b + 64], start=True, stop=True)
                    last.then_inc(A["o"], 1)
                if valid(t - 1, pairs):
                    j = t - 1
                    need(A["he"], min(j + 2, pairs) if isinstance(j, int) else j + 2)
                    wv = Wqkv[:, :].rearrange("p (c e d) -> p c e d", e=2, d=DH)
                    nc.tensor.matmul(bank[2][:, 0:8], identb[:, :], identb[:, 0:8], start=True, stop=True)
                    for b in range(2):
                        for e in range(2):
                            last = nc.tensor.matmul(
                                bank[2][64 * e:64 * e + 64, b * 256:(b + 1) * 256].rearrange("p (c d) -> p c d", d=DH),
                                hT[:, q, 64 * b:64 * b + 64], wv[:, :, e, :], start=True, stop=True)
                    last.then_inc(A["v"], 1)
                if valid(t - 3, pairs):
                    j = t - 3
                    need(A["ote"], j + 1)
                    for c in range(4):
                        last = nc.tensor.matmul(bank[7][:, 0:DIM], OTf[:, c, :], Wo[:, c, :],
                                                start=(c == 0), stop=(c == 3))
                    last.then_inc(A["wo"], 1)

            def mlp_shifted(need, g):
                if valid(g, groups):
                    need(M["hn"], g)
                    ytile = Y[:, bass.ds(g * GROUP, GROUP), :]
                    hb = bank[0][:, :].rearrange("p (t d) -> p t d", t=GROUP)
                    nc.tensor.matmul(hb[:, :, 0:64], ident[:, :], ytile[:, :, 0:64], start=True, stop=False,
                                     skip_group_check=True)
                    nc.tensor.matmul(hb[:, :, 64:P], shift[:, :], ytile[:, :, 64:P],
                                     start=False, stop=True, skip_group_check=True).then_inc(M["h"], 1)

            def mlp_transposed(need, g):
                if valid(g, groups):
                    need(M["hn"], g + 1)
                    need(M["te"], g)
                    for k in range(GROUP):
                        last = nc.tensor.transpose(bank[1][:, k * P:(k + 1) * P], hn[:, k, :], ident[:, :])
                    last.then_inc(M["t"], 1)

            def mlp_group(need, g, p):
                if valid(g, groups):
                    need(M["nl"], g + 1)
                    for k, (h0, hw) in enumerate(HB):
                        need(M["u"], 3 * g + k - 2, True)
                        if k == 0:
                            need(M["res"], g - 1)
                        for o, bk in ((0, 2 + k), (HID, 5 + k)):
                            for m, (l, r) in enumerate(((W1h, nTh), (W1h, nTl), (W1l, nTh))):
                                last = nc.tensor.matmul(bank[bk][0:hw, :], l[:, o + h0:o + h0 + hw], r[:, :],
                                                        start=(m == 0), stop=(m == 2))
                        last.then_inc(M["a"], 1)
                if valid(g - 1, groups):
                    j = g - 1
                    need(M["res"], j)
                    need(M["u"], 3 * min(g, groups - 1) + 1 if isinstance(g, int) else 3 * g + 1, True)
                    if isinstance(g, int) and g == groups:
                        need(M["u"], 3 * groups, True)
                    for k in range(GROUP):
                        for c, (h0, hw) in enumerate(HB):
                            last = nc.tensor.matmul(bank[2][:, k * DIM:(k + 1) * DIM],
                                                    u[0:hw, 1 - p, c, k * P:(k + 1) * P],
                                                    W2[0:hw, c, :], start=(c == 0), stop=(c == 2))
                    last.then_inc(M["d"], 1)
                mlp_transposed(need, g + 1)
                mlp_shifted(need, g + 2)

            with pe.Fori(0, LAYERS) as lay:
                li = lay * pairs
                gi = lay * groups
                gi3 = lay * (3 * groups)
                pe.wait_ge(s_lw, lay * (16 * LW) + 16 * LW)
                pe.wait_ge(s_ws, lay * 2 + 2)
                pe.wait_ge(s_M, lay * 1 + 1)
                att_loop(pe, att_tile, li, pairs)
                pe.wait_ge(s_mw, lay * (16 * MW) + 16 * MW)
                pe.wait_ge(s_w1, lay * 2 + 2)
                pe.wait_ge(s_A, lay * 1 + 2)
                mlp_loop(pe, lambda need: (mlp_shifted(need, 0), mlp_transposed(need, 0), mlp_shifted(need, 1)),
                         mlp_group, gi, gi3, groups)

        @block.scalar
        def _(act):
            act.dma_start(mask_u8[:, :, :], mask[None, :, :]).then_inc(s_msk, 16)
            for dst, src in ((shift[:, :], shift_d),
                             (rot[:, :, :], rot_d),
                             (G[0:SEQ, :], g_media[None, :].to_broadcast([SEQ, DIM])),
                             (G[SEQ:P, :], g_latent[None, :].to_broadcast([SEQ, DIM])),
                             (Bt[0:SEQ, :], b_media[None, :].to_broadcast([SEQ, DIM])),
                             (Bt[SEQ:P, :], b_latent[None, :].to_broadcast([SEQ, DIM])),
                             (bout_t[:, :], bout[None, :].to_broadcast([P, DIM])),
                             (gates[:, 0:1], g_x[None, :].to_broadcast([P, 1])),
                             (gates[:, 1:2], g_f[None, :].to_broadcast([P, 1])),
                             (hT[:, 0, 0:SEQ], causal_d),
                             (yc[:, 0, 0:LAYERS], ln_g.rearrange("l p -> p l")),
                             (yc[:, 0, 2:2 + LAYERS], ln_b.rearrange("l p -> p l"))):
                act.dma_start(dst, src).then_inc(s_ctab, 16)
            for g in (0, 2, 4):
                act.wait_ge(s_tr, g + 1)
                act.activation(WT[:, g // 2, 0:4, :], bank[g][:, :], ACT.Copy).then_inc(s_wta, 1)
            for g in (0, 2):
                act.wait_ge(s_pa, g + 1)
                act.activation(Am[:, g // 2:8:2, :], bank[g][:, :], ACT.Copy).then_inc(s_aa, 1)
            for g in (0, 2):
                act.wait_ge(s_pb, g + 1)
                act.activation(Bm[:, g // 2:8:2, :], bank[4 + g][:, :], ACT.Copy).then_inc(s_ba, 1)
            act.wait_ge(s_ctab, 16 * N_CONST)
            act.activation(causal[:, :], hT[:, 0, 0:SEQ], ACT.Copy).then_inc(s_cb, 1)
            act.activation(identb[:, :], ident[:, :], ACT.Copy).then_inc(s_cb, 1)
            act.activation(tg[:, :], gates[:, :], ACT.Tanh).then_inc(s_tanh, 1)

            def keysT_out(t, par):
                act.wait_ge(s_KT, t + 1)
                wait(act, s_S, 4 * (t - 1))
                wait(act, s_Q, 4 * (t - 1))
                kb = bank[KT_BANK][:, 0:2 * KEYS]
                act.activation(KT[:, par, :, :], kb, ACT.Copy).then_inc(s_KTe, 1)

            def queries_out(t, par, c):
                act.wait_ge(s_Q, 4 * t + c + 1)
                wait(act, s_S, 4 * (t - 1))
                src = bank[Q_BANK[c % 2]][:, :].rearrange("p (h b q) -> p b h q", h=4, b=2)
                act.activation(QP[:, par, :, 4 * c:4 * c + 4, :], src, ACT.Copy).then_inc(s_Qe, 1)

            def probsT_out(n, uu):
                act.wait_ge(s_PT, n + 1)
                wait(act, s_Y, n - 1)
                act.activation(PTh[:, uu % 2, :], bank[PT_BANK][:, :], ACT.Copy).then_inc(s_PTe, 1)

            def keys_high(t, par):
                act.wait_ge(s_KN, t + 1)
                wait(act, s_Y, 4 * (t - 1))
                act.activation(KXh[:, par, :, :], KN[:, par, :, :], ACT.Copy).then_inc(s_KXh, 1)

            def exps(n, uu):
                act.wait_ge(s_sub, n + 1)
                act.activation(Pr[:, uu, :, :], Pr[:, uu, :, :], ACT.Exp, scale=X_SCALE).then_inc(s_exp, 1)

            def mixed_out(t, par, uu):
                b, half = uu // 2, uu % 2
                act.wait_ge(s_Y, 4 * t + uu + 1)
                wait(act, s_OUT, t - 1)
                src = bank[Y_BANK][:, :].rearrange("p (h q) -> p h q", q=SEQ)
                act.activation(YT[:, par, 8 * half:8 * half + 8, b, :], src, ACT.Copy).then_inc(s_Ye, 1)

            keysT_out(0, 0)
            for c in range(4):
                queries_out(0, 0, c)
            keysT_out(1, 1)

            def body(t0):
                for dt in range(2):
                    t = t0 + dt
                    par = dt
                    for uu in range(4):
                        tl, ul = (t, 0) if uu == 3 else (t - 1, uu + 1)
                        if uu == 0 and valid(t, pairs):
                            keys_high(t, par)
                        if valid(tl, pairs):
                            probsT_out(4 * tl + ul, ul)
                        if valid(t, pairs):
                            exps(4 * t + uu, uu)
                        if uu == 3 and valid(t + 2, pairs):
                            keysT_out(t + 2, par)
                        if valid(t + 1, pairs):
                            queries_out(t + 1, 1 - par, uu)
                        if valid(t - 1, pairs):
                            mixed_out(t - 1, 1 - par, uu)

            body(0)
            with act.Fori(1, pairs // 2 - 2) as k:
                body(k * 2)
            body(pairs - 4)
            body(pairs - 2)
            body(pairs)

            def att_tile(need, t, p):
                q = 1 - p
                if valid(t, pairs):
                    need(A["h"], t + 1)
                    need(A["v"], t - 1)
                    act.activation(hTh[:, p, :], bank[2][:, 0:P], ACT.Copy)
                    act.activation(hT[:, p, :], bank[2][:, 0:P], ACT.Copy).then_inc(A["he"], 1)
                if valid(t - 2, pairs):
                    j = t - 2
                    need(A["f"], j + 1)
                    need(A["s"], j)
                    act.activation(FT[:, 0:4, :], bank[3][:, :], ACT.Copy)
                    act.activation(FT[:, 4:8, :], bank[4][:, :], ACT.Copy).then_inc(A["fe"], 1)
                if valid(t, pairs):
                    need(A["qk"], t + 1)
                    need(A["ssd"], t)
                    act.activation(sq[:, 0:8, :], bank[0][:, :], ACT.Square)
                    act.activation(sq[:, 8:16, :], bank[1][:, :], ACT.Square).then_inc(A["sqd"], 1)
                if valid(t - 3, pairs):
                    j = t - 3
                    need(A["pt"], j + 1)
                    need(A["o"], j)
                    act.activation(PTf[:, :, :], bank[7][:, :], ACT.Copy).then_inc(A["pte"], 1)
                if valid(t, pairs):
                    need(A["qnd"], t - 1)
                    act.activation(qs[:, p, 0, :, :], bank[0][:, :], ACT.Copy)
                    act.activation(qs[:, p, 1, :, :], bank[1][:, :], ACT.Copy).then_inc(A["qs"], 1)
                if valid(t - 3, pairs):
                    j = t - 3
                    need(A["o"], j + 1)
                    need(A["wo"], j)
                    act.activation(OTf[0:64, :, :], bank[3][0:64, :], ACT.Copy)
                    act.activation(OTf[64:P, :, :], bank[4][64:P, :], ACT.Copy).then_inc(A["ote"], 1)
                if valid(t - 2, pairs):
                    j = t - 2
                    need(A["sb"], j + 1)
                    act.activation(Pf[:, p, :, :, :], Pf[:, p, :, :, :], ACT.Exp, scale=F_SCALE).then_inc(A["e"], 1)
                if valid(t - 1, pairs):
                    j = t - 1
                    need(A["v"], j + 1)
                    need(A["o"], j - 1)
                    act.activation(V[:, q, :, :, :], bank[2][:, :], ACT.Copy).then_inc(A["ve"], 1)

            def mlp_transposed_out(need, g):
                if valid(g, groups):
                    need(M["t"], g + 1)
                    need(M["nl"], g)
                    act.activation(nT[:, :], bank[1][:, :], ACT.Identity, bias=lnb[:, 0:1],
                                   scale=lng[:, 0:1]).then_inc(M["te"], 1)

            def mlp_group(need, g, p):
                if valid(g, groups):
                    for k, (h0, hw) in enumerate(HB):
                        need(M["a"], 3 * g + k + 1, True)
                        need(M["u"], 3 * g + k - 2, True)
                        act.activation(ge[0:hw, k, :], bank[5 + k][0:hw, :], ACT.Gelu,
                                       bias=b1g[0:hw, k:k + 1]).then_inc(M["g"], 1)
                mlp_transposed_out(need, g + 1)

            with act.Fori(0, LAYERS) as lay:
                att_loop(act, att_tile, lay * pairs, pairs)
                act.wait_ge(s_mw, lay * (16 * MW) + 16 * MW)
                act.wait_ge(s_rt, lay * 2 + 2)
                mlp_loop(act, lambda need: mlp_transposed_out(need, 0), mlp_group, lay * groups,
                         lay * (3 * groups), groups)

        @block.vector
        def _(dve):
            def row_stats(t, par):
                dve.bn_stats(ST[:, par, 0, :], XC[:, bass.ds(2 * t, 1), :])
                dve.bn_stats(ST[:, par, 1, :], XC[:, bass.ds(2 * t + 1, 1), :]).then_inc(s_st, 1)
                dve.wait_ge(s_st, t + 1)
                dve.memset(scratch[:, 5:6], 0.0)
                for b in range(2):
                    last = dve.bn_aggr(MX[:, par, b, :], ST[:, par, b, :])
                last.then_inc(s_ag, 1)
                dve.wait_ge(s_ag, t + 1)
                dve.tensor_scalar(V1[:, par, :], MX[:, par, :, 1], EPS, None, ALU.add).then_inc(s_v1, 1)

            def second_variance(t, par):
                dve.wait_ge(s_r1, t + 1)
                dve.tensor_tensor(V2[:, par, :], R1[:, par, :], R1[:, par, :], ALU.mult).then_inc(s_v2, 1)
                dve.wait_ge(s_v2, 3 * t + 1)
                dve.tensor_tensor(V2[:, par, :], V2[:, par, :], MX[:, par, :, 1], ALU.mult).then_inc(s_v2, 1)
                dve.wait_ge(s_v2, 3 * t + 2)
                dve.tensor_scalar(V2[:, par, :], V2[:, par, :], EPS, None, ALU.add).then_inc(s_v2, 1)

            def latents_rstd(t, par):
                dve.wait_ge(s_r2, t + 1)
                dve.tensor_tensor(R1[SEQ:P, par, :], R1[SEQ:P, par, :], R2[SEQ:P, par, :],
                                  ALU.mult).then_inc(s_r3, 1)

            def normalise(t, par):
                dve.wait_ge(s_r3, t + 1)
                wait(dve, s_KG, t - 1)
                for b in range(2):
                    bb = bass.ds(2 * t + b, 1)
                    last = dve.tensor_scalar(XN[:, par, b, :], XC[:, bb, :].rearrange("p o d -> p (o d)"),
                                             MX[:, par, b, 0:1], R1[:, par, b:b + 1], ALU.subtract, ALU.mult)
                last.then_inc(s_XN, 1)

            def softmax_first(n, uu):
                dve.wait_ge(s_S, n + 1)
                sv = bank[S_BANK[uu % 2]][:, :].rearrange("p (h k) -> p h k", h=4)
                dve.tensor_reduce(mx[:, uu, :], sv, AX.X, ALU.max).then_inc(s_max, 1)
                dve.wait_ge(s_max, n + 1)
                wait(dve, s_PT, n - 3)
                dve.tensor_tensor(Pr[:, uu, :, :], sv, mx[:, uu, :, None].to_broadcast([P, 4, KEYS]),
                                  ALU.subtract).then_inc(s_sub, 1)

            def softmax_second(n, uu):
                dve.wait_ge(s_exp, n + 1)
                dve.tensor_reduce(sm[:, uu, :], Pr[:, uu, :, :], AX.X, ALU.add).then_inc(s_sum, 1)
                dve.wait_ge(s_sum, n + 1)
                dve.reciprocal(rc[:, uu, :], sm[:, uu, :]).then_inc(s_rec, 1)

            def add_cross(t):
                dve.wait_ge(s_OUT, t + 1)
                dve.wait_ge(s_xb, t + 1)
                x1 = X1[:, bass.ds(t, 1), :].rearrange("p o d -> p (o d)")
                dve.scalar_tensor_tensor(x1, bank[OUT_BANK][:, 0:DIM], tg[:, 0:1], x1,
                                         ALU.mult, ALU.add).then_inc(s_xa, 1)

            def x1_stats(t):
                dve.wait_ge(s_xa, t + 1)
                dve.memset(scratch[:, 5:6], 0.0)
                dve.bn_stats(ST1[:, :], X1[:, bass.ds(t, 1), :]).then_inc(s_bn, 1)
                dve.wait_ge(s_bn, t + 1)
                dve.memset(scratch[:, 5:6], 0.0)
                dve.bn_aggr(MX1[:, :], ST1[:, :]).then_inc(s_xg, 1)
                dve.wait_ge(s_xg, t + 1)
                dve.tensor_scalar(VX1[:, :], MX1[:, 1:2], EPS, None, ALU.add).then_inc(s_xv, 1)

            def x1_normalise(t):
                dve.wait_ge(s_xr, t + 1)
                dve.tensor_scalar(Y[:, bass.ds(t, 1), :].rearrange("p o d -> p (o d)"),
                                  X1[:, bass.ds(t, 1), :].rearrange("p o d -> p (o d)"),
                                  MX1[:, 0:1], RX1[:, :], ALU.subtract, ALU.mult).then_inc(s_yn, 1)

            def probsT_split(n, uu):
                dve.wait_ge(s_PTe, n + 1)
                wait(dve, s_Y, n - 1)
                dve.tensor_tensor(PTl[:, uu % 2, :], bank[PT_BANK][:, :], PTh[:, uu % 2, :].bitcast(fp32),
                                  ALU.subtract).then_inc(s_PTl, 1)

            dve.memset(ones_row[:, :], 1.0)
            dve.wait_ge(s_in[0], 32)
            for t in range(3):
                row_stats(t, t % 2) if t < 2 else None
            for t in range(2):
                second_variance(t, t)
            for g in (1, 3, 5):
                dve.wait_ge(s_tr, g + 1)
                dve.tensor_copy(WT[:, g // 2, 4:8, :], bank[g][:, :]).then_inc(s_wtv, 1)
            for t in range(2):
                latents_rstd(t, t)
                normalise(t, t)
            row_stats(2, 0)
            for g in (1, 3):
                dve.wait_ge(s_pa, g + 1)
                dve.tensor_copy(Am[:, 8 + g // 2:16:2, :], bank[g][:, :]).then_inc(s_av, 1)
            for g in (1, 3):
                dve.wait_ge(s_pb, g + 1)
                dve.tensor_copy(Bm[:, 8 + g // 2:16:2, :], bank[4 + g][:, :]).then_inc(s_bv, 1)
            second_variance(2, 0)
            dve.wait_ge(s_tanh, 1)
            dve.wait_ge(s_ctab, 16 * N_CONST)
            dve.tensor_scalar(bout_t[:, :], bout_t[:, :], tg[:, 0:1], None, ALU.mult).then_inc(s_set, 1)

            def body(t0):
                for dt in range(2):
                    t = t0 + dt
                    par = dt
                    for uu in range(4):
                        tl, ul = (t, 0) if uu == 3 else (t - 1, uu + 1)
                        t1, u1 = (t, uu - 1) if uu >= 1 else (t - 1, 3)
                        if valid(t, pairs):
                            softmax_first(4 * t + uu, uu)
                        if valid(t1, pairs):
                            softmax_second(4 * t1 + u1, u1)
                        if valid(tl, pairs):
                            probsT_split(4 * tl + ul, ul)
                        if uu == 3 and valid(t - 2, pairs):
                            add_cross(t - 2)
                            x1_stats(t - 2)
                        if uu == 1 and valid(t - 3, pairs):
                            x1_normalise(t - 3)
                        if uu == 0 and valid(t + 2, pairs):
                            latents_rstd(t + 2, par)
                        if uu == 0 and valid(t + 3, pairs):
                            row_stats(t + 3, 1 - par)
                        if uu == 0 and valid(t + 2, pairs):
                            normalise(t + 2, par)
                        if uu == 2 and valid(t + 3, pairs):
                            second_variance(t + 3, 1 - par)

            body(0)
            dve.wait_ge(s_in[1], 32)
            dve.wait_ge(s_xp, 16)
            body(2)
            with dve.Fori(2, pairs // 2 - 2) as k:
                body(k * 2)
            body(pairs - 4)
            body(pairs - 2)
            body(pairs)
            body(pairs + 2)
            dve.wait_ge(s_yn, pairs)
            dve.memset(scratch[:, 1:2], 0.0).then_inc(s_A, 1)
            dve.memset(scratch[:, 2:3], 0.0).then_inc(s_M, 1)

            def att_tile(need, t, p):
                q = 1 - p

                if valid(t, pairs):
                    need(A["he"], t + 1)
                    need(A["qk"], t - 1)
                    dve.tensor_tensor(hTl[:, p, :], hT[:, p, :], hTh[:, p, :].bitcast(fp32),
                                      ALU.subtract).then_inc(A["hl"], 1)
                if valid(t - 4, pairs):
                    j = t - 4
                    need(A["wo"], j + 1)
                    y = Y[:, bass.ds(t - 4, 1), :].rearrange("p o d -> p (o d)")
                    dve.tensor_tensor(y, bank[7][:, 0:DIM], y, ALU.add).then_inc(A["res"], 1)
                if valid(t - 1, pairs):
                    j = t - 1
                    need(A["rnd"], j + 1)
                    need(A["qs"], j + 1)
                    need(A["rad"], j)
                    need(A["rbd"], j)
                    dve.tensor_tensor(qn[:, 0, :, :], qs[:, q, 0, :, :],
                                      rn[:, q, 0:8, None].to_broadcast([P, FH, DH]), ALU.mult)
                    dve.tensor_tensor(qn[:, 1, :, :], qs[:, q, 1, :, :],
                                      rn[:, q, 8:16, None].to_broadcast([P, FH, DH]),
                                      ALU.mult).then_inc(A["qnd"], 1)
                    need(A["qnd"], j + 1)
                    need(A["f"], j)
                    for o, s_ in ((0, 32), (32, 0)):
                        last = dve.tensor_tensor(rb[:, :, :, o:o + 32], qn[:, :, :, s_:s_ + 32],
                                                 RT2[:, :, None, o:o + 32].to_broadcast([P, 2, FH, 32]), ALU.mult)
                    last.then_inc(A["rbd"], 1)
                if valid(t, pairs):
                    need(A["sqd"], t + 1)
                    dve.tensor_reduce(ss[:, p, :], sq[:, :, :], AX.X, ALU.add).then_inc(A["ssd"], 1)
                    need(A["ssd"], t + 1)
                    dve.tensor_scalar(ss[:, p, :], ss[:, p, :], 1e-24, None, ALU.max).then_inc(A["cl"], 1)
                if valid(t - 2, pairs):
                    j = t - 2
                    need(A["s"], j + 1)
                    need(A["pt"], j - 1)
                    for e in range(2):
                        sv = bank[5 + e][:, 0:256].rearrange("p (c k) -> p c k", c=4)
                        last = dve.tensor_reduce(fm[:, p, :, e], sv, AX.X, ALU.max)
                    last.then_inc(A["m"], 1)
                    need(A["m"], j + 1)
                    for e in range(2):
                        sv = bank[5 + e][:, 0:256].rearrange("p (c k) -> p c k", c=4)
                        last = dve.tensor_tensor(Pf[:, p, :, e, :], sv,
                                                 fm[:, p, :, e:e + 1].to_broadcast([P, 4, SEQ]), ALU.subtract)
                    last.then_inc(A["sb"], 1)
                if valid(t - 1, pairs):
                    j = t - 1
                    need(A["rad"], j + 1)
                    need(A["rbd"], j + 1)
                    dve.tensor_tensor(rb[:, :, :, :], rb[:, :, :, :], ra[:, :, :, :], ALU.add).then_inc(A["ad"], 1)
                if valid(t - 2, pairs):
                    j = t - 2
                    need(A["e"], j + 1)
                    dve.tensor_reduce(fs[:, p, :, :], Pf[:, p, :, :, :], AX.X, ALU.add).then_inc(A["su"], 1)
                    need(A["su"], j + 1)
                    dve.reciprocal(fr[:, p, :, :], fs[:, p, :, :]).then_inc(A["r"], 1)

            def mlp_stats(need, g):
                if valid(g, groups):
                    need(M["h"], g + 1)
                    hb = bank[0][:, :].rearrange("p (t d) -> p t d", t=GROUP)
                    for k in range(GROUP):
                        last = dve.bn_stats(ST2[:, k, :], hb[:, k, :])
                    last.then_inc(M["bs"], 1)
                    need(M["bs"], g + 1)
                    dve.memset(scratch[:, 0:1], 0.0)
                    for k in range(GROUP):
                        last = dve.bn_aggr(MV[:, k, :], ST2[:, k, :])
                    last.then_inc(M["ba"], 1)
                    need(M["ba"], g + 1)
                    dve.tensor_scalar(ve[:, :], MV[:, :, 1], EPS, None, ALU.add).then_inc(M["ve"], 1)

            def mlp_normed(need, g):
                if valid(g, groups):
                    need(M["rs"], g + 1)
                    need(M["t"], g)
                    hb = bank[0][:, :].rearrange("p (t d) -> p t d", t=GROUP)
                    for k in range(GROUP):
                        last = dve.tensor_scalar(hn[:, k, :], hb[:, k, :], MV[:, k, 0:1], rs[:, k:k + 1],
                                                 ALU.subtract, ALU.mult)
                    last.then_inc(M["hn"], 1)

            def mlp_split(need, g):
                if valid(g, groups):
                    need(M["te"], g + 1)
                    need(M["a"], 3 * g, True)
                    dve.tensor_copy(nTh[:, :], nT[:, :]).then_inc(M["nh"], 1)
                    need(M["nh"], g + 1)
                    dve.tensor_tensor(nTl[:, :], nT[:, :], nTh[:, :].bitcast(fp32),
                                      ALU.subtract).then_inc(M["nl"], 1)

            def mlp_group(need, g, p):
                if valid(g, groups):
                    for k, (h0, hw) in enumerate(HB):
                        need(M["g"], 3 * g + k + 1, True)
                        need(M["d"], g - 1)
                        dve.scalar_tensor_tensor(u[0:hw, p, k, :], bank[2 + k][0:hw, :], b1a[0:hw, k:k + 1],
                                                 ge[0:hw, k, :], ALU.add, ALU.mult).then_inc(M["u"], 1)
                        if k == 0:
                            mlp_normed(need, g + 1)
                if valid(g - 1, groups):
                    j = g - 1
                    need(M["d"], j + 1)
                    y = Y[:, bass.ds((g - 1) * GROUP, GROUP), :]
                    dve.tensor_tensor(y, bank[2][:, :].rearrange("p (t d) -> p t d", t=GROUP), y,
                                      ALU.add).then_inc(M["res"], 1)
                mlp_split(need, g + 1)
                if valid(g - 1, groups):
                    need(M["res"], j + 1)
                    dve.tensor_tensor(y, y, b2t[:, None, :].to_broadcast([P, GROUP, DIM]), ALU.add).then_inc(M["r2"], 1)
                mlp_stats(need, g + 2)

            with dve.Fori(0, LAYERS) as lay:
                li = lay * pairs
                gi = lay * groups
                gi3 = lay * (3 * groups)
                dve.wait_ge(s_lw, lay * (16 * LW) + 16 * LW)
                dve.tensor_tensor(RT1[:, :, :], rot[:, 0:2, :], qks[:, :, :], ALU.mult)
                for o, s_ in ((0, 32), (32, 0)):
                    last = dve.tensor_tensor(RT2[:, :, o:o + 32], rot[:, 2:4, o:o + 32], qks[:, :, s_:s_ + 32], ALU.mult)
                last.then_inc(s_rt, 1)
                dve.wait_ge(s_rt, lay * 2 + 1)
                dve.wait_ge(s_pm, 2)
                dve.wait_ge(s_M, lay * 1 + 1)
                dve.memset(scratch[:, 3:4], 0.0)
                dve.tensor_copy(lng[:, :], lnp[:, bass.ds(lay, 1)])
                dve.tensor_copy(lnb[:, :], lnp[:, bass.ds(lay + LAYERS, 1)]).then_inc(s_rt, 1)
                att_loop(dve, att_tile, li, pairs)
                dve.wait_ge(A["res"], li + pairs)
                dve.memset(scratch[:, 1:2], 0.0).then_inc(s_A, 1)
                dve.wait_ge(s_mw, lay * (16 * MW) + 16 * MW)
                dve.memset(scratch[:, 3:4], 0.0)
                mlp_loop(dve, lambda need: (mlp_stats(need, 0), mlp_normed(need, 0), mlp_split(need, 0),
                                            mlp_stats(need, 1)), mlp_group, gi, gi3, groups)
                dve.wait_ge(M["r2"], gi + groups)
                dve.memset(scratch[:, 2:3], 0.0).then_inc(s_M, 1)
            dve.wait_ge(s_M, LAYERS + 1)
            q = pairs // 4
            for c in range(4):
                r = slice(c * q, (c + 1) * q)
                dve.scalar_tensor_tensor(Y[:, r, :], Y[:, r, :], tg[:, 1:2], X1[:, r, :],
                                         ALU.mult, ALU.add).then_inc(s_fin, 1)

        @block.gpsimd
        def _(pool):
            pool.memset(mhb[:, :], -0.5).then_inc(s_pm, 1)
            pool.wait_ge(s_pm, 1)
            def rows_rstd(t, par):
                pool.wait_ge(s_v1, t + 1)
                pool.tensor_tensor(R1[:, par, :], V1[:, par, :], mhb[:, 0:2], ALU.pow).then_inc(s_r1, 1)

            def rows_rstd2(t, par):
                pool.wait_ge(s_v2, 3 * t + 3)
                pool.tensor_tensor(R2[:, par, :], V2[:, par, :], mhb[:, 0:2], ALU.pow).then_inc(s_r2, 1)

            def scale_keys(t, par):
                pool.wait_ge(s_XN, t + 1)
                wait(pool, s_KT, t - 1)
                wait(pool, s_KX, t - 1)
                pool.tensor_tensor(KN[:, par, :, :], XN[:, par, :, :], G[:, None, :].to_broadcast([P, 2, DIM]),
                                   ALU.mult).then_inc(s_KG, 1)
                pool.wait_ge(s_KG, t + 1)
                pool.tensor_tensor(KN[:, par, :, :], KN[:, par, :, :], Bt[:, None, :].to_broadcast([P, 2, DIM]),
                                   ALU.add).then_inc(s_KN, 1)

            def keys_low(t, par):
                pool.wait_ge(s_KXh, t + 1)
                pool.tensor_tensor(KXl[:, par, :, :], KN[:, par, :, :], KXh[:, par, :, :].bitcast(fp32),
                                   ALU.subtract).then_inc(s_KX, 1)

            def add_bias(t):
                x1 = X1[:, bass.ds(t, 1), :].rearrange("p o d -> p (o d)")
                pool.tensor_tensor(x1, x1, bout_t[:, :], ALU.add).then_inc(s_xb, 1)

            def x1_rstd(t):
                pool.wait_ge(s_xv, t + 1)
                pool.tensor_tensor(RX1[:, :], VX1[:, :], mhb[:, 0:1], ALU.pow).then_inc(s_xr, 1)

            def split_attention(lay):
                pool.wait_ge(s_lw, lay * (16 * LW) + 16 * LW)
                pool.tensor_tensor(scratch[:, 4:5], mhb[:, 0:1], mhb[:, 0:1], ALU.add)
                pool.tensor_copy(Wh[:, :], Wraw).then_inc(s_ws, 1)
                pool.wait_ge(s_ws, lay * 2 + 1)
                pool.tensor_tensor(Wl[:, :], Wraw, Wh[:, :].bitcast(fp32), ALU.subtract).then_inc(s_ws, 1)

            def split_mlp(lay):
                pool.wait_ge(s_mw, lay * (16 * MW) + 16 * MW)
                pool.tensor_tensor(scratch[:, 4:5], mhb[:, 0:1], mhb[:, 0:1], ALU.add)
                pool.tensor_copy(W1h[:, :], W1raw).then_inc(s_w1, 1)
                pool.wait_ge(s_w1, lay * 2 + 1)
                pool.tensor_tensor(W1l[:, :], W1raw, W1h[:, :].bitcast(fp32), ALU.subtract).then_inc(s_w1, 1)

            rows_rstd(0, 0)
            rows_rstd(1, 1)
            rows_rstd2(0, 0)
            rows_rstd2(1, 1)
            pool.wait_ge(s_ctab, 16 * N_CONST)
            scale_keys(0, 0)
            scale_keys(1, 1)
            pool.wait_ge(s_msk, 16)
            pool.tensor_scalar(mask_row[:, :, :], mask_u8[:, :, :], NEG, 0.0, ALU.mult, ALU.add).then_inc(s_mr, 1)
            rows_rstd(2, 0)
            pool.tensor_copy(lnp[:, :], yc[:, 0, 0:2 * LAYERS]).then_inc(s_pm, 1)
            rows_rstd2(2, 0)

            def body(t0):
                for dt in range(2):
                    t = t0 + dt
                    par = dt
                    for uu in range(4):
                        n = 4 * t + uu
                        if uu == 0 and valid(t + 3, pairs):
                            rows_rstd(t + 3, 1 - par)
                        if uu == 1 and valid(t, pairs):
                            keys_low(t, par)
                        if uu == 1 and valid(t + 2, pairs):
                            scale_keys(t + 2, par)
                        if uu == 3 and valid(t + 3, pairs):
                            rows_rstd2(t + 3, 1 - par)
                        if uu == 2 and valid(t - 2, pairs):
                            add_bias(t - 2)
                        if valid(t, pairs):
                            pool.wait_ge(s_rec, n + 1)
                            pool.tensor_tensor(Pr[:, uu, :, :], Pr[:, uu, :, :],
                                               rc[:, uu, :, None].to_broadcast([P, 4, KEYS]), ALU.mult).then_inc(s_pn, 1)
                        if uu == 3 and valid(t - 2, pairs):
                            x1_rstd(t - 2)

            body(0)
            pool.wait_ge(s_set, 1)
            pool.wait_ge(s_xp, 16)
            with pool.Fori(1, pairs // 2 - 2) as k:
                body(k * 2)
            body(pairs - 4)
            body(pairs - 2)
            split_attention(0)
            body(pairs)

            def att_tile(need, t, p):
                q = 1 - p
                if valid(t - 3, pairs):
                    j = t - 3
                    need(A["r"], j + 1)
                    pool.tensor_tensor(Pf[:, q, :, :, :], Pf[:, q, :, :, :],
                                       fr[:, q, :, :, None].to_broadcast([P, 4, 2, SEQ]), ALU.mult).then_inc(A["pn"], 1)
                if valid(t - 1, pairs):
                    j = t - 1
                    need(A["qnd"], j + 1)
                    need(A["ad"], j)
                    pool.tensor_tensor(ra[:, :, :, :], qn[:, :, :, :],
                                       RT1[:, :, None, :].to_broadcast([P, 2, FH, DH]), ALU.mult).then_inc(A["rad"], 1)
                if valid(t, pairs) and valid(t + 1, pairs):
                    copy_tile(t + 1, 1 - p)
                if valid(t, pairs):
                    need(A["cl"], t + 1)
                    pool.tensor_tensor(rn[:, p, :], ss[:, p, :], mhb[:, 0:16], ALU.pow).then_inc(A["rnd"], 1)

            def copy_tile(t, p):
                pool.tensor_copy(yc[:, p, :], Y[:, bass.ds(t, 1), :].rearrange("p o d -> p (o d)")).then_inc(A["yc"], 1)

            def mlp_rstd(need, g):
                if valid(g, groups):
                    need(M["ve"], g + 1)
                    pool.tensor_tensor(rs[:, :], ve[:, :], mhb[:, 0:GROUP], ALU.pow).then_inc(M["rs"], 1)

            def mlp_group(need, g, p):
                mlp_rstd(need, g + 2)

            def layer(lay):
                pool.wait_ge(s_M, lay * 1 + 1)
                pool.wait_ge(s_rt, lay * 2 + 2)
                pool.tensor_tensor(scratch[:, 4:5], mhb[:, 0:1], mhb[:, 0:1], ALU.add)
                copy_tile(0, 0)
                att_loop(pool, att_tile, lay * pairs, pairs)
                split_mlp(lay)
                mlp_loop(pool, lambda need: (mlp_rstd(need, 0), mlp_rstd(need, 1)), mlp_group, lay * groups,
                         lay * (3 * groups), groups)

            with pool.Fori(0, LAYERS - 1) as lay:
                layer(lay)
                split_attention(lay + 1)
            layer(LAYERS - 1)


def tables():
    import numpy as np
    ident = np.eye(P, dtype=np.float32)
    shift = np.zeros((P, P), np.float32)
    for o in range(P):
        if o % SEQ:
            shift[o - 1, o] = 1.0
    q = np.arange(P)[:, None] % SEQ
    causal = np.where(q < np.arange(SEQ)[None, :], np.float32(NEG), np.float32(0.0)).astype(np.float32)
    half = np.arange(0, DH, 2, dtype=np.float32)
    freqs = np.arange(SEQ, dtype=np.float32)[:, None] * (1.0 / 10000.0 ** (half / DH)).astype(np.float32)[None, :]
    freqs = np.concatenate([freqs, freqs], -1)
    base = (half + 0.4 * DH) / (1.4 * DH)
    power = (np.arange(SEQ, dtype=np.float32) - SEQ // 2) / 32.0
    scale = base[None, :] ** power[:, None]
    scale = np.concatenate([scale, scale], -1)
    cos, sin = np.cos(freqs), np.sin(freqs)
    sign = np.where(np.arange(DH) < DH // 2, -1.0, 1.0)[None, :]
    rot = np.stack([cos * scale, cos / scale, sign * sin * scale, sign * sin / scale], 1).astype(np.float32)
    return ident, shift, causal, np.ascontiguousarray(np.concatenate([rot, rot], 0))


_INS = ["x", "ctx_1024", "mask_BxS2_bk0", "g_xattn", "g_ffn", "L0_xattn_Wq", "L0_xattn_Wkv",
        "L0_xattn_Wout", "L0_xattn_bout", "L0_xattn_g_media", "L0_xattn_b_media",
        "L0_xattn_g_latent", "L0_xattn_b_latent", "L0_ffn_wqkv", "L0_ffn_q_scale",
        "L0_ffn_k_scale", "L0_ffn_wo", "L0_ffn_ln_g", "L0_ffn_ln_b", "L0_ffn_w1", "L0_ffn_b1",
        "L0_ffn_w2", "L0_ffn_b2"]


def kernel(**inputs):
    import numpy as np
    import concourse.bacc as bacc
    from concourse.bass_utils import run_bass_kernel_spmd

    nc = bacc.Bacc("TRN2", target_bir_lowering=False, num_devices=1)
    arrays, args = {}, []
    for name, a in [(n, inputs[n]) for n in _INS] + list(zip(("ident", "shift", "causal", "rot"), tables())):
        a = np.ascontiguousarray(a)
        arrays[f"in_{name}"] = a
        args.append(nc.dram_tensor(f"in_{name}", a.shape, mybir.dt.from_np(a.dtype), kind="ExternalInput").ap())
    shape = (BATCH, SEQ, DIM)
    args.append(nc.dram_tensor("out", shape, fp32, kind="ExternalOutput").ap())
    build(nc, *args)
    r = run_bass_kernel_spmd(nc, [arrays], core_ids=[0])
    return r.results[0]["out"]
```

```python
import concourse.bass as bass
from concourse import mybir
from contextlib import ExitStack

fp32 = mybir.dt.float32
bf16 = mybir.dt.bfloat16
fp32r = mybir.dt.float32r
u8 = mybir.dt.uint8
ALU = mybir.AluOpType
ACT = mybir.ActivationFunctionType
AX = mybir.AxisListType

BATCH, SEQ, DIM = 64, 64, 128
P = 128
PAIRS = BATCH // 2
XH, DH = 16, 64
HPB = XH // 2
KEYS = 2 * SEQ
FH = 8
INNER = FH * DH
LAYERS = 2
HID = DIM * 4 * 2 // 3
HB = [(0, 128), (128, 128), (256, HID - 256)]
GROUP = 4
GROUPS = PAIRS // GROUP
EPS = 1e-5
NEG = -1e30
X_SCALE = DH ** -0.5
F_SCALE = 8.0


def valid(i, n):
    return not isinstance(i, int) or 0 <= i < n


def wait(eng, sem, value):
    if not isinstance(value, int) or value > 0:
        eng.wait_ge(sem, value)


def att_loop(eng, tile, base, n, lead_in):
    def need(sem, value):
        if not isinstance(value, int) or value > 0:
            eng.wait_ge(sem, base + value)
    for t in range(6):
        lead_in(need, t - n)
        tile(need, t, t % 2)
    with eng.Fori(3, n // 2 - 1) as k:
        tile(need, k * 2, 0)
        tile(need, k * 2 + 1, 1)
    for t in range(n - 2, n + 4):
        lead_in(need, t - n)
        tile(need, t, t % 2)


def mlp_need(eng, base, base3):
    def need(sem, value, triple=False):
        if not isinstance(value, int) or value > 0:
            eng.wait_ge(sem, (base3 if triple else base) + value)
    return need


def mlp_loop(eng, group, need, n):
    group(need, 0, 0)
    group(need, 1, 1)
    with eng.Fori(1, n // 2 - 1) as k:
        group(need, k * 2, 0)
        group(need, k * 2 + 1, 1)
    for g in range(n - 2, n + 1):
        group(need, g, g % 2)


def build(nc, x, ctx_t, mask, g_x, g_f, wq, wkv, wout, bout, g_media, b_media, g_latent, b_latent,
          wqkv, q_scale, k_scale, wo, ln_g, ln_b, w1, b1, w2, b2, ident_d, shift_d, causal_d,
          rot_d, out, pairs=PAIRS):
    groups = pairs // GROUP
    stack = ExitStack()
    with stack:
        stack.enter_context(nc.allow_non_contiguous_dma(reason="parameters that lie one to a partition"))

        def sb(name, shape, dt=fp32):
            return stack.enter_context(nc.sbuf_tensor(name, shape, dt))

        def sem(name):
            return stack.enter_context(nc.semaphore(name))

        NB = 2 * pairs
        XC = sb("XC", [P, BATCH, DIM])
        X1 = sb("X1", [P, pairs, DIM])
        Y = XC[:, 0:pairs, :]
        XS = XC[:, PAIRS:BATCH, :].rearrange("p (k a) d -> p k (a d)", k=4)
        ident = sb("ident", [P, P])
        identb = sb("identb", [P, P], bf16)
        shift = sb("shift", [P, P])
        causal = sb("causal", [P, SEQ], bf16)
        ones_row = sb("ones_row", [1, P], bf16)
        mask_row = sb("mask_row", [1, NB, SEQ], bf16)
        G = sb("G", [P, DIM])
        Bt = sb("Bt", [P, DIM])
        bout_t = sb("bout_t", [P, DIM])
        gates = sb("gates", [P, 2])
        tg = sb("tg", [P, 2])
        minus_half = sb("minus_half", [P, 2 * FH])
        scratch = sb("scratch", [P, 8])
        lnp = sb("lnp", [P, 2 * LAYERS])
        ST = sb("ST", [P, 2, 2, 6])
        MX = sb("MX", [P, 2, 2, 2])
        V1 = sb("V1", [P, 2, 2])
        R1 = sb("R1", [P, 2, 2])
        V2 = sb("V2", [P, 2, 2])
        R2 = sb("R2", [P, 2, 2])
        ST1 = sb("ST1", [P, 6])
        MX1 = sb("MX1", [P, 2])
        VX1 = sb("VX1", [P, 1])
        RX1 = sb("RX1", [P, 1])
        Am = sb("Am", [P, XH, DIM])
        Bm = sb("Bm", [P, XH, DIM])
        XN = sb("XN", [P, 2, 2, DIM])
        KN = sb("KN", [P, 2, 2, DIM])
        KXh = sb("KXh", [P, 2, 2, DIM], fp32r)
        KXl = sb("KXl", [P, 2, 2, DIM], fp32r)
        KT = sb("KT", [P, 2, 2, KEYS])
        QP = sb("QP", [P, 2, 2, XH, SEQ])
        YT = sb("YT", [P, 2, XH, 2, SEQ])
        QPf = QP[:, :, :, :, :].rearrange("p a b h q -> p (a b h q)")
        YTf = YT[:, :, :, :, :].rearrange("p a h b q -> p (a h b q)")
        Wq = QPf[:, 0:XH * DH]
        Wkv = QPf[:, XH * DH:3 * XH * DH]
        Wout = QPf[:, 3 * XH * DH:4 * XH * DH].rearrange("p (c o) -> p c o", o=DIM)
        WT = YTf[:, 0:3 * XH * DH].rearrange("p (w c o) -> p w c o", w=3, o=DIM)
        mask_u8 = YTf[0:1, 3 * XH * DH:3 * XH * DH + NB * SEQ // 4].bitcast(u8).rearrange("p (b s) -> p b s", s=SEQ)
        Pr = sb("Pr", [P, 4, 4, KEYS])
        PTh = sb("PTh", [P, 2, 512], fp32r)
        PTl = sb("PTl", [P, 2, 512], fp32r)
        mx = sb("mx", [P, 4, 4])
        sm = sb("sm", [P, 4, 4])
        rc = sb("rc", [P, 4, 4])
        Wqkv = sb("Wv", [P, INNER])
        Wh = sb("Wh", [P, 2 * INNER], fp32r)
        Wl = sb("Wl", [P, 2 * INNER], fp32r)
        Wo = sb("Wo", [P, FH // 2, DIM])
        W1h = sb("W1h", [P, 2 * HID], fp32r)
        W1l = sb("W1l", [P, 2 * HID], fp32r)
        W2 = sb("W2", [P, 3, DIM])
        b1a = sb("b1a", [P, 3])
        b1g = sb("b1g", [P, 3])
        b2t = sb("b2t", [P, DIM])
        lng = sb("lng", [P, 1])
        lnb = sb("lnb", [P, 1])
        rot = sb("rot", [P, 4, DH])
        qks = sb("qks", [P, 2, DH])
        RT1 = sb("RT1", [P, 2, DH])
        RT2 = sb("RT2", [P, 2, DH])
        yc = sb("yc", [P, 2, DIM])
        hT = sb("hT", [P, 2, P])
        hTh = sb("hTh", [P, 2, P], fp32r)
        hTl = sb("hTl", [P, 2, P], fp32r)
        sq = XS[:, 0, :].rearrange("p (h d) -> p h d", d=DH)
        ss = sb("ss", [P, 2, 16])
        rn = sb("rn", [P, 2, 16])
        qn = XS[:, 1, :].rearrange("p (w h d) -> p w h d", w=2, d=DH)
        qs = QPf[:, 2048:4096].rearrange("p (a w h d) -> p a w h d", a=2, w=2, d=DH)
        ra = XS[:, 2, :].rearrange("p (w h d) -> p w h d", w=2, d=DH)
        rb = XS[:, 3, :].rearrange("p (w h d) -> p w h d", w=2, d=DH)
        Wraw = XS[:, 1, :]
        FT = YTf[:, 0:1024].rearrange("p (c n) -> p c n", n=P)
        V = sb("V", [P, 2, 2, 4, DH])
        Pf = sb("Pf", [P, 2, 4, 2, SEQ])
        fm = sb("fm", [P, 2, 4, 2])
        fs = sb("fs", [P, 2, 4, 2])
        fr = sb("fr", [P, 2, 4, 2])
        PTf = YTf[:, 1024:1536].rearrange("p (c n) -> p c n", n=P)
        OTf = YTf[:, 2048:2560].rearrange("p (c n) -> p c n", n=P)
        ST2 = sb("ST2", [P, GROUP, 6])
        MV = sb("MV", [P, GROUP, 2])
        ve = sb("ve", [P, GROUP])
        rs = sb("rs", [P, GROUP])
        hn = YTf[:, 2560:3072].rearrange("p (t d) -> p t d", d=DIM)
        nT = YTf[:, 3072:3584]
        nTh = sb("nTh", [P, 512], fp32r)
        nTl = sb("nTl", [P, 512], fp32r)
        W1raw = Pr[:, :, :, :].rearrange("p a h k -> p (a h k)")[:, 0:2 * HID]
        ge = QPf[:, 0:3 * 512].rearrange("p (k n) -> p k n", k=3)
        u = sb("u", [P, 2, 3, 512])

        bank = [stack.enter_context(nc.psum_tensor(f"bank{i}", [P, 512], fp32)) for i in range(8)]

        s_wq, s_wk, s_wo_ = sem("wq_loaded"), sem("wkv_loaded"), sem("wout_loaded")
        s_id = sem("identity_loaded")
        s_gb = sem("token_norms_loaded")
        s_ctab = sem("constants_loaded")
        s_msk = sem("mask_loaded")
        s_in = [sem(f"tokens_loaded{i}") for i in range(2)]
        s_xp = sem("pair_tiles_loaded")
        s_tr, s_pa, s_pb = sem("weights_transposed"), sem("qk_products"), sem("vo_products")
        s_wta, s_wtv = sem("weightsT_by_scalar"), sem("weightsT_by_vector")
        s_aa, s_av = sem("qk_products_by_scalar"), sem("qk_products_by_vector")
        s_ba, s_bv = sem("vo_products_by_scalar"), sem("vo_products_by_vector")
        s_tanh, s_cb = sem("gates_ready"), sem("bf16_constants")
        s_mr = sem("mask_row_ready")
        s_bias = sem("cross_bias_gated")

        block = stack.enter_context(nc.Block())
        N_CONST = 8
        FIRST = min(12, NB)

        s_out = sem("output_stored")
        s_gated, s_fin, s_fin_last = sem("output_gated"), sem("output_ready"), sem("last_output_ready")
        s_lw = sem("attention_weights_loaded")
        s_mw = sem("mlp_weights_loaded")
        s_A = sem("attention_phase_done")
        s_M = sem("mlp_phase_done")
        s_ready = sem("layer_input_tiles")
        s_rt = sem("rotary_tables_built")
        s_bn = sem("row_statistics")
        s_ws = sem("attention_weights_split")
        s_w1 = sem("mlp_weights_split")
        s_pm = sem("pool_constants")
        s_XN = sem("tokens_normalised")
        LW, MW = 5, 11
        RAW_FREE = 3 * PAIRS // 4

        @block.sync
        def _(sp):
            sp.dma_start(ident[:, :], ident_d).then_inc(s_id, 16)
            sp.dma_start(Wq[:, :], wq).then_inc(s_wq, 16)
            for i, r in enumerate((slice(0, FIRST), slice(FIRST, NB))):
                sp.dma_start(XC[0:SEQ, r, :], ctx_t[r].rearrange("b s d -> s b d")).then_inc(s_in[i], 16)
                sp.dma_start(XC[SEQ:P, r, :], x[r].rearrange("b s d -> s b d")).then_inc(s_in[i], 16)
                if i == 0:
                    sp.dma_start(Wkv[:, :], wkv).then_inc(s_wk, 16)
                    sp.dma_start(Wout[:, :, :], wout.rearrange("(c p) o -> p c o", p=P)).then_inc(s_wo_, 16)
            sp.dma_start(X1[:, :, :], x.rearrange("(t b) s d -> (b s) t d", b=2)).then_inc(s_xp, 16)

            def load_attention(lay):
                wl = wqkv[bass.ds(lay, 1)].rearrange("l p n -> (l p) n")
                sp.dma_start(Wraw, wl[:, 0:2 * INNER]).then_inc(s_lw, 16)
                sp.dma_start(Wqkv[:, :], wl[:, 2 * INNER:]).then_inc(s_lw, 16)
                sp.dma_start(Wo[:, :, :], wo[bass.ds(lay, 1)].rearrange("l (c p) o -> p (l c) o", p=P)).then_inc(s_lw, 16)
                sp.dma_start(qks[:, 0, :], q_scale[bass.ds(lay, 1), :].to_broadcast([P, DH])).then_inc(s_lw, 16)
                sp.dma_start(qks[:, 1, :], k_scale[bass.ds(lay, 1), :].to_broadcast([P, DH])).then_inc(s_lw, 16)

            def load_mlp(lay):
                sp.dma_start(W1raw, w1[bass.ds(lay, 1)].rearrange("l p n -> (l p) n")).then_inc(s_mw, 16)
                w2l = w2[bass.ds(lay, 1)].rearrange("l k o -> (l k) o")
                b1l = b1[bass.ds(lay, 1), :].rearrange("l k -> k l")
                for j, (h0, hn_) in enumerate(HB):
                    sp.dma_start(W2[0:hn_, j, :], w2l[h0:h0 + hn_, :]).then_inc(s_mw, 16)
                    sp.dma_start(b1a[0:hn_, j:j + 1], b1l[h0:h0 + hn_, :]).then_inc(s_mw, 16)
                    sp.dma_start(b1g[0:hn_, j:j + 1], b1l[HID + h0:HID + h0 + hn_, :]).then_inc(s_mw, 16)
                sp.dma_start(b2t[:, :], b2[bass.ds(lay, 1), :].to_broadcast([P, DIM])).then_inc(s_mw, 16)

            sp.wait_ge(s_XN, min(RAW_FREE, pairs))
            load_attention(0)
            sp.wait_ge(s_A, 1)
            load_mlp(0)
            with sp.Fori(1, LAYERS) as lay:
                sp.wait_ge(s_A, lay + 1)
                load_attention(lay)
                sp.wait_ge(s_M, lay + 1)
                sp.wait_ge(s_ready, lay * pairs + pairs)
                load_mlp(lay)
            stores = [(g, g + 2) for g in range(0, groups - 2, 2)] + [(groups - 2, groups - 1), (groups - 1, groups)]
            for g0, g1 in stores:
                if g1 < groups:
                    sp.wait_ge(s_fin, g1)
                else:
                    sp.wait_ge(s_fin_last, 1)
                r = slice(g0 * GROUP, g1 * GROUP)
                sp.dma_start(out.rearrange("(t b) s d -> (b s) t d", b=2)[:, r, :], Y[:, r, :]).then_inc(s_out, 16)
            sp.wait_ge(s_out, 16 * len(stores))

        s_S, s_max, s_sub, s_exp = sem("scores"), sem("maxima"), sem("shifted"), sem("exps")
        s_sum, s_rec, s_pn = sem("sums"), sem("reciprocals"), sem("probs_normalised")
        s_PT, s_PTe = sem("probs_transposed"), sem("probsT_in_sbuf")
        s_Y, s_Ye = sem("mixed_keys"), sem("mixed_keys_in_sbuf")
        s_xb, s_xg, s_xv, s_xr = sem("x_biased"), sem("x1_aggr"), sem("x1_var_eps"), sem("x1_rstd")
        s_Q, s_Qe = sem("queries"), sem("queries_in_sbuf")
        s_KG, s_KN = sem("keys_scaled"), sem("keys_ready")
        s_PTl = sem("probsT_split")
        s_st, s_ag, s_v1, s_r1 = sem("x_stats"), sem("x_aggr"), sem("x_var_eps"), sem("x_rstd")
        s_v2, s_r2, s_r3 = sem("x_var2"), sem("x_rstd2"), sem("x_rstd_product")
        s_KXh = sem("keys_high")
        s_KT, s_KTe, s_KX = sem("keys_transposed"), sem("keysT_in_sbuf"), sem("keys_copied")
        s_OUT, s_xa = sem("cross_out"), sem("cross_out_added")
        S_BANK, Q_BANK, PT_BANK, Y_BANK, OUT_BANK, KT_BANK = (0, 1), (2, 3), 4, 5, 6, 7

        label = {"yc": "copied", "h": "hT_psum", "he": "hT_sbuf", "hl": "hT_low_part", "qk": "qk_psum",
                 "qs": "qk_sbuf", "sqd": "squares", "ssd": "norms2", "cl": "norms2_clipped",
                 "rnd": "inv_norms", "qnd": "qk_normed", "rad": "cos_part", "rbd": "sin_part",
                 "ad": "qk_rotated", "v": "v_psum", "ve": "v_sbuf", "f": "qkT_psum", "fe": "qkT_sbuf",
                 "s": "f_scores", "m": "f_max", "sb": "f_shifted", "e": "f_exp", "su": "f_sum",
                 "r": "f_rec", "pn": "f_probs", "pt": "f_probsT_psum", "pte": "f_probsT_sbuf",
                 "o": "f_outT_psum", "ote": "f_outT_sbuf", "wo": "f_proj", "res": "f_residual"}
        A = {k: sem(v) for k, v in label.items()}
        mnames = {"hc": "m_unshifted", "h": "m_shifted", "bs": "m_stats", "ba": "m_aggr",
                  "ve": "m_var_eps", "rs": "m_rstd",
                  "hn": "m_normed", "t": "m_normedT", "te": "m_normedT_sbuf", "a": "m_up", "g": "m_gelu",
                  "u": "m_gated", "d": "m_down", "res": "m_residual",
                  "nh": "m_high_part", "nl": "m_low_part"}
        M = {k: sem(v) for k, v in mnames.items()}

        @block.tensor
        def _(pe):
            pe.wait_ge(s_id, 16)
            pe.wait_ge(s_wq, 16)
            for g in range(6):
                if g == 2:
                    pe.wait_ge(s_wk, 16)
                for i in range(4):
                    blk = 4 * (g % 2) + i
                    src = Wq if g < 2 else Wkv
                    c = (blk + (HPB if g >= 4 else 0)) * P
                    last = nc.tensor.transpose(bank[g][:, i * P:(i + 1) * P], src[:, c:c + P], ident[:, :])
                last.then_inc(s_tr, 1)
            for g in range(8):
                par, quad, isb = g // 2 % 2, g % 2, g // 4
                if g == 0:
                    pe.wait_ge(s_wta, 2)
                    pe.wait_ge(s_wtv, 2)
                if g == 4:
                    pe.wait_ge(s_wta, 3)
                    pe.wait_ge(s_wtv, 3)
                    pe.wait_ge(s_wo_, 16)
                r = slice(64 * par, 64 * par + 64)
                for i in range(4):
                    hb = 4 * quad + i
                    if isb:
                        l, rr = WT[r, 2, hb, :], Wout[r, hb, :]
                    else:
                        l, rr = WT[r, 0, hb, :], WT[r, 1, hb, :]
                    last = nc.tensor.matmul(bank[g][:, i * P:(i + 1) * P], l, rr, start=True, stop=True)
                last.then_inc(s_pb if isb else s_pa, 1)

            def keys_transposed(t, par):
                pe.wait_ge(s_KN, t + 1)
                wait(pe, s_KTe, t)
                for b in range(2):
                    last = nc.tensor.transpose(bank[KT_BANK][:, b * KEYS:(b + 1) * KEYS],
                                               KN[:, par, b, :], ident[:, :])
                last.then_inc(s_KT, 1)

            def queries(t, par, c):
                pe.wait_ge(s_KTe, t + 1)
                wait(pe, s_Qe, 4 * t + c - 1)
                for i in range(4):
                    last = nc.tensor.matmul(bank[Q_BANK[c % 2]][:, i * P:(i + 1) * P], Am[:, 4 * c + i, :],
                                            KT[:, par, :, SEQ:KEYS], start=True, stop=True)
                last.then_inc(s_Q, 1)

            def probs_transposed(n, uu):
                pe.wait_ge(s_pn, n + 1)
                wait(pe, s_PTl, n)
                for i in range(4):
                    last = nc.tensor.transpose(bank[PT_BANK][:, i * P:(i + 1) * P], Pr[:, uu, i, :], ident[:, :])
                last.then_inc(s_PT, 1)

            def scores(t, par, uu):
                n, b, half = 4 * t + uu, uu // 2, uu % 2
                pe.wait_ge(s_Qe, 4 * t + 2 * half + 2)
                pe.wait_ge(s_KTe, t + 1)
                wait(pe, s_sub, n - 1)
                for i in range(4):
                    h = 8 * half + 2 * i
                    nc.tensor.matmul(bank[S_BANK[uu % 2]][:, i * P:(i + 1) * P], QP[:, par, b, h:h + 2, :],
                                     KT[:, par, b, :], start=(i == 0), stop=False, skip_group_check=True)
                m = mask_row[0:1, bass.ds(2 * t + b, 1), :].to_broadcast([1, 4, SEQ])
                sv = bank[S_BANK[uu % 2]][:, :].rearrange("p (a k) -> p a k", a=4)[:, :, 0:SEQ]
                nc.tensor.matmul(sv, ones_row[:, :], m,
                                 start=False, stop=True, skip_group_check=True).then_inc(s_S, 1)

            def mixed(t, par, uu):
                n, b = 4 * t + uu, uu // 2
                pe.wait_ge(s_PTl, n + 1)
                pe.wait_ge(s_KX, t + 1)
                wait(pe, s_Ye, n)
                for k, (l, r) in enumerate(((KXh, PTh), (KXh, PTl), (KXl, PTh))):
                    last = nc.tensor.matmul(bank[Y_BANK][:, :], l[:, par, b, :], r[:, uu % 2, :],
                                            start=(k == 0), stop=(k == 2))
                last.then_inc(s_Y, 1)

            def cross_out(t, par, quarter):
                if quarter == 0:
                    pe.wait_ge(s_Ye, 4 * t + 4)
                    wait(pe, s_xa, t)
                for h in range(4 * quarter, 4 * quarter + 4):
                    last = nc.tensor.matmul(bank[OUT_BANK][:, 0:DIM], YT[:, par, h, :, :], Bm[:, h, :],
                                            start=(h == 0), stop=(h == XH - 1))
                if quarter == 3:
                    last.then_inc(s_OUT, 1)

            pe.wait_ge(s_aa, 2)
            pe.wait_ge(s_av, 2)
            pe.wait_ge(s_ba, 2)
            pe.wait_ge(s_bv, 2)
            keys_transposed(0, 0)
            for c in range(4):
                queries(0, 0, c)
            keys_transposed(1, 1)
            pe.wait_ge(s_mr, 1)
            pe.wait_ge(s_cb, 2)

            def body(t0):
                for dt in range(2):
                    t = t0 + dt
                    par = dt
                    for uu in range(4):
                        tl, ul = (t, 0) if uu == 3 else (t - 1, uu + 1)
                        if valid(t, pairs):
                            scores(t, par, uu)
                        if valid(t - 2, pairs):
                            cross_out(t - 2, par, uu)
                        if valid(tl, pairs):
                            probs_transposed(4 * tl + ul, ul)
                        if uu == 3 and valid(t + 2, pairs):
                            keys_transposed(t + 2, par)
                        if valid(t + 1, pairs):
                            queries(t + 1, 1 - par, uu)
                        if valid(t - 1, pairs):
                            mixed(t - 1, 1 - par, uu)

            body(0)
            with pe.Fori(1, pairs // 2 - 2) as k:
                body(k * 2)
            body(pairs - 4)
            body(pairs - 2)
            body(pairs)

            def att_tile(need, t, p):
                q = 1 - p
                if valid(t, pairs):
                    need(A["yc"], t + 1)
                    need(A["ve"], t - 1)
                    nc.tensor.matmul(bank[2][0:64, 0:P], yc[:, p, 0:64], ident[:, :], start=True, stop=True)
                    nc.tensor.matmul(bank[2][64:P, 0:P], yc[:, p, 64:P], shift[:, :],
                                     start=True, stop=True).then_inc(A["h"], 1)
                if valid(t - 2, pairs):
                    j = t - 2
                    need(A["ote"], j - 1)
                    need(A["ad"], j + 1)
                    for c in range(8):
                        last = nc.tensor.transpose(bank[3 + c // 4][:, (c % 4) * P:(c % 4 + 1) * P],
                                                   rb[:, c // 4, 2 * (c % 4):2 * (c % 4) + 2, :], ident[:, :])
                    last.then_inc(A["f"], 1)
                if valid(t, pairs):
                    need(A["hl"], t + 1)
                    need(A["qs"], t)
                    for w in range(2):
                        for k, (l, r) in enumerate(((hTh, Wh), (hTh, Wl), (hTl, Wh))):
                            last = nc.tensor.matmul(bank[w][:, :], l[:, p, :], r[:, w * 512:(w + 1) * 512],
                                                    start=(k == 0), stop=(k == 2))
                    last.then_inc(A["qk"], 1)
                if valid(t - 3, pairs):
                    j = t - 3
                    need(A["pn"], j + 1)
                    need(A["res"], j)
                    for c in range(4):
                        last = nc.tensor.transpose(bank[7][:, c * P:(c + 1) * P], Pf[:, q, c, :, :], ident[:, :])
                    last.then_inc(A["pt"], 1)
                if valid(t - 2, pairs):
                    j = t - 2
                    need(A["fe"], j + 1)
                    need(A["sb"], j)
                    for e in range(2):
                        nc.tensor.matmul(bank[5 + e][:, 0:256].rearrange("p (c k) -> p c k", c=4), identb[:, :],
                                         causal[:, None, :].to_broadcast([P, 4, SEQ]),
                                         start=True, stop=False, skip_group_check=True)
                    for c in range(4):
                        for e in range(2):
                            for b in range(2):
                                r = slice(64 * e, 64 * e + 64)
                                last = nc.tensor.matmul(
                                    bank[5 + e][64 * b:64 * b + 64, c * SEQ:(c + 1) * SEQ],
                                    FT[r, c, 64 * b:64 * b + 64], FT[r, 4 + c, 64 * b:64 * b + 64],
                                    start=False, stop=(c == 3), skip_group_check=True)
                    last.then_inc(A["s"], 1)
                if valid(t - 3, pairs):
                    j = t - 3
                    need(A["pte"], j + 1)
                    need(A["fe"], min(j + 2, pairs) if isinstance(j, int) else j + 2)
                    need(A["ve"], j + 1)
                    nc.tensor.matmul(bank[3][:, 0:8], identb[:, :], identb[:, 0:8], start=True, stop=True)
                    for c in range(4):
                        for b in range(2):
                            for e in range(2):
                                r = slice(64 * e, 64 * e + 64)
                                last = nc.tensor.matmul(
                                    bank[3 + e][r, c * P + 64 * b:c * P + 64 * b + 64],
                                    V[r, q, b, c, :], PTf[r, c, 64 * b:64 * b + 64], start=True, stop=True)
                    last.then_inc(A["o"], 1)
                if valid(t - 1, pairs):
                    j = t - 1
                    need(A["he"], min(j + 2, pairs) if isinstance(j, int) else j + 2)
                    wv = Wqkv[:, :].rearrange("p (c e d) -> p c e d", e=2, d=DH)
                    nc.tensor.matmul(bank[2][:, 0:8], identb[:, :], identb[:, 0:8], start=True, stop=True)
                    for b in range(2):
                        for e in range(2):
                            last = nc.tensor.matmul(
                                bank[2][64 * e:64 * e + 64, b * 256:(b + 1) * 256].rearrange("p (c d) -> p c d", d=DH),
                                hT[:, q, 64 * b:64 * b + 64], wv[:, :, e, :], start=True, stop=True)
                    last.then_inc(A["v"], 1)
                if valid(t - 3, pairs):
                    j = t - 3
                    need(A["ote"], j + 1)
                    for c in range(4):
                        last = nc.tensor.matmul(bank[7][:, 0:DIM], OTf[:, c, :], Wo[:, c, :],
                                                start=(c == 0), stop=(c == 3))
                    last.then_inc(A["wo"], 1)

            def mlp_shifted(need, g):
                if valid(g, groups):
                    need(M["hc"], g + 1)
                    ytile = Y[:, bass.ds(g * GROUP, GROUP), :]
                    hb = bank[0][:, :].rearrange("p (t d) -> p t d", t=GROUP)
                    nc.tensor.matmul(hb[:, :, DIM // 2:], shift[:, :], ytile[:, :, DIM // 2:],
                                     start=True, stop=True).then_inc(M["h"], 1)

            def mlp_transposed(need, g):
                if valid(g, groups):
                    need(M["hn"], g + 1)
                    need(M["te"], g)
                    for k in range(GROUP):
                        last = nc.tensor.transpose(bank[1][:, k * P:(k + 1) * P], hn[:, k, :], ident[:, :])
                    last.then_inc(M["t"], 1)

            def mlp_group(need, g, p):
                if valid(g, groups):
                    need(M["nl"], g + 1)
                    for k, (h0, hw) in enumerate(HB):
                        need(M["u"], 3 * g + k - 2, True)
                        if k == 1:
                            need(M["res"], g - 1)
                        for o, bk in ((0, 2 + k), (HID, 5 + k)):
                            for m, (l, r) in enumerate(((W1h, nTh), (W1h, nTl), (W1l, nTh))):
                                last = nc.tensor.matmul(bank[bk][0:hw, :], l[:, o + h0:o + h0 + hw], r[:, :],
                                                        start=(m == 0), stop=(m == 2))
                        last.then_inc(M["a"], 1)
                mlp_transposed(need, g + 1)
                mlp_shifted(need, g + 2)
                if valid(g - 1, groups):
                    j = g - 1
                    need(M["res"], j)
                    if isinstance(g, int) and g == groups:
                        need(M["u"], 3 * groups, True)
                    else:
                        need(M["u"], 3 * g + 2, True)
                    for k in range(GROUP):
                        for c, (h0, hw) in enumerate(HB):
                            last = nc.tensor.matmul(bank[3][:, k * DIM:(k + 1) * DIM],
                                                    u[0:hw, 1 - p, c, k * P:(k + 1) * P],
                                                    W2[0:hw, c, :], start=(c == 0), stop=(c == 2))
                    last.then_inc(M["d"], 1)

            with pe.Fori(0, LAYERS) as lay:
                li = lay * pairs
                gi = lay * groups
                gi3 = lay * (3 * groups)
                pe.wait_ge(s_lw, lay * (16 * LW) + 16 * LW)
                pe.wait_ge(s_ws, lay * 2 + 2)
                pe.wait_ge(s_M, lay + 1)
                need = mlp_need(pe, gi, gi3)

                def lead_in(att_need, late):
                    if late == 0:
                        mlp_shifted(need, 0)
                    if late == 2:
                        mlp_transposed(need, 0)
                        mlp_shifted(need, 1)

                att_loop(pe, att_tile, li, pairs, lead_in)
                pe.wait_ge(s_mw, lay * (16 * MW) + 16 * MW)
                pe.wait_ge(s_w1, lay * 2 + 2)
                pe.wait_ge(s_A, lay + 2)
                mlp_loop(pe, mlp_group, need, groups)

        @block.scalar
        def _(act):
            act.dma_start(mask_u8[:, :, :], mask[None, :, :]).then_inc(s_msk, 16)
            for dst, src in ((G[0:SEQ, :], g_media[None, :].to_broadcast([SEQ, DIM])),
                             (G[SEQ:P, :], g_latent[None, :].to_broadcast([SEQ, DIM])),
                             (Bt[0:SEQ, :], b_media[None, :].to_broadcast([SEQ, DIM])),
                             (Bt[SEQ:P, :], b_latent[None, :].to_broadcast([SEQ, DIM]))):
                act.dma_start(dst, src).then_inc(s_gb, 16)
            for dst, src in ((bout_t[:, :], bout[None, :].to_broadcast([P, DIM])),
                             (gates[:, 0:1], g_x[None, :].to_broadcast([P, 1])),
                             (gates[:, 1:2], g_f[None, :].to_broadcast([P, 1])),
                             (hT[:, 0, 0:SEQ], causal_d),
                             (shift[:, :], shift_d),
                             (rot[:, :, :], rot_d),
                             (yc[:, 0, 0:LAYERS], ln_g.rearrange("l p -> p l")),
                             (yc[:, 0, 2:2 + LAYERS], ln_b.rearrange("l p -> p l"))):
                act.dma_start(dst, src).then_inc(s_ctab, 16)
            for g in (0, 2, 4):
                act.wait_ge(s_tr, g + 1)
                act.activation(WT[:, g // 2, 0:4, :], bank[g][:, :], ACT.Copy).then_inc(s_wta, 1)
            for g in (0, 2):
                act.wait_ge(s_pa, g + 1)
                act.activation(Am[:, g // 2:8:2, :], bank[g][:, :], ACT.Copy).then_inc(s_aa, 1)
            for g in (0, 2):
                act.wait_ge(s_pb, g + 1)
                act.activation(Bm[:, g // 2:8:2, :], bank[4 + g][:, :], ACT.Copy).then_inc(s_ba, 1)
            act.wait_ge(s_ctab, 16 * N_CONST)
            act.activation(causal[:, :], hT[:, 0, 0:SEQ], ACT.Copy).then_inc(s_cb, 1)
            act.activation(identb[:, :], ident[:, :], ACT.Copy).then_inc(s_cb, 1)
            act.activation(tg[:, :], gates[:, :], ACT.Tanh).then_inc(s_tanh, 1)

            def keysT_out(t, par):
                act.wait_ge(s_KT, t + 1)
                wait(act, s_S, 4 * (t - 1))
                wait(act, s_Q, 4 * (t - 1))
                kb = bank[KT_BANK][:, 0:2 * KEYS]
                act.activation(KT[:, par, :, :], kb, ACT.Copy).then_inc(s_KTe, 1)

            def queries_out(t, par, c):
                act.wait_ge(s_Q, 4 * t + c + 1)
                wait(act, s_S, 4 * (t - 1))
                src = bank[Q_BANK[c % 2]][:, :].rearrange("p (h b q) -> p b h q", h=4, b=2)
                act.activation(QP[:, par, :, 4 * c:4 * c + 4, :], src, ACT.Copy).then_inc(s_Qe, 1)

            def probsT_out(n, uu):
                act.wait_ge(s_PT, n + 1)
                wait(act, s_Y, n - 1)
                act.activation(PTh[:, uu % 2, :], bank[PT_BANK][:, :], ACT.Copy).then_inc(s_PTe, 1)

            def keys_high(t, par):
                act.wait_ge(s_KN, t + 1)
                wait(act, s_Y, 4 * (t - 1))
                act.activation(KXh[:, par, :, :], KN[:, par, :, :], ACT.Copy).then_inc(s_KXh, 1)

            def exps(n, uu):
                act.wait_ge(s_sub, n + 1)
                act.activation(Pr[:, uu, :, :], Pr[:, uu, :, :], ACT.Exp, scale=X_SCALE).then_inc(s_exp, 1)

            def mixed_out(t, par, uu):
                b, half = uu // 2, uu % 2
                act.wait_ge(s_Y, 4 * t + uu + 1)
                wait(act, s_OUT, t - 1)
                src = bank[Y_BANK][:, :].rearrange("p (h q) -> p h q", q=SEQ)
                act.activation(YT[:, par, 8 * half:8 * half + 8, b, :], src, ACT.Copy).then_inc(s_Ye, 1)

            keysT_out(0, 0)
            for c in range(4):
                queries_out(0, 0, c)
            keysT_out(1, 1)

            def body(t0):
                for dt in range(2):
                    t = t0 + dt
                    par = dt
                    for uu in range(4):
                        tl, ul = (t, 0) if uu == 3 else (t - 1, uu + 1)
                        if uu == 0 and valid(t, pairs):
                            keys_high(t, par)
                        if valid(tl, pairs):
                            probsT_out(4 * tl + ul, ul)
                        if valid(t, pairs):
                            exps(4 * t + uu, uu)
                        if uu == 3 and valid(t + 2, pairs):
                            keysT_out(t + 2, par)
                        if valid(t + 1, pairs):
                            queries_out(t + 1, 1 - par, uu)
                        if valid(t - 1, pairs):
                            mixed_out(t - 1, 1 - par, uu)

            body(0)
            with act.Fori(1, pairs // 2 - 2) as k:
                body(k * 2)
            body(pairs - 4)
            body(pairs - 2)
            act.wait_ge(s_lw, 16 * LW)
            act.activation(Wh[:, :], Wraw, ACT.Copy).then_inc(s_ws, 1)
            body(pairs)

            def att_tile(need, t, p):
                q = 1 - p
                if valid(t, pairs):
                    need(A["h"], t + 1)
                    need(A["v"], t - 1)
                    act.activation(hTh[:, p, :], bank[2][:, 0:P], ACT.Copy)
                    act.activation(hT[:, p, :], bank[2][:, 0:P], ACT.Copy).then_inc(A["he"], 1)
                if valid(t - 2, pairs):
                    j = t - 2
                    need(A["f"], j + 1)
                    need(A["s"], j)
                    act.activation(FT[:, 0:4, :], bank[3][:, :], ACT.Copy)
                    act.activation(FT[:, 4:8, :], bank[4][:, :], ACT.Copy).then_inc(A["fe"], 1)
                if valid(t, pairs):
                    need(A["qk"], t + 1)
                    need(A["ssd"], t)
                    act.activation(sq[:, 0:8, :], bank[0][:, :], ACT.Square)
                    act.activation(sq[:, 8:16, :], bank[1][:, :], ACT.Square).then_inc(A["sqd"], 1)
                if valid(t - 3, pairs):
                    j = t - 3
                    need(A["pt"], j + 1)
                    need(A["o"], j)
                    act.activation(PTf[:, :, :], bank[7][:, :], ACT.Copy).then_inc(A["pte"], 1)
                if valid(t, pairs):
                    need(A["qnd"], t - 1)
                    act.activation(qs[:, p, 0, :, :], bank[0][:, :], ACT.Copy)
                    act.activation(qs[:, p, 1, :, :], bank[1][:, :], ACT.Copy).then_inc(A["qs"], 1)
                if valid(t, pairs) and valid(t + 1, pairs):
                    if isinstance(t, int) and t == 0:
                        need(s_ready, pairs)
                    copy_tile(t + 1, 1 - p)
                if valid(t - 3, pairs):
                    j = t - 3
                    need(A["o"], j + 1)
                    need(A["wo"], j)
                    act.activation(OTf[0:64, :, :], bank[3][0:64, :], ACT.Copy)
                    act.activation(OTf[64:P, :, :], bank[4][64:P, :], ACT.Copy).then_inc(A["ote"], 1)
                if valid(t - 2, pairs):
                    j = t - 2
                    need(A["sb"], j + 1)
                    act.activation(Pf[:, p, :, :, :], Pf[:, p, :, :, :], ACT.Exp, scale=F_SCALE).then_inc(A["e"], 1)
                if valid(t - 1, pairs):
                    j = t - 1
                    need(A["v"], j + 1)
                    need(A["o"], j - 1)
                    act.activation(V[:, q, :, :, :], bank[2][:, :], ACT.Copy).then_inc(A["ve"], 1)

            def copy_tile(t, p):
                act.activation(yc[:, p, :], Y[:, bass.ds(t, 1), :].rearrange("p o d -> p (o d)"),
                               ACT.Copy).then_inc(A["yc"], 1)

            def mlp_unshifted(need, g):
                if valid(g, groups):
                    need(M["hn"], g)
                    act.activation(bank[0][:, :].rearrange("p (t d) -> p t d", t=GROUP)[:, :, 0:DIM // 2],
                                   Y[:, bass.ds(g * GROUP, GROUP), 0:DIM // 2], ACT.Copy).then_inc(M["hc"], 1)

            def mlp_transposed_out(need, g):
                if valid(g, groups):
                    need(M["t"], g + 1)
                    need(M["nl"], g)
                    act.activation(nT[:, :], bank[1][:, :], ACT.Identity, bias=lnb[:, 0:1],
                                   scale=lng[:, 0:1]).then_inc(M["te"], 1)

            def mlp_group(need, g, p):
                if valid(g, groups):
                    for k, (h0, hw) in enumerate(HB):
                        need(M["a"], 3 * g + k + 1, True)
                        need(M["u"], 3 * g + k - 2, True)
                        act.activation(ge[0:hw, k, :], bank[5 + k][0:hw, :], ACT.Gelu,
                                       bias=b1g[0:hw, k:k + 1]).then_inc(M["g"], 1)
                        if k == 1:
                            mlp_unshifted(need, g + 2)
                mlp_transposed_out(need, g + 1)

            def mlp_weights_high(lay):
                act.wait_ge(s_mw, lay * (16 * MW) + 16 * MW)
                act.activation(W1h[:, :], W1raw, ACT.Copy).then_inc(s_w1, 1)

            def layer(lay):
                need = mlp_need(act, lay * groups, lay * (3 * groups))

                def lead_in(att_need, late):
                    if late == -1:
                        mlp_weights_high(lay)
                    if late == 0:
                        att_need(A["res"], GROUP)
                        att_need(A["qs"], pairs)
                        mlp_unshifted(need, 0)
                    if late == 2:
                        act.wait_ge(s_rt, lay * 2 + 2)
                        mlp_transposed_out(need, 0)
                        mlp_unshifted(need, 1)

                act.wait_ge(s_ready, lay * pairs + 1)
                copy_tile(0, 0)
                att_loop(act, att_tile, lay * pairs, pairs, lead_in)
                mlp_loop(act, mlp_group, need, groups)

            with act.Fori(0, LAYERS) as lay:
                layer(lay)

        @block.vector
        def _(dve):
            def row_stats(t, par):
                dve.bn_stats(ST[:, par, 0, :], XC[:, bass.ds(2 * t, 1), :])
                dve.bn_stats(ST[:, par, 1, :], XC[:, bass.ds(2 * t + 1, 1), :]).then_inc(s_st, 1)
                dve.wait_ge(s_st, t + 1)
                dve.memset(scratch[:, 5:6], 0.0)
                for b in range(2):
                    last = dve.bn_aggr(MX[:, par, b, :], ST[:, par, b, :])
                last.then_inc(s_ag, 1)
                dve.wait_ge(s_ag, t + 1)
                dve.tensor_scalar(V1[:, par, :], MX[:, par, :, 1], EPS, None, ALU.add).then_inc(s_v1, 1)

            def second_variance(t, par):
                dve.wait_ge(s_r1, t + 1)
                dve.tensor_tensor(V2[:, par, :], R1[:, par, :], R1[:, par, :], ALU.mult).then_inc(s_v2, 1)
                dve.wait_ge(s_v2, 3 * t + 1)
                dve.tensor_tensor(V2[:, par, :], V2[:, par, :], MX[:, par, :, 1], ALU.mult).then_inc(s_v2, 1)
                dve.wait_ge(s_v2, 3 * t + 2)
                dve.tensor_scalar(V2[:, par, :], V2[:, par, :], EPS, None, ALU.add).then_inc(s_v2, 1)

            def latents_rstd(t, par):
                dve.wait_ge(s_r2, t + 1)
                dve.tensor_tensor(R1[SEQ:P, par, :], R1[SEQ:P, par, :], R2[SEQ:P, par, :],
                                  ALU.mult).then_inc(s_r3, 1)

            def normalise(t, par):
                dve.wait_ge(s_r3, t + 1)
                wait(dve, s_KG, t - 1)
                for b in range(2):
                    bb = bass.ds(2 * t + b, 1)
                    last = dve.tensor_scalar(XN[:, par, b, :], XC[:, bb, :].rearrange("p o d -> p (o d)"),
                                             MX[:, par, b, 0:1], R1[:, par, b:b + 1], ALU.subtract, ALU.mult)
                last.then_inc(s_XN, 1)

            def softmax_first(n, uu):
                dve.wait_ge(s_S, n + 1)
                sv = bank[S_BANK[uu % 2]][:, :].rearrange("p (h k) -> p h k", h=4)
                dve.tensor_reduce(mx[:, uu, :], sv, AX.X, ALU.max).then_inc(s_max, 1)
                dve.wait_ge(s_max, n + 1)
                wait(dve, s_PT, n - 3)
                dve.tensor_tensor(Pr[:, uu, :, :], sv, mx[:, uu, :, None].to_broadcast([P, 4, KEYS]),
                                  ALU.subtract).then_inc(s_sub, 1)

            def softmax_second(n, uu):
                dve.wait_ge(s_exp, n + 1)
                dve.tensor_reduce(sm[:, uu, :], Pr[:, uu, :, :], AX.X, ALU.add).then_inc(s_sum, 1)
                dve.wait_ge(s_sum, n + 1)
                dve.reciprocal(rc[:, uu, :], sm[:, uu, :]).then_inc(s_rec, 1)

            def add_cross(t):
                dve.wait_ge(s_OUT, t + 1)
                dve.wait_ge(s_xb, t + 1)
                x1 = X1[:, bass.ds(t, 1), :].rearrange("p o d -> p (o d)")
                dve.scalar_tensor_tensor(x1, bank[OUT_BANK][:, 0:DIM], tg[:, 0:1], x1,
                                         ALU.mult, ALU.add).then_inc(s_xa, 1)

            def x1_stats(t):
                dve.wait_ge(s_xa, t + 1)
                dve.memset(scratch[:, 5:6], 0.0)
                dve.bn_stats(ST1[:, :], X1[:, bass.ds(t, 1), :]).then_inc(s_bn, 1)
                dve.wait_ge(s_bn, t + 1)
                dve.memset(scratch[:, 5:6], 0.0)
                dve.bn_aggr(MX1[:, :], ST1[:, :]).then_inc(s_xg, 1)
                dve.wait_ge(s_xg, t + 1)
                dve.tensor_scalar(VX1[:, :], MX1[:, 1:2], EPS, None, ALU.add).then_inc(s_xv, 1)

            def x1_normalise(t):
                dve.wait_ge(s_xr, t + 1)
                dve.tensor_scalar(Y[:, bass.ds(t, 1), :].rearrange("p o d -> p (o d)"),
                                  X1[:, bass.ds(t, 1), :].rearrange("p o d -> p (o d)"),
                                  MX1[:, 0:1], RX1[:, :], ALU.subtract, ALU.mult).then_inc(s_ready, 1)

            def probsT_split(n, uu):
                dve.wait_ge(s_PTe, n + 1)
                wait(dve, s_Y, n - 1)
                dve.tensor_tensor(PTl[:, uu % 2, :], bank[PT_BANK][:, :], PTh[:, uu % 2, :].bitcast(fp32),
                                  ALU.subtract).then_inc(s_PTl, 1)

            dve.memset(ones_row[:, :], 1.0)
            dve.wait_ge(s_in[0], 32)
            for t in range(2):
                row_stats(t, t)
            for t in range(2):
                second_variance(t, t)
            for g in (1, 3, 5):
                dve.wait_ge(s_tr, g + 1)
                dve.tensor_copy(WT[:, g // 2, 4:8, :], bank[g][:, :]).then_inc(s_wtv, 1)
            for t in range(2):
                latents_rstd(t, t)
                normalise(t, t)
            row_stats(2, 0)
            for g in (1, 3):
                dve.wait_ge(s_pa, g + 1)
                dve.tensor_copy(Am[:, 8 + g // 2:16:2, :], bank[g][:, :]).then_inc(s_av, 1)
            for g in (1, 3):
                dve.wait_ge(s_pb, g + 1)
                dve.tensor_copy(Bm[:, 8 + g // 2:16:2, :], bank[4 + g][:, :]).then_inc(s_bv, 1)
            second_variance(2, 0)
            dve.wait_ge(s_tanh, 1)
            dve.wait_ge(s_ctab, 16 * N_CONST)
            dve.tensor_scalar(bout_t[:, :], bout_t[:, :], tg[:, 0:1], None, ALU.mult).then_inc(s_bias, 1)

            def body(t0):
                for dt in range(2):
                    t = t0 + dt
                    par = dt
                    for uu in range(4):
                        tl, ul = (t, 0) if uu == 3 else (t - 1, uu + 1)
                        t1, u1 = (t, uu - 1) if uu >= 1 else (t - 1, 3)
                        if valid(t, pairs):
                            softmax_first(4 * t + uu, uu)
                        if valid(t1, pairs):
                            softmax_second(4 * t1 + u1, u1)
                        if valid(tl, pairs):
                            probsT_split(4 * tl + ul, ul)
                        if uu == 3 and valid(t - 2, pairs):
                            add_cross(t - 2)
                            if isinstance(t, int) and t - 2 == pairs - 1:
                                dve.wait_ge(s_xa, pairs)
                                dve.memset(scratch[:, 2:3], 0.0).then_inc(s_M, 1)
                            x1_stats(t - 2)
                        if uu == 1 and valid(t - 3, pairs):
                            x1_normalise(t - 3)
                        if uu == 0 and valid(t + 2, pairs):
                            latents_rstd(t + 2, par)
                        if uu == 0 and valid(t + 3, pairs):
                            row_stats(t + 3, 1 - par)
                        if uu == 0 and valid(t + 2, pairs):
                            normalise(t + 2, par)
                        if uu == 2 and valid(t + 3, pairs):
                            second_variance(t + 3, 1 - par)

            body(0)
            dve.wait_ge(s_in[1], 32)
            dve.wait_ge(s_xp, 16)
            body(2)
            with dve.Fori(2, pairs // 2 - 2) as k:
                body(k * 2)
            body(pairs - 4)
            body(pairs - 2)
            body(pairs)
            body(pairs + 2)
            dve.wait_ge(s_xa, pairs)
            dve.memset(scratch[:, 1:2], 0.0).then_inc(s_A, 1)

            def att_tile(need, t, p):
                q = 1 - p

                if valid(t, pairs):
                    need(A["he"], t + 1)
                    need(A["qk"], t - 1)
                    dve.tensor_tensor(hTl[:, p, :], hT[:, p, :], hTh[:, p, :].bitcast(fp32),
                                      ALU.subtract).then_inc(A["hl"], 1)
                if valid(t - 4, pairs):
                    j = t - 4
                    need(A["wo"], j + 1)
                    y = Y[:, bass.ds(t - 4, 1), :].rearrange("p o d -> p (o d)")
                    dve.tensor_tensor(y, bank[7][:, 0:DIM], y, ALU.add).then_inc(A["res"], 1)
                if valid(t - 1, pairs):
                    j = t - 1
                    need(A["rnd"], j + 1)
                    need(A["qs"], j + 1)
                    need(A["rad"], j)
                    dve.tensor_tensor(qn[:, 0, :, :], qs[:, q, 0, :, :],
                                      rn[:, q, 0:8, None].to_broadcast([P, FH, DH]), ALU.mult)
                    dve.tensor_tensor(qn[:, 1, :, :], qs[:, q, 1, :, :],
                                      rn[:, q, 8:16, None].to_broadcast([P, FH, DH]),
                                      ALU.mult).then_inc(A["qnd"], 1)
                    need(A["qnd"], j + 1)
                    need(A["f"], j)
                    for o, s_ in ((0, 32), (32, 0)):
                        last = dve.tensor_tensor(rb[:, :, :, o:o + 32], qn[:, :, :, s_:s_ + 32],
                                                 RT2[:, :, None, o:o + 32].to_broadcast([P, 2, FH, 32]), ALU.mult)
                    last.then_inc(A["rbd"], 1)
                if valid(t, pairs):
                    need(A["sqd"], t + 1)
                    dve.tensor_reduce(ss[:, p, :], sq[:, :, :], AX.X, ALU.add).then_inc(A["ssd"], 1)
                    need(A["ssd"], t + 1)
                    dve.tensor_scalar(ss[:, p, :], ss[:, p, :], 1e-24, None, ALU.max).then_inc(A["cl"], 1)
                if valid(t - 2, pairs):
                    j = t - 2
                    need(A["s"], j + 1)
                    need(A["pt"], j - 1)
                    for e in range(2):
                        sv = bank[5 + e][:, 0:256].rearrange("p (c k) -> p c k", c=4)
                        last = dve.tensor_reduce(fm[:, p, :, e], sv, AX.X, ALU.max)
                    last.then_inc(A["m"], 1)
                    need(A["m"], j + 1)
                    for e in range(2):
                        sv = bank[5 + e][:, 0:256].rearrange("p (c k) -> p c k", c=4)
                        last = dve.tensor_tensor(Pf[:, p, :, e, :], sv,
                                                 fm[:, p, :, e:e + 1].to_broadcast([P, 4, SEQ]), ALU.subtract)
                    last.then_inc(A["sb"], 1)
                if valid(t - 1, pairs):
                    j = t - 1
                    need(A["rad"], j + 1)
                    need(A["rbd"], j + 1)
                    dve.tensor_tensor(rb[:, :, :, :], rb[:, :, :, :], ra[:, :, :, :], ALU.add).then_inc(A["ad"], 1)
                if valid(t - 2, pairs):
                    j = t - 2
                    need(A["e"], j + 1)
                    dve.tensor_reduce(fs[:, p, :, :], Pf[:, p, :, :, :], AX.X, ALU.add).then_inc(A["su"], 1)
                    need(A["su"], j + 1)
                    dve.reciprocal(fr[:, p, :, :], fs[:, p, :, :]).then_inc(A["r"], 1)

            def mlp_stats(need, g):
                if valid(g, groups):
                    need(M["h"], g + 1)
                    hb = bank[0][:, :].rearrange("p (t d) -> p t d", t=GROUP)
                    for k in range(GROUP):
                        last = dve.bn_stats(ST2[:, k, :], hb[:, k, :])
                    last.then_inc(M["bs"], 1)
                    need(M["bs"], g + 1)
                    dve.memset(scratch[:, 0:1], 0.0)
                    for k in range(GROUP):
                        last = dve.bn_aggr(MV[:, k, :], ST2[:, k, :])
                    last.then_inc(M["ba"], 1)
                    need(M["ba"], g + 1)
                    dve.tensor_scalar(ve[:, :], MV[:, :, 1], EPS, None, ALU.add).then_inc(M["ve"], 1)

            def mlp_normed(need, g):
                if valid(g, groups):
                    need(M["rs"], g + 1)
                    need(M["t"], g)
                    hb = bank[0][:, :].rearrange("p (t d) -> p t d", t=GROUP)
                    for k in range(GROUP):
                        last = dve.tensor_scalar(hn[:, k, :], hb[:, k, :], MV[:, k, 0:1], rs[:, k:k + 1],
                                                 ALU.subtract, ALU.mult)
                    last.then_inc(M["hn"], 1)

            def mlp_split(need, g):
                if valid(g, groups):
                    need(M["te"], g + 1)
                    need(M["a"], 3 * g, True)
                    dve.tensor_copy(nTh[:, :], nT[:, :]).then_inc(M["nh"], 1)
                    need(M["nh"], g + 1)
                    dve.tensor_tensor(nTl[:, :], nT[:, :], nTh[:, :].bitcast(fp32),
                                      ALU.subtract).then_inc(M["nl"], 1)

            def mlp_group(need, g, p):
                mlp_normed(need, g + 1)
                if valid(g, groups):
                    for k, (h0, hw) in enumerate(HB):
                        need(M["g"], 3 * g + k + 1, True)
                        need(M["d"], g - 1)
                        dve.scalar_tensor_tensor(u[0:hw, p, k, :], bank[2 + k][0:hw, :], b1a[0:hw, k:k + 1],
                                                 ge[0:hw, k, :], ALU.add, ALU.mult).then_inc(M["u"], 1)
                mlp_split(need, g + 1)
                mlp_stats(need, g + 2)
                if valid(g - 1, groups):
                    j = g - 1
                    need(M["d"], j + 1)
                    y = Y[:, bass.ds((g - 1) * GROUP, GROUP), :]
                    dve.tensor_tensor(y, bank[3][:, :].rearrange("p (t d) -> p t d", t=GROUP), y,
                                      ALU.add).then_inc(M["res"], 1)
                if valid(g - 1, groups):
                    need(M["res"], j + 1)
                    if isinstance(g, int) and g == groups:
                        dve.memset(scratch[:, 2:3], 0.0).then_inc(s_M, 1)
                    dve.tensor_tensor(y, y, b2t[:, None, :].to_broadcast([P, GROUP, DIM]), ALU.add).then_inc(s_ready, GROUP)

            with dve.Fori(0, LAYERS) as lay:
                li = lay * pairs
                gi = lay * groups
                gi3 = lay * (3 * groups)
                need = mlp_need(dve, gi, gi3)

                def lead_in(att_need, late):
                    if late == 1 - pairs:
                        dve.wait_ge(s_lw, lay * (16 * LW) + 16 * LW)
                        dve.tensor_tensor(RT1[:, :, :], rot[:, 0:2, :], qks[:, :, :], ALU.mult)
                        for o, s_ in ((0, 32), (32, 0)):
                            last = dve.tensor_tensor(RT2[:, :, o:o + 32], rot[:, 2:4, o:o + 32], qks[:, :, s_:s_ + 32], ALU.mult)
                        last.then_inc(s_rt, 1)
                        dve.wait_ge(s_rt, lay * 2 + 1)
                        dve.wait_ge(s_pm, 2)
                        dve.wait_ge(s_M, lay + 1)
                        dve.memset(scratch[:, 3:4], 0.0)
                        dve.tensor_copy(lng[:, :], lnp[:, bass.ds(lay, 1)])
                        dve.tensor_copy(lnb[:, :], lnp[:, bass.ds(lay + LAYERS, 1)]).then_inc(s_rt, 1)
                    if late == 0:
                        mlp_stats(need, 0)
                    if late == 1:
                        mlp_normed(need, 0)
                    if late == 3:
                        mlp_split(need, 0)
                        mlp_stats(need, 1)

                att_loop(dve, att_tile, li, pairs, lead_in)
                dve.wait_ge(A["res"], li + pairs)
                dve.memset(scratch[:, 1:2], 0.0).then_inc(s_A, 1)
                dve.wait_ge(s_mw, lay * (16 * MW) + 16 * MW)
                dve.memset(scratch[:, 3:4], 0.0)
                mlp_loop(dve, mlp_group, need, groups)
            dve.wait_ge(s_ready, (LAYERS + 1) * pairs)
            r = slice(pairs - GROUP, pairs)
            dve.scalar_tensor_tensor(Y[:, r, :], Y[:, r, :], tg[:, 1:2], X1[:, r, :],
                                     ALU.mult, ALU.add).then_inc(s_fin_last, 1)

        @block.gpsimd
        def _(pool):
            pool.memset(minus_half[:, :], -0.5).then_inc(s_pm, 1)
            pool.wait_ge(s_pm, 1)
            def rows_rstd(t, par):
                pool.wait_ge(s_v1, t + 1)
                pool.tensor_tensor(R1[:, par, :], V1[:, par, :], minus_half[:, 0:2], ALU.pow).then_inc(s_r1, 1)

            def rows_rstd2(t, par):
                pool.wait_ge(s_v2, 3 * t + 3)
                pool.tensor_tensor(R2[:, par, :], V2[:, par, :], minus_half[:, 0:2], ALU.pow).then_inc(s_r2, 1)

            def scale_keys(t, par):
                pool.wait_ge(s_XN, t + 1)
                wait(pool, s_KT, t - 1)
                wait(pool, s_KX, t - 1)
                pool.tensor_tensor(KN[:, par, :, :], XN[:, par, :, :], G[:, None, :].to_broadcast([P, 2, DIM]),
                                   ALU.mult).then_inc(s_KG, 1)
                pool.wait_ge(s_KG, t + 1)
                pool.tensor_tensor(KN[:, par, :, :], KN[:, par, :, :], Bt[:, None, :].to_broadcast([P, 2, DIM]),
                                   ALU.add).then_inc(s_KN, 1)

            def keys_low(t, par):
                pool.wait_ge(s_KXh, t + 1)
                pool.tensor_tensor(KXl[:, par, :, :], KN[:, par, :, :], KXh[:, par, :, :].bitcast(fp32),
                                   ALU.subtract).then_inc(s_KX, 1)

            def add_bias(t):
                x1 = X1[:, bass.ds(t, 1), :].rearrange("p o d -> p (o d)")
                pool.tensor_tensor(x1, x1, bout_t[:, :], ALU.add).then_inc(s_xb, 1)

            def x1_rstd(t):
                pool.wait_ge(s_xv, t + 1)
                pool.tensor_tensor(RX1[:, :], VX1[:, :], minus_half[:, 0:1], ALU.pow).then_inc(s_xr, 1)

            def attention_weights_low(lay):
                pool.wait_ge(s_ws, lay * 2 + 1)
                pool.tensor_tensor(Wl[:, :], Wraw, Wh[:, :].bitcast(fp32), ALU.subtract).then_inc(s_ws, 1)

            def mlp_weights_low(lay):
                pool.wait_ge(s_w1, lay * 2 + 1)
                pool.tensor_tensor(W1l[:, :], W1raw, W1h[:, :].bitcast(fp32), ALU.subtract).then_inc(s_w1, 1)

            pool.wait_ge(s_msk, 16)
            pool.tensor_scalar(mask_row[:, :, :], mask_u8[:, :, :], NEG, 0.0, ALU.mult, ALU.add).then_inc(s_mr, 1)
            rows_rstd(0, 0)
            rows_rstd(1, 1)
            rows_rstd2(0, 0)
            rows_rstd2(1, 1)
            pool.wait_ge(s_gb, 64)
            scale_keys(0, 0)
            scale_keys(1, 1)
            rows_rstd(2, 0)
            pool.wait_ge(s_ctab, 16 * N_CONST)
            pool.tensor_copy(lnp[:, :], yc[:, 0, 0:2 * LAYERS]).then_inc(s_pm, 1)
            rows_rstd2(2, 0)

            def body(t0):
                for dt in range(2):
                    t = t0 + dt
                    par = dt
                    for uu in range(4):
                        n = 4 * t + uu
                        if uu == 0 and valid(t + 3, pairs):
                            rows_rstd(t + 3, 1 - par)
                        if uu == 1 and valid(t, pairs):
                            keys_low(t, par)
                        if uu == 1 and valid(t + 2, pairs):
                            scale_keys(t + 2, par)
                        if uu == 3 and valid(t + 3, pairs):
                            rows_rstd2(t + 3, 1 - par)
                        if uu == 2 and valid(t - 2, pairs):
                            add_bias(t - 2)
                        if valid(t, pairs):
                            pool.wait_ge(s_rec, n + 1)
                            pool.tensor_tensor(Pr[:, uu, :, :], Pr[:, uu, :, :],
                                               rc[:, uu, :, None].to_broadcast([P, 4, KEYS]), ALU.mult).then_inc(s_pn, 1)
                        if uu == 3 and valid(t - 2, pairs):
                            x1_rstd(t - 2)

            body(0)
            pool.wait_ge(s_bias, 1)
            pool.wait_ge(s_xp, 16)
            with pool.Fori(1, pairs // 2 - 2) as k:
                body(k * 2)
            body(pairs - 4)
            body(pairs - 2)
            attention_weights_low(0)
            body(pairs)

            def att_tile(need, t, p):
                q = 1 - p
                if valid(t - 3, pairs):
                    j = t - 3
                    need(A["r"], j + 1)
                    pool.tensor_tensor(Pf[:, q, :, :, :], Pf[:, q, :, :, :],
                                       fr[:, q, :, :, None].to_broadcast([P, 4, 2, SEQ]), ALU.mult).then_inc(A["pn"], 1)
                if valid(t - 1, pairs):
                    j = t - 1
                    need(A["qnd"], j + 1)
                    need(A["ad"], j)
                    pool.tensor_tensor(ra[:, :, :, :], qn[:, :, :, :],
                                       RT1[:, :, None, :].to_broadcast([P, 2, FH, DH]), ALU.mult).then_inc(A["rad"], 1)
                if valid(t, pairs):
                    need(A["cl"], t + 1)
                    pool.tensor_tensor(rn[:, p, :], ss[:, p, :], minus_half[:, 0:16], ALU.pow).then_inc(A["rnd"], 1)

            def mlp_rstd(need, g):
                if valid(g, groups):
                    need(M["ve"], g + 1)
                    pool.tensor_tensor(rs[:, :], ve[:, :], minus_half[:, 0:GROUP], ALU.pow).then_inc(M["rs"], 1)

            def mlp_group(need, g, p):
                mlp_rstd(need, g + 2)

            def last_group(need, g, p):
                mlp_rstd(need, g + 2)
                if valid(g - 2, groups):
                    r = bass.ds((g - 2) * GROUP, GROUP)
                    pool.wait_ge(s_ready, (g - 1) * GROUP + LAYERS * pairs)
                    pool.tensor_tensor(scratch[:, 7:8], minus_half[:, 0:1], minus_half[:, 0:1], ALU.add)
                    pool.tensor_tensor(Y[:, r, :], Y[:, r, :], tg[:, None, 1:2].to_broadcast([P, GROUP, DIM]),
                                       ALU.mult).then_inc(s_gated, 1)
                    pool.wait_ge(s_gated, (g - 2) + 1)
                    pool.tensor_tensor(Y[:, r, :], Y[:, r, :], X1[:, r, :], ALU.add).then_inc(s_fin, 1)

            def layer(lay, group):
                need = mlp_need(pool, lay * groups, lay * (3 * groups))

                def lead_in(att_need, late):
                    if late == 1 - pairs:
                        pool.wait_ge(s_rt, lay * 2 + 2)
                        pool.tensor_tensor(scratch[:, 4:5], minus_half[:, 0:1], minus_half[:, 0:1], ALU.add)
                    if late == 0:
                        mlp_weights_low(lay)
                    if late == 1:
                        mlp_rstd(need, 0)


                att_loop(pool, att_tile, lay * pairs, pairs, lead_in)
                mlp_rstd(need, 1)
                mlp_loop(pool, group, need, groups)

            with pool.Fori(0, LAYERS - 1) as lay:
                layer(lay, mlp_group)
                pool.wait_ge(s_lw, lay * (16 * LW) + 32 * LW)
                pool.tensor_tensor(scratch[:, 4:5], minus_half[:, 0:1], minus_half[:, 0:1], ALU.add)
                pool.tensor_copy(Wh[:, :], Wraw).then_inc(s_ws, 1)
                attention_weights_low(lay + 1)
            layer(LAYERS - 1, last_group)


def tables():
    import numpy as np
    ident = np.eye(P, dtype=np.float32)
    shift = np.zeros((P, P), np.float32)
    for o in range(P):
        if o % SEQ:
            shift[o - 1, o] = 1.0
    q = np.arange(P)[:, None] % SEQ
    causal = np.where(q < np.arange(SEQ)[None, :], np.float32(NEG), np.float32(0.0)).astype(np.float32)
    half = np.arange(0, DH, 2, dtype=np.float32)
    freqs = np.arange(SEQ, dtype=np.float32)[:, None] * (1.0 / 10000.0 ** (half / DH)).astype(np.float32)[None, :]
    freqs = np.concatenate([freqs, freqs], -1)
    base = (half + 0.4 * DH) / (1.4 * DH)
    power = (np.arange(SEQ, dtype=np.float32) - SEQ // 2) / 32.0
    scale = base[None, :] ** power[:, None]
    scale = np.concatenate([scale, scale], -1)
    cos, sin = np.cos(freqs), np.sin(freqs)
    sign = np.where(np.arange(DH) < DH // 2, -1.0, 1.0)[None, :]
    rot = np.stack([cos * scale, cos / scale, sign * sin * scale, sign * sin / scale], 1).astype(np.float32)
    return ident, shift, causal, np.ascontiguousarray(np.concatenate([rot, rot], 0))


_INS = ["x", "ctx_1024", "mask_BxS2_bk0", "g_xattn", "g_ffn", "L0_xattn_Wq", "L0_xattn_Wkv",
        "L0_xattn_Wout", "L0_xattn_bout", "L0_xattn_g_media", "L0_xattn_b_media",
        "L0_xattn_g_latent", "L0_xattn_b_latent", "L0_ffn_wqkv", "L0_ffn_q_scale",
        "L0_ffn_k_scale", "L0_ffn_wo", "L0_ffn_ln_g", "L0_ffn_ln_b", "L0_ffn_w1", "L0_ffn_b1",
        "L0_ffn_w2", "L0_ffn_b2"]


def kernel(**inputs):
    import numpy as np
    import concourse.bacc as bacc
    from concourse.bass_utils import run_bass_kernel_spmd

    nc = bacc.Bacc("TRN2", target_bir_lowering=False, num_devices=1)
    arrays, args = {}, []
    for name, a in [(n, inputs[n]) for n in _INS] + list(zip(("ident", "shift", "causal", "rot"), tables())):
        a = np.ascontiguousarray(a)
        arrays[f"in_{name}"] = a
        args.append(nc.dram_tensor(f"in_{name}", a.shape, mybir.dt.from_np(a.dtype), kind="ExternalInput").ap())
    shape = (BATCH, SEQ, DIM)
    args.append(nc.dram_tensor("out", shape, fp32, kind="ExternalOutput").ap())
    build(nc, *args)
    r = run_bass_kernel_spmd(nc, [arrays], core_ids=[0])
    return r.results[0]["out"]
```
